# Optimizing a Trainium2 kernel written in Bass

```python
import numpy as np
import jax
import jax.numpy as jnp

def _softmax(x, axis=-1):
    return jax.nn.softmax(x, axis=axis)

def _gelu(x):
    return jax.nn.gelu(x, approximate=True)

def _silu(x):
    return jax.nn.silu(x)

def _sigmoid(x):
    return jax.nn.sigmoid(x)

def _layernorm(x, axis=-1, eps=1e-05):
    m = jnp.mean(x, axis=axis, keepdims=True)
    v = jnp.var(x, axis=axis, keepdims=True)
    return (x - m) / jnp.sqrt(v + eps)

def _scatter_add(tgt, idx, src, axis=0):
    return tgt.at[idx].add(src)

def _segment_sum(src, seg, n):
    return jax.ops.segment_sum(src, seg, n)
kernel_name = 'mk_seq_postln_d2_jaxref_r8_638d07'

def setup_inputs(seed: int=0):
    np.random.seed(seed)
    _w = jnp.asarray

    def _L0_attn_setup():
        import jax, jax.numpy as jnp
        import numpy as np
        D_MODEL, D_K, D_V, N_HEADS = (128, 64, 64, 16)
        BATCH, N_CTX = (2, 256)

        def half_causal_allowed(n):
            i = jnp.arange(n)[:, None]
            j = jnp.arange(n)[None, :]
            top = (i < n // 2) & (j < n // 2)
            bot = (i >= n // 2) & (j <= i)
            return top | bot
        key = jax.random.key(seed)
        ks = jax.random.split(key, 8)
        s_in = 1.0 / np.sqrt(D_MODEL)
        s_out = 1.0 / np.sqrt(D_V * N_HEADS)
        return {'x': jax.random.normal(ks[0], (BATCH, N_CTX, D_MODEL), jnp.float32), 'Wq': jax.random.uniform(ks[1], (D_MODEL, D_K * N_HEADS), jnp.float32, -s_in, s_in), 'bq': jax.random.uniform(ks[2], (D_K * N_HEADS,), jnp.float32, -s_in, s_in), 'Wk': jax.random.uniform(ks[3], (D_MODEL, D_K * N_HEADS), jnp.float32, -s_in, s_in), 'bk': jax.random.uniform(ks[4], (D_K * N_HEADS,), jnp.float32, -s_in, s_in), 'Wv': jax.random.uniform(ks[5], (D_MODEL, D_V * N_HEADS), jnp.float32, -s_in, s_in), 'bv': jax.random.uniform(ks[6], (D_V * N_HEADS,), jnp.float32, -s_in, s_in), 'Wo': jax.random.uniform(ks[7], (D_V * N_HEADS, D_MODEL), jnp.float32, -s_out, s_out)}
    _L0_attn_in = _L0_attn_setup()

    def _L0_ffn_setup():
        import jax, jax.numpy as jnp
        import numpy as np
        D_IN, D_HID = (128, 512)

        def _ternary(key, shape):
            return jax.random.randint(key, shape, -1, 2).astype(jnp.float32)

        def _tlin(x, w, s):
            return jnp.einsum('bsi,oi->bso', x, w) * s
        key = jax.random.key(seed)
        ks = jax.random.split(key, 12)
        inv = lambda fan: 1.0 / np.sqrt(fan).astype(np.float32)
        return {'x': jax.random.normal(ks[0], (4, 256, D_IN), dtype=jnp.float32), 'w1_w': _ternary(ks[1], (D_HID, D_IN)), 'w1_s': jax.random.uniform(ks[2], (D_HID,), dtype=jnp.float32) * inv(D_IN), 'w2_w': _ternary(ks[3], (D_HID, D_IN)), 'w2_s': jax.random.uniform(ks[4], (D_HID,), dtype=jnp.float32) * inv(D_IN), 'h1_w': _ternary(ks[5], (D_HID, D_HID)), 'h1_s': jax.random.uniform(ks[6], (D_HID,), dtype=jnp.float32) * inv(D_HID), 'h2_w': _ternary(ks[7], (D_HID, D_HID)), 'h2_s': jax.random.uniform(ks[8], (D_HID,), dtype=jnp.float32) * inv(D_HID), 'w3_w': _ternary(ks[9], (D_IN, D_HID)), 'w3_s': jax.random.uniform(ks[10], (D_IN,), dtype=jnp.float32) * inv(D_HID)}
    _L0_ffn_in = _L0_ffn_setup()

    def _L1_attn_setup():
        import jax, jax.numpy as jnp
        import numpy as np
        D_MODEL = 128
        D_STATE = 16
        D_CONV = 4
        EXPAND = 2
        D_INNER = EXPAND * D_MODEL
        DT_RANK = (D_MODEL + 15) // 16
        B, L = (1, 256)

        def _silu(v):
            return v * jax.nn.sigmoid(v)

        def _mamba_fwd(x, in_proj_w, conv_w, conv_b, x_proj_w, dt_proj_w, dt_proj_b, A_log, D_param, out_proj_w):
            b, l, _ = x.shape
            d_state = A_log.shape[1]
            dt_rank = dt_proj_w.shape[1]
            xz = x @ in_proj_w.T
            x_inner, z = jnp.split(xz, 2, axis=-1)
            x_c = jax.lax.conv_general_dilated(x_inner.transpose(0, 2, 1), conv_w, window_strides=(1,), padding=[(conv_w.shape[-1] - 1, 0)], feature_group_count=x_inner.shape[-1], dimension_numbers=('NCH', 'OIH', 'NCH'))
            x_conv = _silu((x_c + conv_b[None, :, None]).transpose(0, 2, 1))
            x_dbl = x_conv @ x_proj_w.T
            dt_lr = x_dbl[..., :dt_rank]
            B_ssm = x_dbl[..., dt_rank:dt_rank + d_state]
            C_ssm = x_dbl[..., dt_rank + d_state:]
            dt = jax.nn.softplus(dt_lr @ dt_proj_w.T + dt_proj_b)
            A = -jnp.exp(A_log)
            dA = jnp.exp(jnp.einsum('bld,dn->bldn', dt, A))
            dBx = jnp.einsum('bld,bln->bldn', dt * x_conv, B_ssm)

            def step(h, inp):
                a_t, bx_t, c_t = inp
                h = a_t * h + bx_t
                y_t = jnp.einsum('bdn,bn->bd', h, c_t)
                return (h, y_t)
            h0 = jnp.zeros((b, x_conv.shape[-1], d_state), dtype=x.dtype)
            _, ys = jax.lax.scan(step, h0, (dA.transpose(1, 0, 2, 3), dBx.transpose(1, 0, 2, 3), C_ssm.transpose(1, 0, 2)))
            y = ys.transpose(1, 0, 2) + x_conv * D_param
            return y * _silu(z) @ out_proj_w.T
        key = jax.random.key(seed)
        ks = jax.random.split(key, 8)
        s = lambda fan_in: 1.0 / np.sqrt(fan_in)
        x = jax.random.normal(ks[0], (B, L, D_MODEL), dtype=jnp.float32)
        in_proj_w = jax.random.normal(ks[1], (2 * D_INNER, D_MODEL), dtype=jnp.float32) * s(D_MODEL)
        conv_w = jax.random.normal(ks[2], (D_INNER, 1, D_CONV), dtype=jnp.float32) * s(D_CONV)
        conv_b = jax.random.normal(ks[3], (D_INNER,), dtype=jnp.float32) * s(D_CONV)
        x_proj_w = jax.random.normal(ks[4], (DT_RANK + 2 * D_STATE, D_INNER), dtype=jnp.float32) * s(D_INNER)
        dt_proj_w = jax.random.normal(ks[5], (D_INNER, DT_RANK), dtype=jnp.float32) * s(DT_RANK)
        dt_proj_b = jax.random.normal(ks[6], (D_INNER,), dtype=jnp.float32) * s(DT_RANK)
        A_log = jnp.log(jnp.arange(1, D_STATE + 1, dtype=jnp.float32))[None, :] * jnp.ones((D_INNER, 1), jnp.float32)
        D_param = jnp.ones((D_INNER,), dtype=jnp.float32)
        out_proj_w = jax.random.normal(ks[7], (D_MODEL, D_INNER), dtype=jnp.float32) * s(D_INNER)
        return {'x': x, 'in_proj_w': in_proj_w, 'conv_w': conv_w, 'conv_b': conv_b, 'x_proj_w': x_proj_w, 'dt_proj_w': dt_proj_w, 'dt_proj_b': dt_proj_b, 'A_log': A_log, 'D_param': D_param, 'out_proj_w': out_proj_w}
    _L1_attn_in = _L1_attn_setup()

    def _L1_ffn_setup():
        import jax, jax.numpy as jnp
        import numpy as np
        EPS = 1e-05

        def _quantize(W):
            gamma = jnp.mean(jnp.abs(W))
            return jnp.clip(jnp.round(W / (gamma + EPS)), -1.0, 1.0)
        key = jax.random.key(seed)
        k_x, k_w1, k_b1, k_w2, k_b2 = jax.random.split(key, 5)
        n_embd = 128
        d_ff = 4 * n_embd
        B, S = (4, 512)
        bound1 = 1.0 / np.sqrt(n_embd)
        bound2 = 1.0 / np.sqrt(d_ff)
        x = jax.random.normal(k_x, (B, S, n_embd), dtype=jnp.float32)
        W1 = jax.random.uniform(k_w1, (d_ff, n_embd), jnp.float32, -bound1, bound1)
        b1 = jax.random.uniform(k_b1, (d_ff,), jnp.float32, -bound1, bound1)
        W2 = jax.random.uniform(k_w2, (n_embd, d_ff), jnp.float32, -bound2, bound2)
        b2 = jax.random.uniform(k_b2, (n_embd,), jnp.float32, -bound2, bound2)
        return {'x': x, 'W1': W1, 'b1': b1, 'W2': W2, 'b2': b2}
    _L1_ffn_in = _L1_ffn_setup()
    _d = {'L0_attn_x': _L0_attn_in['x'], 'L0_attn_Wq': _L0_attn_in['Wq'], 'L0_attn_bq': _L0_attn_in['bq'], 'L0_attn_Wk': _L0_attn_in['Wk'], 'L0_attn_bk': _L0_attn_in['bk'], 'L0_attn_Wv': _L0_attn_in['Wv'], 'L0_attn_bv': _L0_attn_in['bv'], 'L0_attn_Wo': _L0_attn_in['Wo'], 'L0_ffn_w1_w': _L0_ffn_in['w1_w'], 'L0_ffn_w1_s': _L0_ffn_in['w1_s'], 'L0_ffn_w2_w': _L0_ffn_in['w2_w'], 'L0_ffn_w2_s': _L0_ffn_in['w2_s'], 'L0_ffn_h1_w': _L0_ffn_in['h1_w'], 'L0_ffn_h1_s': _L0_ffn_in['h1_s'], 'L0_ffn_h2_w': _L0_ffn_in['h2_w'], 'L0_ffn_h2_s': _L0_ffn_in['h2_s'], 'L0_ffn_w3_w': _L0_ffn_in['w3_w'], 'L0_ffn_w3_s': _L0_ffn_in['w3_s'], 'L1_attn_in_proj_w': _L1_attn_in['in_proj_w'], 'L1_attn_conv_w': _L1_attn_in['conv_w'], 'L1_attn_conv_b': _L1_attn_in['conv_b'], 'L1_attn_x_proj_w': _L1_attn_in['x_proj_w'], 'L1_attn_dt_proj_w': _L1_attn_in['dt_proj_w'], 'L1_attn_dt_proj_b': _L1_attn_in['dt_proj_b'], 'L1_attn_A_log': _L1_attn_in['A_log'], 'L1_attn_D_param': _L1_attn_in['D_param'], 'L1_attn_out_proj_w': _L1_attn_in['out_proj_w'], 'L1_ffn_W1': _L1_ffn_in['W1'], 'L1_ffn_b1': _L1_ffn_in['b1'], 'L1_ffn_W2': _L1_ffn_in['W2'], 'L1_ffn_b2': _L1_ffn_in['b2']}
    _x0 = _d['L0_attn_x']
    _d['L0_attn_x'] = jax.random.normal(jax.random.fold_in(jax.random.key(seed), 1), (4, 1024, 128), dtype=_x0.dtype)
    del _x0
    return _d

def reference(L0_attn_x, L0_attn_Wq, L0_attn_bq, L0_attn_Wk, L0_attn_bk, L0_attn_Wv, L0_attn_bv, L0_attn_Wo, L0_ffn_w1_w, L0_ffn_w1_s, L0_ffn_w2_w, L0_ffn_w2_s, L0_ffn_h1_w, L0_ffn_h1_s, L0_ffn_h2_w, L0_ffn_h2_s, L0_ffn_w3_w, L0_ffn_w3_s, L1_attn_in_proj_w, L1_attn_conv_w, L1_attn_conv_b, L1_attn_x_proj_w, L1_attn_dt_proj_w, L1_attn_dt_proj_b, L1_attn_A_log, L1_attn_D_param, L1_attn_out_proj_w, L1_ffn_W1, L1_ffn_b1, L1_ffn_W2, L1_ffn_b2):

    def _L0_attn_ref(x, Wq, bq, Wk, bk, Wv, bv, Wo):
        import jax, jax.numpy as jnp
        import numpy as np
        D_MODEL, D_K, D_V, N_HEADS = (128, 64, 64, 16)
        BATCH, N_CTX = (2, 256)

        def half_causal_allowed(n):
            i = jnp.arange(n)[:, None]
            j = jnp.arange(n)[None, :]
            top = (i < n // 2) & (j < n // 2)
            bot = (i >= n // 2) & (j <= i)
            return top | bot
        b, n, _ = x.shape
        h, dk, dv = (N_HEADS, D_K, D_V)
        q = (x @ Wq + bq).reshape(b, n, h, dk).transpose(0, 2, 1, 3)
        k = (x @ Wk + bk).reshape(b, n, h, dk).transpose(0, 2, 1, 3)
        v = (x @ Wv + bv).reshape(b, n, h, dv).transpose(0, 2, 1, 3)
        scores = jnp.einsum('bhqd,bhkd->bhqk', q / jnp.sqrt(jnp.float32(dk)), k)
        allowed = half_causal_allowed(n)
        scores = jnp.where(allowed, scores, -jnp.inf)
        attn = jax.nn.softmax(scores, axis=-1)
        out = jnp.einsum('bhqk,bhkd->bhqd', attn, v)
        out = out.transpose(0, 2, 1, 3).reshape(b, n, h * dv)
        return out @ Wo

    def _L0_ffn_ref(x, w1_w, w1_s, w2_w, w2_s, h1_w, h1_s, h2_w, h2_s, w3_w, w3_s):
        import jax, jax.numpy as jnp
        import numpy as np
        D_IN, D_HID = (128, 512)

        def _ternary(key, shape):
            return jax.random.randint(key, shape, -1, 2).astype(jnp.float32)

        def _tlin(x, w, s):
            return jnp.einsum('bsi,oi->bso', x, w) * s
        h = jax.nn.silu(_tlin(x, w1_w, w1_s)) * _tlin(x, w2_w, w2_s)
        h = jax.nn.gelu(_tlin(h, h1_w, h1_s), approximate=False)
        h = jax.nn.gelu(_tlin(h, h2_w, h2_s), approximate=False)
        return _tlin(h, w3_w, w3_s)

    def _L1_attn_ref(x, in_proj_w, conv_w, conv_b, x_proj_w, dt_proj_w, dt_proj_b, A_log, D_param, out_proj_w):
        import jax, jax.numpy as jnp
        import numpy as np
        D_MODEL = 128
        D_STATE = 16
        D_CONV = 4
        EXPAND = 2
        D_INNER = EXPAND * D_MODEL
        DT_RANK = (D_MODEL + 15) // 16
        B, L = (1, 256)

        def _silu(v):
            return v * jax.nn.sigmoid(v)

        def _mamba_fwd(x, in_proj_w, conv_w, conv_b, x_proj_w, dt_proj_w, dt_proj_b, A_log, D_param, out_proj_w):
            b, l, _ = x.shape
            d_state = A_log.shape[1]
            dt_rank = dt_proj_w.shape[1]
            xz = x @ in_proj_w.T
            x_inner, z = jnp.split(xz, 2, axis=-1)
            x_c = jax.lax.conv_general_dilated(x_inner.transpose(0, 2, 1), conv_w, window_strides=(1,), padding=[(conv_w.shape[-1] - 1, 0)], feature_group_count=x_inner.shape[-1], dimension_numbers=('NCH', 'OIH', 'NCH'))
            x_conv = _silu((x_c + conv_b[None, :, None]).transpose(0, 2, 1))
            x_dbl = x_conv @ x_proj_w.T
            dt_lr = x_dbl[..., :dt_rank]
            B_ssm = x_dbl[..., dt_rank:dt_rank + d_state]
            C_ssm = x_dbl[..., dt_rank + d_state:]
            dt = jax.nn.softplus(dt_lr @ dt_proj_w.T + dt_proj_b)
            A = -jnp.exp(A_log)
            dA = jnp.exp(jnp.einsum('bld,dn->bldn', dt, A))
            dBx = jnp.einsum('bld,bln->bldn', dt * x_conv, B_ssm)

            def step(h, inp):
                a_t, bx_t, c_t = inp
                h = a_t * h + bx_t
                y_t = jnp.einsum('bdn,bn->bd', h, c_t)
                return (h, y_t)
            h0 = jnp.zeros((b, x_conv.shape[-1], d_state), dtype=x.dtype)
            _, ys = jax.lax.scan(step, h0, (dA.transpose(1, 0, 2, 3), dBx.transpose(1, 0, 2, 3), C_ssm.transpose(1, 0, 2)))
            y = ys.transpose(1, 0, 2) + x_conv * D_param
            return y * _silu(z) @ out_proj_w.T
        return _mamba_fwd(x, in_proj_w, conv_w, conv_b, x_proj_w, dt_proj_w, dt_proj_b, A_log, D_param, out_proj_w)

    def _L1_ffn_ref(x, W1, b1, W2, b2):
        import jax, jax.numpy as jnp
        import numpy as np
        EPS = 1e-05

        def _quantize(W):
            gamma = jnp.mean(jnp.abs(W))
            return jnp.clip(jnp.round(W / (gamma + EPS)), -1.0, 1.0)
        Wq1 = _quantize(W1)
        Wq2 = _quantize(W2)
        h = jax.nn.relu(jnp.einsum('bsd,fd->bsf', x, Wq1) + b1)
        out = jnp.einsum('bsf,df->bsd', h, Wq2) + b2
        return out
    x = L0_attn_x
    x = _layernorm(x + _L0_attn_ref(x, L0_attn_Wq, L0_attn_bq, L0_attn_Wk, L0_attn_bk, L0_attn_Wv, L0_attn_bv, L0_attn_Wo), axis=-1)
    x = _layernorm(x + _L0_ffn_ref(x, L0_ffn_w1_w, L0_ffn_w1_s, L0_ffn_w2_w, L0_ffn_w2_s, L0_ffn_h1_w, L0_ffn_h1_s, L0_ffn_h2_w, L0_ffn_h2_s, L0_ffn_w3_w, L0_ffn_w3_s), axis=-1)
    x = _layernorm(x + _L1_attn_ref(x, L1_attn_in_proj_w, L1_attn_conv_w, L1_attn_conv_b, L1_attn_x_proj_w, L1_attn_dt_proj_w, L1_attn_dt_proj_b, L1_attn_A_log, L1_attn_D_param, L1_attn_out_proj_w), axis=-1)
    x = _layernorm(x + _L1_ffn_ref(x, L1_ffn_W1, L1_ffn_b1, L1_ffn_W2, L1_ffn_b2), axis=-1)
    return x

_drawn_inputs = setup_inputs


def setup_inputs(seed=0):
    import zlib

    import numpy as np

    out = dict(_drawn_inputs(seed))
    spreads = {'L1_attn_D_param': (1.0, 0.2)}
    factors = {'L0_attn_Wq': 3.981,
     'L0_attn_bq': 8.0,
     'L0_attn_Wk': 3.925,
     'L0_attn_bk': 200.0,
     'L0_ffn_w1_w': 8.0,
     'L0_ffn_w1_s': 8.0,
     'L0_ffn_w2_w': 8.0,
     'L0_ffn_w2_s': 8.0,
     'L0_ffn_h1_w': 8.0,
     'L0_ffn_h1_s': 8.0,
     'L0_ffn_h2_w': 8.0,
     'L0_ffn_h2_s': 8.0,
     'L0_ffn_w3_w': 8.0,
     'L0_ffn_w3_s': 8.0,
     'L1_ffn_b1': 8.0,
     'L1_ffn_b2': 200.0}
    for name, (base, spread) in spreads.items():
        noise = np.random.default_rng([zlib.crc32(name.encode()), seed]).standard_normal(out[name].shape)
        drawn = base * np.exp(spread * noise) if base else spread * noise
        out[name] = jnp.asarray(drawn.astype(out[name].dtype))
    for name, factor in factors.items():
        out[name] = (out[name] * factor).astype(out[name].dtype)
    return out
```

```python
from contextlib import ExitStack

import concourse.bass as bass
from concourse import mybir

ALU = mybir.AluOpType
ACT = mybir.ActivationFunctionType
AX = mybir.AxisListType
F32 = mybir.dt.float32
F32R = mybir.dt.float32r
BF16 = mybir.dt.bfloat16

P = 128
BANK = 512
BATCH, CTX, D = 4, 1024, 128
TOK = BATCH * CTX
HEADS, DK = 16, 64
PAIRS = HEADS // 2
CHUNKS = TOK // BANK
TILES = BANK // P
HID = 512
EPS = 1e-5

WQ, WK, WV = 0, 256, 512
WBQ, WBK, WBV = 640, 642, 644
WCOLS = 772


def attention(nc, xT, wpk, ident, mask, ot_d):
    ITERS = BATCH * PAIRS
    NT = CTX // P
    STEPS = 2 * NT
    LAG = 3
    UNITS = 8
    PJ = UNITS + 2

    def width(t):
        return 512 if t < 4 else P * (t + 1)

    def pieces(s):
        t = s % NT
        if t < 4:
            return [(0, 0, 4, "act")] if t % 2 == 0 else [(1, 0, 4, "dve")]
        a, d = ("act", "dve") if t % 2 == 0 else ("dve", "act")
        return [(0, 0, 4, a), (1, 4, t - 3, d)]

    def copied(who, s, upto=None):
        n = sum(e == who for u in range(s) for _, _, _, e in pieces(u))
        return n + sum(e == who for _, _, _, e in pieces(s)[:upto or 0])

    ACOP, DCOP = copied("act", STEPS), copied("dve", STEPS)

    def last_copy(s, bank):
        for u in range(s - 1, -1, -1):
            for k, (b, _, _, e) in enumerate(pieces(u)):
                if b == bank:
                    return e, copied(e, u, k + 1)
        return None

    SLOT_UNIT = {8: [2], 9: [3], 10: [4], 11: [5], 12: [6], 13: [7], 14: [8], 15: [9]}
    SLOT_V = {1: [0], 2: [1]}
    PV0_SLOT = 13

    with ExitStack() as ctx:
        def sb(name, shape, dt):
            return ctx.enter_context(nc.sbuf_tensor(name, shape, dt))

        def sem(name):
            return ctx.enter_context(nc.semaphore(name))

        xh = sb("a_xh", [P, TOK], F32R)
        xl = sb("a_xl", [P, TOK], F32R)
        xb = sb("a_xb", [P, 2, CTX], F32)
        w = sb("a_w", [P, WCOLS], F32)
        wh = sb("a_wh", [P, 512], F32R)
        wl = sb("a_wl", [P, 512], F32R)
        qs = sb("a_qs", [P, 2, CTX], F32R)
        kh = sb("a_kh", [P, 2, CTX], F32R)
        kl = sb("a_kl", [P, 2, CTX], F32R)
        v = sb("a_v", [P, NT, P], F32)
        p = sb("a_p", [P, 4, CTX], F32)
        pt0 = sb("a_pt0", [P, 2, 4, 512], F32)
        pt1 = sb("a_pt1", [P, 2, 8, 512], F32)
        ots = sb("a_ots", [P, 2, 512], F32)
        nmax = sb("a_nmax", [P, STEPS], F32)
        rsum = sb("a_rsum", [P, STEPS], F32)
        rinv = sb("a_rinv", [P, STEPS], F32)
        idf = sb("a_idf", [P, P], F32)
        mkf = sb("a_mkf", [P, P], F32)
        idb = sb("a_idb", [P, P], BF16)
        mkb = sb("a_mkb", [P, P], BF16)

        ps = ctx.enter_context(nc.psum_tensor("a_ps", [P, 2, 1024], F32))
        pt = ctx.enter_context(nc.psum_tensor("a_pt", [P, 2, 4, P], F32))
        po = ctx.enter_context(nc.psum_tensor("a_po", [P, BANK], F32))
        pj = ctx.enter_context(nc.psum_tensor("a_pj", [P, BANK], F32))

        held = sem("a_held")
        const_in = sem("a_const_in")
        const_ok = sem("a_const_ok")
        xin = [sem(f"a_xin{i}") for i in range(2)]
        x_hi = sem("a_x_hi")
        x_lo = sem("a_x_lo")
        w_in = sem("a_w_in")
        xb_in = sem("a_xb_in")
        w_scaled = sem("a_w_scaled")
        w_split = sem("a_w_split")
        pj_done = sem("a_pj_done")
        pj_hi = sem("a_pj_hi")
        pj_free = sem("a_pj_free")
        s_done = sem("a_s_done")
        max_done = sem("a_max_done")
        exp_done = sem("a_exp_done")
        rinv_done = sem("a_rinv_done")
        norm_done = sem("a_norm_done")
        t_done = sem("a_t_done")
        t_act = sem("a_t_act")
        t_dve = sem("a_t_dve")
        pv_done = sem("a_pv_done")
        o_copied = sem("a_o_copied")
        o_out = [sem(f"a_o_out{i}") for i in range(2)]

        def unit(n):
            n -= 2
            return n // 4, (n % 4) >= 2, n % 2

        block = ctx.enter_context(nc.Block())

        @block.sync
        def _(sp):
            sp.dma_start(idf[:, :], ident).then_inc(const_in, 16)
            sp.dma_start(mkf[:, :], mask).then_inc(const_in, 16)
            sp.dma_start(w[:, :], wpk[0]).then_inc(w_in, 16)
            for b in range(BATCH):
                if b >= 2:
                    sp.wait_ge(x_lo, b - 1)
                sp.dma_start(xb[:, b % 2, :], xT[:, b * CTX:(b + 1) * CTX]).then_inc(xin[b % 2], 16)
            sp.wait_ge(x_lo, BATCH)
            sp.dma_start(xb[:, 0, :], xT[:, 0:CTX]).then_inc(xb_in, 16)

            def outputs(it, c):
                sp.wait_ge(o_copied, 2 * it + c + 1)
                sp.dma_start(ot_d[2 * (it // PAIRS) + c, :, it % PAIRS, :], ots[:, c, :]).then_inc(o_out[c], 16)

            with sp.Fori(0, ITERS - 1) as it:
                sp.wait_ge(pj_free, UNITS + PJ * it + 2)
                sp.dma_start(w[:, :], wpk[(it + 1) % PAIRS]).then_inc(w_in, 16)
                sp.dma_start(xb[:, 0, :], xT[:, bass.ds(((it + 1) // PAIRS) * CTX, CTX)]).then_inc(xb_in, 16)
                outputs(it, 0)
                outputs(it, 1)
            outputs(ITERS - 1, 0)
            outputs(ITERS - 1, 1)
            for c in range(2):
                sp.wait_ge(o_out[c], 16 * ITERS)

        @block.gpsimd
        def _(pool):
            def split_weights(i):
                pool.wait_ge(w_in, 16 * (i + 1))
                pool.sem_inc(held, 1)
                pool.tensor_scalar(w[:, WQ:WQ + 256], w[:, WQ:WQ + 256], 0.125, 1.0, ALU.mult,
                                   ALU.mult).then_inc(w_scaled, 1)
                pool.tensor_scalar(w[:, WBQ:WBQ + 2], w[:, WBQ:WBQ + 2], 0.125, 1.0, ALU.mult,
                                   ALU.mult).then_inc(w_scaled, 1)
                pool.wait_ge(w_scaled, 3 * i + 2)
                pool.sem_inc(held, 1)
                pool.tensor_scalar(wh[:, :], w[:, 0:512], 1.0, 1.0, ALU.mult, ALU.mult).then_inc(w_scaled, 1)
                pool.wait_ge(w_scaled, 3 * i + 3)
                pool.tensor_tensor(wl[:, :], w[:, 0:512], wh[:, :].bitcast(F32),
                                   ALU.subtract).then_inc(w_split, 1)

            def normalise(it, j):
                pool.wait_ge(rinv_done, STEPS * it + j + 1)
                pool.sem_inc(held, 1)
                t = j % NT
                pool.tensor_scalar(p[:, j % 4, 0:width(t)], p[:, j % 4, 0:width(t)],
                                   rinv[:, j % STEPS:j % STEPS + 1], 1.0, ALU.mult,
                                   ALU.mult).then_inc(norm_done, 1)

            def body(it, last):
                for s in range(STEPS):
                    if not last or s + LAG - 1 < STEPS:
                        normalise(it, s + LAG - 1)
                    if s == 4 and not last:
                        pool.wait_ge(pj_done, UNITS + PJ * it)
                        split_weights(it + 1)

            split_weights(0)
            for j in range(LAG - 1):
                normalise(0, j)
            with pool.Fori(0, ITERS - 1) as it:
                body(it, False)
            body(ITERS - 1, True)

        @block.scalar
        def _(act):
            for b in range(BATCH):
                act.wait_ge(xin[b % 2], 16 * (b // 2 + 1))
                act.activation(xh[:, b * CTX:(b + 1) * CTX], xb[:, b % 2, :], ACT.Identity).then_inc(x_hi, 1)

            def project_hi(g, m, n):
                h, query, half = unit(n)
                cols = slice(half * BANK, (half + 1) * BANK)
                act.wait_ge(pj_done, g + 1)
                dst = (qs if query else kh)[:, h, cols]
                bias = w[:, (WBQ if query else WBK) + h:(WBQ if query else WBK) + h + 1]
                act.activation(dst, pj[:, :], ACT.Identity, bias=bias).then_inc(pj_hi, 1)

            def exps(it, j):
                t = j % NT
                act.wait_ge(max_done, STEPS * it + j + 1)
                if not isinstance(it, int) or j >= 4 or it > 0:
                    act.wait_ge(t_done, STEPS * it + j - 3)
                c = j % STEPS
                act.activation(p[:, j % 4, 0:width(t)], ps[:, j % 2, 0:width(t)], ACT.Exp,
                               bias=nmax[:, c:c + 1], accum_out=rsum[:, c:c + 1]).then_inc(exp_done, 1)

            def copy_pieces(it, s):
                h, t = s // NT, s % NT
                dst = pt0 if t < 4 else pt1
                for bank, j0, n, who in pieces(s):
                    if who == "act":
                        act.wait_ge(t_done, STEPS * it + s + 1)
                        act.activation(dst[:, h, j0:j0 + n, (t % 4) * P:(t % 4 + 1) * P], pt[:, bank, 0:n, :],
                                       ACT.Copy).then_inc(t_act, 1)

            def copy_output(it, c):
                act.wait_ge(pv_done, 2 * it + c + 1)
                act.wait_ge(o_out[c], 16 * it)
                act.activation(ots[:, c, :], po[:, :], ACT.Copy).then_inc(o_copied, 1)

            def body(it, last):
                for s in range(STEPS):
                    copy_pieces(it, s)
                    if not last or s + LAG < STEPS:
                        exps(it, s + LAG)
                    if not last:
                        for n in SLOT_UNIT.get(s, []):
                            project_hi(UNITS + PJ * it + n, UNITS * (it + 1) + n - 2, n)
                    if s == PV0_SLOT:
                        copy_output(it, 0)
                copy_output(it, 1)

            for n in range(2, PJ):
                project_hi(n - 2, n - 2, n)
            for j in range(LAG):
                exps(0, j)
            with act.Fori(0, ITERS - 1) as it:
                body(it, False)
            body(ITERS - 1, True)

        @block.tensor
        def _(pe):
            def project(g, n, b):
                h, query, half = unit(n)
                cols = slice((WQ if query else WK) + P * h, (WQ if query else WK) + P * (h + 1))
                pe.wait_ge(pj_free, g)
                at = b * CTX + half * BANK
                moving = [x[:, bass.ds(at, BANK)] for x in (xh, xl)]
                pe.matmul(pj[:, :], wh[:, cols], moving[0], start=True, stop=False)
                pe.matmul(pj[:, :], wh[:, cols], moving[1], start=False, stop=False)
                pe.matmul(pj[:, :], wl[:, cols], moving[0], start=False, stop=True).then_inc(pj_done, 1)

            def values(it, half):
                pe.wait_ge(xb_in, 16 * (it + 1))
                pe.wait_ge(pj_free, UNITS + PJ * it + half)
                for k in range(4):
                    t = 4 * half + k
                    m = pe.matmul(pj[:, k * P:(k + 1) * P], xb[:, 0, t * P:(t + 1) * P], w[:, WV:WV + P],
                                  start=True, stop=True)
                m.then_inc(pj_done, 1)

            def scores(it, j):
                h, t = (j // NT) % 2, j % NT
                if not isinstance(it, int) or j >= 2 or it > 0:
                    pe.wait_ge(exp_done, STEPS * it + j - 1)
                q = qs[:, h, t * P:(t + 1) * P]
                for lo in range(0, width(t), BANK):
                    hi = min(lo + BANK, width(t))
                    dst = ps[:, j % 2, lo:hi]
                    diag = t >= 4 and hi == width(t)
                    pe.matmul(dst, q, kh[:, h, lo:hi], start=True, stop=False)
                    m = pe.matmul(dst, q, kl[:, h, lo:hi], start=False, stop=not diag)
                if t >= 4:
                    m = pe.matmul(ps[:, j % 2, width(t) - P:width(t)], idb[:, :], mkb[:, :],
                                  start=False, stop=True)
                m.then_inc(s_done, 1)

            def transposes(it, s):
                pe.wait_ge(norm_done, STEPS * it + s + 1)
                t = s % NT
                for bank, j0, n, who in pieces(s):
                    found = last_copy(s, bank)
                    if found:
                        pe.wait_ge(t_act if found[0] == "act" else t_dve,
                                   (ACOP if found[0] == "act" else DCOP) * it + found[1])
                    else:
                        pe.wait_ge(t_act, ACOP * it)
                        pe.wait_ge(t_dve, DCOP * it)
                    for k in range(n):
                        j = j0 + k
                        m = pe.transpose(pt[:, bank, k, :], p[:, s % 4, j * P:(j + 1) * P], idf[:, :])
                m.then_inc(t_done, 1)

            def outputs(it, c):
                last = NT + 4 * c + 3
                pe.wait_ge(t_act, ACOP * it + copied("act", last + 1))
                pe.wait_ge(t_dve, DCOP * it + copied("dve", last + 1))
                if c == 0:
                    pe.wait_ge(pj_free, UNITS + PJ * it + 2)
                pe.wait_ge(o_copied, 2 * it + c)
                src = pt1 if c else pt0
                blocks = 4 * c + 4
                for j in range(blocks):
                    lo = max(0, (j - 4) * P)
                    for h in range(2):
                        m = pe.matmul(po[h * DK:(h + 1) * DK, lo:BANK], v[:, j, h * DK:(h + 1) * DK],
                                      src[:, h, j, lo:BANK], start=(j == 0), stop=(j == blocks - 1))
                m.then_inc(pv_done, 1)

            def body(it, last):
                for s in range(STEPS):
                    if not last or s + LAG < STEPS:
                        scores(it, s + LAG)
                    transposes(it, s)
                    for half in SLOT_V.get(s, []):
                        values(it, half)
                    if not last:
                        for n in SLOT_UNIT.get(s, []):
                            if n == 2:
                                pe.wait_ge(w_split, it + 2)
                            project(UNITS + PJ * it + n, n, (it + 1) // PAIRS)
                    if s == PV0_SLOT:
                        outputs(it, 0)
                outputs(it, 1)

            pe.wait_ge(x_lo, BATCH)
            pe.wait_ge(w_split, 1)
            for n in range(2, PJ):
                project(n - 2, n, 0)
            pe.wait_ge(pj_free, UNITS)
            pe.wait_ge(const_ok, 2)
            for j in range(LAG):
                scores(0, j)
            with pe.Fori(0, ITERS - 1) as it:
                body(it, False)
            body(ITERS - 1, True)

        @block.vector
        def _(dve):
            dve.wait_ge(const_in, 32)
            dve.tensor_copy(idb[:, :], idf[:, :]).then_inc(const_ok, 1)
            dve.tensor_copy(mkb[:, :], mkf[:, :]).then_inc(const_ok, 1)
            for b in range(BATCH):
                dve.wait_ge(x_hi, b + 1)
                cols = slice(b * CTX, (b + 1) * CTX)
                dve.tensor_tensor(xl[:, cols], xb[:, b % 2, :], xh[:, cols].bitcast(F32),
                                  ALU.subtract).then_inc(x_lo, 1)

            def project_lo(m, n):
                h, query, half = unit(n)
                cols = slice(half * BANK, (half + 1) * BANK)
                dve.wait_ge(pj_hi, m + 1)
                rows = slice(DK, P) if query else slice(0, P)
                dst = (qs if query else kl)[rows, h, cols]
                hi = (qs if query else kh)[rows, h, cols].bitcast(F32)
                at = (WBQ if query else WBK) + h
                dve.scalar_tensor_tensor(dst, pj[rows, :], w[rows, at:at + 1], hi, ALU.add,
                                         ALU.subtract).then_inc(pj_free, 1)

            def values(it, half):
                dve.wait_ge(pj_done, UNITS + PJ * it + half + 1)
                bias = w[:, WBV:WBV + P].unsqueeze(1).to_broadcast([P, 4, P])
                dve.tensor_tensor(v[:, 4 * half:4 * half + 4, :], pj[:, :].rearrange("p (t d) -> p t d", t=4),
                                  bias, ALU.add).then_inc(pj_free, 1)

            def maxima(it, j):
                t = j % NT
                dve.wait_ge(s_done, STEPS * it + j + 1)
                c = j % STEPS
                dve.tensor_reduce(nmax[:, c:c + 1], ps[:, j % 2, 0:width(t)], AX.X, ALU.max,
                                  negate=True).then_inc(max_done, 1)

            def inverse(it, j):
                dve.wait_ge(exp_done, STEPS * it + j + 1)
                c = j % STEPS
                dve.reciprocal(rinv[:, c:c + 1], rsum[:, c:c + 1]).then_inc(rinv_done, 1)

            def copy_pieces(it, s):
                h, t = s // NT, s % NT
                dst = pt0 if t < 4 else pt1
                for bank, j0, n, who in pieces(s):
                    if who == "dve":
                        dve.wait_ge(t_done, STEPS * it + s + 1)
                        dve.tensor_copy(dst[:, h, j0:j0 + n, (t % 4) * P:(t % 4 + 1) * P],
                                        pt[:, bank, 0:n, :]).then_inc(t_dve, 1)

            def body(it, last):
                for s in range(STEPS):
                    if not last or s + LAG < STEPS:
                        maxima(it, s + LAG)
                    if not last or s + LAG - 1 < STEPS:
                        inverse(it, s + LAG - 1)
                    copy_pieces(it, s)
                    for half in SLOT_V.get(s, []):
                        values(it, half)
                    if not last:
                        for n in SLOT_UNIT.get(s, []):
                            project_lo(UNITS * (it + 1) + n - 2, n)

            for n in range(2, PJ):
                project_lo(n - 2, n)
            for j in range(LAG):
                maxima(0, j)
                if j < LAG - 1:
                    inverse(0, j)
            with dve.Fori(0, ITERS - 1) as it:
                body(it, False)
            body(ITERS - 1, True)


def gated_ffn(nc, ot_d, x_tok, wo, w_in, w_hid, w_out, scales, s3, ident, y_d):
    KC = HID // P
    UN = 4 * KC
    LN1, LN2 = 5, 6
    LINKS = LN1 + LN2

    with ExitStack() as ctx:
        def sb(name, shape, dt):
            return ctx.enter_context(nc.sbuf_tensor(name, shape, dt))

        def sem(name):
            return ctx.enter_context(nc.semaphore(name))

        ot = sb("f_ot", [P, PAIRS, BANK], F32)
        xt = sb("f_xt", [P, TILES, P], F32)
        wo_s = sb("f_wo", [P, PAIRS, P], F32)
        raw = sb("f_raw", [P, KC * HID], F32)
        w12h = sb("f_w12h", [P, 2, HID], F32R)
        w12l = sb("f_w12l", [P, 2, HID], F32R)
        hh = sb("f_hh", [P, 2, KC, HID], F32R)
        hl = sb("f_hl", [P, 2, KC, HID], F32R)
        w3h = sb("f_w3h", [P, KC, P], F32R)
        w3l = sb("f_w3l", [P, KC, P], F32R)
        sc = sb("f_sc", [P, 4, KC], F32)
        s3b = sb("f_s3b", [P, P], F32)
        idf = sb("f_idf", [P, P], F32)
        half = sb("f_half", [P, TILES], F32)
        r1 = sb("f_r1", [P, TILES, P], F32)
        r2 = sb("f_r2", [P, TILES, P], F32)
        x1n = sb("f_x1n", [P, TILES, P], F32)
        x1 = sb("f_x1", [P, TILES, P], F32)
        x1h = sb("f_x1h", [P, BANK], F32R)
        x1l = sb("f_x1l", [P, BANK], F32R)
        gate = sb("f_gate", [P, 2, BANK], F32)
        act_f = sb("f_act", [P, 4, BANK], F32)
        ah = sb("f_ah", [P, 3, KC, BANK], F32R)
        al = sb("f_al", [P, 3, KC, BANK], F32R)
        y2 = sb("f_y2", [P, TILES, P], F32)
        st = sb("f_st", [P, TILES, 6], F32)
        mv = sb("f_mv", [P, TILES, 2], F32)
        ve = sb("f_ve", [P, TILES], F32)
        rstd = sb("f_rstd", [P, TILES], F32)

        pu = ctx.enter_context(nc.psum_tensor("f_pu", [P, 4, BANK], F32))
        py = ctx.enter_context(nc.psum_tensor("f_py", [P, TILES, P], F32))
        pz = ctx.enter_context(nc.psum_tensor("f_pz", [P, TILES, P], F32))

        held = sem("f_held")
        c_in = sem("f_c_in")
        raw_in = sem("f_raw_in")
        raw_hi = sem("f_raw_hi")
        raw_lo = sem("f_raw_lo")
        half_ok = sem("f_half_ok")
        ot_in = sem("f_ot_in")
        xt_in = sem("f_xt_in")
        wo_done = sem("f_wo_done")
        chain = sem("f_chain")
        pow_done = sem("f_pow_done")
        tr_done = sem("f_tr_done")
        tr_hi = sem("f_tr_hi")
        tr_lo = sem("f_tr_lo")
        u_done = sem("f_u_done")
        gate_ok = sem("f_gate_ok")
        prod_ok = sem("f_prod_ok")
        gelu_ok = sem("f_gelu_ok")
        hi_ok = sem("f_hi_ok")
        lo_ok = sem("f_lo_ok")
        z_done = sem("f_z_done")
        x1_ok = sem("f_x1_ok")
        y_out = sem("f_y_out")

        WEIGHTS = [(w12h[:, 0, :], w12l[:, 0, :], HID), (w12h[:, 1, :], w12l[:, 1, :], HID),
                   (hh[:, 0], hl[:, 0], KC * HID), (hh[:, 1], hl[:, 1], KC * HID),
                   (w3h[:, :, :], w3l[:, :, :], KC * P)]
        SOURCES = [w_in[0], w_in[1], w_hid[0], w_hid[1], w_out]

        def flat(ap):
            return ap if len(ap.shape) == 2 else ap.rearrange("p a b -> p (a b)")

        block = ctx.enter_context(nc.Block())

        @block.sync
        def _(sp):
            sp.dma_start(ot[:, :, :], ot_d[0]).then_inc(ot_in, 16)
            sp.dma_start(xt[:, :, :], x_tok[0]).then_inc(xt_in, 16)
            sp.dma_start(wo_s[:, :, :], wo).then_inc(c_in, 16)
            sp.dma_start(sc[:, :, :], scales).then_inc(c_in, 16)
            sp.dma_start(s3b[:, :], s3).then_inc(c_in, 16)
            sp.dma_start(idf[:, :], ident).then_inc(c_in, 16)
            for k, (src, (hi, lo, n)) in enumerate(zip(SOURCES, WEIGHTS)):
                if k:
                    sp.wait_ge(raw_lo, k)
                sp.dma_start(raw[:, 0:n], src).then_inc(raw_in, 16)
            sp.wait_ge(wo_done, 1)
            sp.dma_start(ot[:, :, :], ot_d[1]).then_inc(ot_in, 16)
            sp.wait_ge(chain, 1)
            sp.dma_start(xt[:, :, :], x_tok[1]).then_inc(xt_in, 16)
            with sp.Fori(0, CHUNKS - 2) as i:
                sp.wait_ge(wo_done, i + 2)
                sp.dma_start(ot[:, :, :], ot_d[i + 2]).then_inc(ot_in, 16)
                sp.wait_ge(chain, LINKS * i + LN1 + 1)
                sp.dma_start(xt[:, :, :], x_tok[i + 2]).then_inc(xt_in, 16)
                sp.wait_ge(chain, LINKS * i + LN1 + LINKS)
                sp.dma_start(y_d[i], y2[:, :, :]).then_inc(y_out, 16)
            for i in (CHUNKS - 2, CHUNKS - 1):
                sp.wait_ge(chain, LN1 + LINKS * (i + 1) - (LN1 if i == CHUNKS - 1 else 0))
                sp.dma_start(y_d[i], y2[:, :, :]).then_inc(y_out, 16)
            sp.wait_ge(y_out, 16 * CHUNKS)

        @block.gpsimd
        def _(pool):
            def power(n, at):
                pool.wait_ge(chain, at)
                pool.tensor_tensor(rstd[:, :], ve[:, :], half[:, :], ALU.pow).then_inc(pow_done, 1)

            def split(i, k):
                layer = k // KC
                if layer == 0:
                    pool.wait_ge(prod_ok, KC * i + k + 1)
                else:
                    pool.wait_ge(gelu_ok, 2 * KC * i + k - KC + 1)
                pool.sem_inc(held, 1)
                pool.tensor_scalar(ah[:, layer, k % KC, :], act_f[:, k % 4, :], 1.0, 1.0, ALU.mult,
                                   ALU.mult).then_inc(hi_ok, 1)

            def body(i, last):
                pool.wait_ge(chain, LINKS * i + LN1)
                pool.sem_inc(held, 1)
                pool.tensor_scalar(x1[:, :, :], x1n[:, :, :], 1.0, 1.0, ALU.mult, ALU.mult).then_inc(x1_ok, 1)
                for k in range(KC):
                    split(i, k)
                if not last:
                    power(2 * i + 1, LINKS * i + LN1 + 4)
                for k in range(KC, 3 * KC):
                    split(i, k)
                power(2 * i + (1 if last else 2), LINKS * i + LN1 + (0 if last else LN1) + 5)

            pool.memset(half[:, :], -0.5).then_inc(half_ok, 1)
            pool.wait_ge(half_ok, 1)
            power(0, 4)
            with pool.Fori(0, CHUNKS - 1) as i:
                body(i, False)
            body(CHUNKS - 1, True)

        @block.scalar
        def _(act):
            for k, (hi, lo, n) in enumerate(WEIGHTS):
                act.wait_ge(raw_in, 16 * (k + 1))
                act.activation(flat(hi), raw[:, 0:n], ACT.Copy).then_inc(raw_hi, 1)

            def tokens_hi(n):
                act.wait_ge(tr_done, n + 1)
                act.activation(x1h[:, :], py[:, :, :].rearrange("p t d -> p (t d)"), ACT.Copy).then_inc(tr_hi, 1)

            def body(i, last):
                for m in range(KC):
                    act.wait_ge(u_done, UN * i + 2 * m + 1)
                    if m >= 2:
                        act.wait_ge(prod_ok, KC * i + m - 1)
                    act.activation(gate[:, m % 2, :], pu[:, (2 * m) % 4, :], ACT.Silu,
                                   scale=sc[:, 0, m:m + 1]).then_inc(gate_ok, 1)
                for k in range(KC, 3 * KC):
                    act.wait_ge(u_done, UN * i + KC + k + 1)
                    act.wait_ge(lo_ok, 3 * KC * i + k - 3)
                    act.activation(act_f[:, k % 4, :], pu[:, (KC + k) % 4, :], ACT.Gelu,
                                   scale=sc[:, 1 + k // KC, k % KC:k % KC + 1]).then_inc(gelu_ok, 1)
                    if k == 2 * KC - 1 and not last:
                        tokens_hi(i + 1)

            tokens_hi(0)
            with act.Fori(0, CHUNKS - 1) as i:
                body(i, False)
            body(CHUNKS - 1, True)

        @block.tensor
        def _(pe):
            def project(n):
                pe.wait_ge(ot_in, 16 * (n + 1))
                if not isinstance(n, int):
                    pe.wait_ge(tr_lo, n)
                for t in range(TILES):
                    for r in range(PAIRS):
                        m = pe.matmul(py[:, t, :], ot[:, r, t * P:(t + 1) * P], wo_s[:, r, :],
                                      start=(r == 0), stop=(r == PAIRS - 1))
                m.then_inc(wo_done, 1)

            def transposes(n, at):
                pe.wait_ge(chain, at)
                for t in range(TILES):
                    m = pe.transpose(py[:, t, :], x1n[:, t, :], idf[:, :])
                m.then_inc(tr_done, 1)

            def unit(i, u, wh, wl, xh, xl):
                dst = pu[:, u % 4, :]
                n = len(wh)
                for k in range(n):
                    pe.matmul(dst, wh[k], xh[k], start=(k == 0), stop=False)
                    pe.matmul(dst, wh[k], xl[k], start=False, stop=False)
                    m = pe.matmul(dst, wl[k], xh[k], start=False, stop=(k == n - 1))
                m.then_inc(u_done, 1)

            def body(i, last):
                pe.wait_ge(tr_lo, i + 1)
                for u in range(2 * KC):
                    m, second = u // 2, u % 2
                    if u >= 4:
                        if second:
                            pe.wait_ge(prod_ok, KC * i + m - 1)
                        else:
                            pe.wait_ge(gate_ok, KC * i + m - 1)
                    else:
                        pe.wait_ge(gelu_ok, 2 * KC * i)
                    cols = slice(m * P, (m + 1) * P)
                    unit(i, u, [w12h[:, second, cols]], [w12l[:, second, cols]], [x1h[:, :]], [x1l[:, :]])
                if not last:
                    project(i + 1)
                for k in range(KC, 3 * KC):
                    layer, m = k // KC, k % KC
                    if layer == 1:
                        pe.wait_ge(prod_ok, KC * (i + 1))
                        pe.wait_ge(lo_ok, 3 * KC * i + KC)
                    else:
                        pe.wait_ge(gelu_ok, 2 * KC * i + m + 1)
                        pe.wait_ge(lo_ok, 3 * KC * i + 2 * KC)
                    cols = slice(m * P, (m + 1) * P)
                    unit(i, KC + k, [hh[:, layer - 1, j, cols] for j in range(KC)],
                         [hl[:, layer - 1, j, cols] for j in range(KC)],
                         [ah[:, layer - 1, j, :] for j in range(KC)], [al[:, layer - 1, j, :] for j in range(KC)])
                    if k == 2 * KC - 1 and not last:
                        transposes(i + 1, LINKS * i + 2 * LN1)
                pe.wait_ge(lo_ok, 3 * KC * (i + 1))
                pe.wait_ge(chain, LINKS * i)
                for t in range(TILES):
                    cols = slice(t * P, (t + 1) * P)
                    for j in range(KC):
                        pe.matmul(pz[:, t, :], ah[:, 2, j, cols], w3h[:, j, :], start=(j == 0), stop=False)
                        pe.matmul(pz[:, t, :], al[:, 2, j, cols], w3h[:, j, :], start=False, stop=False)
                        m = pe.matmul(pz[:, t, :], ah[:, 2, j, cols], w3l[:, j, :], start=False, stop=(j == KC - 1))
                m.then_inc(z_done, 1)

            pe.wait_ge(c_in, 64)
            project(0)
            transposes(0, LN1)
            pe.wait_ge(raw_lo, len(WEIGHTS))
            with pe.Fori(0, CHUNKS - 1) as i:
                body(i, False)
            body(CHUNKS - 1, True)

        @block.vector
        def _(dve):
            for k, (hi, lo, n) in enumerate(WEIGHTS):
                dve.wait_ge(raw_hi, k + 1)
                dve.tensor_tensor(flat(lo), raw[:, 0:n], flat(hi).bitcast(F32), ALU.subtract).then_inc(raw_lo, 1)

            def norm(r, dst, n, at):
                dve.wait_ge(chain, at)
                for t in range(TILES):
                    m = dve.bn_stats(st[:, t, :], r[:, t, :])
                m.then_inc(chain, 1)
                dve.wait_ge(chain, at + 1)
                dve.sem_inc(held, 1)
                for t in range(TILES):
                    m = dve.bn_aggr(mv[:, t, :], st[:, t, :])
                m.then_inc(chain, 1)
                dve.wait_ge(chain, at + 2)
                dve.tensor_scalar(ve[:, :], mv[:, :, 1], EPS, None, ALU.add).then_inc(chain, 1)
                dve.wait_ge(pow_done, n + 1)
                for t in range(TILES):
                    m = dve.tensor_scalar(dst[:, t, :], r[:, t, :], mv[:, t, 0:1], rstd[:, t:t + 1],
                                          ALU.subtract, ALU.mult)
                m.then_inc(chain, 1)

            def norm1(i, n, at):
                dve.wait_ge(wo_done, i + 1)
                dve.wait_ge(xt_in, 16 * (i + 1))
                dve.tensor_tensor(r1[:, :, :], py[:, :, :], xt[:, :, :], ALU.add).then_inc(chain, 1)
                norm(r1, x1n, n, at + 1)

            def tokens_lo(n):
                dve.wait_ge(tr_hi, n + 1)
                dve.tensor_tensor(x1l[:, :], py[:, :, :].rearrange("p t d -> p (t d)"), x1h[:, :].bitcast(F32),
                                  ALU.subtract).then_inc(tr_lo, 1)

            def split(i, k):
                dve.wait_ge(hi_ok, 3 * KC * i + k + 1)
                dve.tensor_tensor(al[:, k // KC, k % KC, :], act_f[:, k % 4, :],
                                  ah[:, k // KC, k % KC, :].bitcast(F32), ALU.subtract).then_inc(lo_ok, 1)

            def body(i, last):
                for m in range(KC):
                    dve.wait_ge(u_done, UN * i + 2 * m + 2)
                    dve.wait_ge(gate_ok, KC * i + m + 1)
                    dve.scalar_tensor_tensor(act_f[:, m % 4, :], pu[:, (2 * m + 1) % 4, :], sc[:, 1, m:m + 1],
                                             gate[:, m % 2, :], ALU.mult, ALU.mult).then_inc(prod_ok, 1)
                    if m:
                        split(i, m - 1)
                split(i, KC - 1)
                at = LINKS * i + LN1
                if not last:
                    dve.wait_ge(x1_ok, i + 1)
                    norm1(i + 1, 2 * i + 1, at)
                    at = at + LN1
                for k in range(KC, 3 * KC):
                    split(i, k)
                    if k == 2 * KC - 1 and not last:
                        tokens_lo(i + 1)
                dve.wait_ge(z_done, i + 1)
                dve.tensor_tensor(r2[:, :, :], pz[:, :, :], s3b[:, :].unsqueeze(1).to_broadcast([P, TILES, P]),
                                  ALU.mult).then_inc(chain, 1)
                dve.wait_ge(chain, at + 1)
                dve.tensor_tensor(r2[:, :, :], r2[:, :, :], x1[:, :, :], ALU.add).then_inc(chain, 1)
                dve.wait_ge(y_out, 16 * i)
                norm(r2, y2, 2 * i + (1 if last else 2), at + 2)

            norm1(0, 0, 0)
            tokens_lo(0)
            with dve.Fori(0, CHUNKS - 1) as i:
                body(i, False)
            body(CHUNKS - 1, True)


def state_space(nc, y_d, w_proj, conv, w_x, w_dt, a_log, w_out, sel, ident, z_d):
    NB = 2
    NS = 16
    STEPS = NB * NS
    NT = CTX // P
    HALVES = CTX // BANK
    KW = 4
    CB, CD, CT = KW, KW + 1, KW + 2
    PE_PRE = 16
    ACT_PRE = 26
    DVE_PRE = 22
    LINKS = 9

    with ExitStack() as ctx:
        def sb(name, shape, dt):
            return ctx.enter_context(nc.sbuf_tensor(name, shape, dt))

        def sem(name):
            return ctx.enter_context(nc.semaphore(name))

        xt = sb("m_xt", [P, NT, P], F32)
        xh = sb("m_xh", [P, CTX], F32R)
        xl = sb("m_xl", [P, CTX], F32R)
        raw = sb("m_raw", [P, 2 * NS * P], F32)
        wph = sb("m_wph", [P, 4 * P], F32R)
        wpl = sb("m_wpl", [P, 4 * P], F32R)
        cv = sb("m_cv", [P, NB, KW + 3], F32)
        wx = sb("m_wx", [P, NB, DK], F32)
        wdh = sb("m_wdh", [P, NB * P], F32R)
        wdl = sb("m_wdl", [P, NB * P], F32R)
        av = sb("m_av", [P, NB * NS], F32)
        wo_s = sb("m_wo", [P, NB, P], F32)
        sl = sb("m_sl", [P, 2 * NS, P], F32R)
        idf = sb("m_idf", [P, P], F32)
        xin = sb("m_xin", [P, NB, KW - 1 + CTX], F32)
        acc = sb("m_acc", [P, NB, CTX], F32)
        xc = sb("m_xc", [P, NB, CTX], F32)
        sz = sb("m_sz", [P, NB, CTX], F32)
        xs = sb("m_xs", [P, CTX], F32R)
        dt = sb("m_dt", [P, NB, CTX], F32)
        dtx = sb("m_dtx", [P, NB, CTX], F32)
        ex = sb("m_ex", [P, NB, CTX], F32)
        rl = sb("m_rl", [P, NB, CTX], F32)
        a = sb("m_a", [P, 2, CTX], F32)
        cs = sb("m_cs", [P, 2, CTX], F32)
        hs = sb("m_hs", [P, 2, CTX], F32)
        hc = sb("m_hc", [P, 2, CTX], F32)
        yz = sb("m_yz", [P, NB, CTX], F32)
        r = sb("m_r", [P, NT, P], F32)
        y3 = sb("m_y3", [P, NT, P], F32)
        st = sb("m_st", [P, NT, 6], F32)
        mv = sb("m_mv", [P, NT, 2], F32)
        ve = sb("m_ve", [P, NT], F32)
        rstd = sb("m_rstd", [P, NT], F32)
        mhalf = sb("m_mhalf", [P, NT], F32)

        ps = ctx.enter_context(nc.psum_tensor("m_ps", [P, 8 * BANK], F32))
        pb, pc, px, py = (ps[:, k * CTX:(k + 1) * CTX] for k in range(4))

        def bank(k):
            return ps[:, (k % 8) * BANK:(k % 8 + 1) * BANK]

        held = sem("m_held")
        c_in = sem("m_c_in")
        raw_in = sem("m_raw_in")
        raw_hi = sem("m_raw_hi")
        raw_lo = sem("m_raw_lo")
        a_exp = sem("m_a_exp")
        set_ok = sem("m_set_ok")
        mh_ok = sem("m_mh_ok")
        xt_in = sem("m_xt_in")
        pe_pre = sem("m_pe_pre")
        act_pre = sem("m_act_pre")
        dve_pre = sem("m_dve_pre")
        bb_done = sem("m_bb_done")
        cc_done = sem("m_cc_done")
        a_done = sem("m_a_done")
        c_copied = sem("m_c_copied")
        bx_done = sem("m_bx_done")
        scan_done = sem("m_scan_done")
        hc_done = sem("m_hc_done")
        y_acc = sem("m_y_acc")
        chain = sem("m_chain")
        o_done = sem("m_o_done")
        pow_done = sem("m_pow_done")
        z_out = sem("m_z_out")

        block = ctx.enter_context(nc.Block())

        @block.sync
        def _(sp):
            def load(b):
                for half in range(HALVES):
                    sp.dma_start(xt[:, half * TILES:(half + 1) * TILES, :], y_d[HALVES * b + half]).then_inc(xt_in, 16)

            def store(b):
                sp.wait_ge(chain, LINKS * (b + 1))
                for half in range(HALVES):
                    sp.dma_start(z_d[HALVES * b + half], y3[:, half * TILES:(half + 1) * TILES, :]).then_inc(z_out, 16)

            load(0)
            for k, (src, n) in enumerate(((w_proj, 4 * P), (w_dt, NB * P), (sel, 2 * NS * P))):
                if k:
                    sp.wait_ge(raw_lo, k)
                sp.dma_start(raw[:, 0:n], src).then_inc(raw_in, 16)
                if k == 0:
                    sp.dma_start(cv[:, :, :], conv).then_inc(c_in, 16)
                    sp.dma_start(wx[:, :, :], w_x).then_inc(c_in, 16)
                    sp.dma_start(av[:, :], a_log).then_inc(c_in, 16)
                    sp.dma_start(wo_s[:, :, :], w_out).then_inc(c_in, 16)
                    sp.dma_start(idf[:, :], ident).then_inc(c_in, 16)
            with sp.Fori(0, BATCH - 1) as b:
                sp.wait_ge(chain, LINKS * b + 5)
                load(b + 1)
                store(b)
            store(BATCH - 1)
            sp.wait_ge(z_out, 16 * HALVES * BATCH)

        @block.gpsimd
        def _(pool):
            pool.memset(mhalf[:, :], -0.5).then_inc(mh_ok, 1)
            pool.wait_ge(mh_ok, 1)
            with pool.Fori(0, BATCH) as b:
                for k in range(STEPS):
                    pool.wait_ge(scan_done, STEPS * b + k + 1)
                    pool.wait_ge(c_copied, STEPS * b + k + 1)
                    if k >= 2:
                        pool.wait_ge(y_acc, STEPS * b + k - 1)
                    pool.tensor_tensor(hc[:, k % 2, :], hs[:, k % 2, :], cs[:, k % 2, :],
                                       ALU.mult).then_inc(hc_done, 1)
                pool.wait_ge(chain, LINKS * b + 8)
                pool.tensor_tensor(rstd[:, :], ve[:, :], mhalf[:, :], ALU.pow).then_inc(pow_done, 1)

        @block.scalar
        def _(act):
            for k, (dst, n) in enumerate(((wph[:, :], 4 * P), (wdh[:, :], NB * P),
                                          (sl[:, :, :].rearrange("p a b -> p (a b)"), 2 * NS * P))):
                act.wait_ge(raw_in, 16 * (k + 1))
                act.activation(dst, raw[:, 0:n], ACT.Copy).then_inc(raw_hi, 1)
            act.wait_ge(c_in, 80)
            act.activation(av[:, :], av[:, :], ACT.Exp).then_inc(a_exp, 1)
            with act.Fori(0, BATCH) as b:
                P0, A0, D0, S0 = PE_PRE * b, ACT_PRE * b, DVE_PRE * b, STEPS * b
                for half in range(HALVES):
                    cols = slice(half * BANK, (half + 1) * BANK)
                    act.wait_ge(pe_pre, P0 + half + 1)
                    act.activation(xh[:, cols], bank(half), ACT.Copy).then_inc(act_pre, 1)
                for u in range(4):
                    act.wait_ge(pe_pre, P0 + 3 + u)
                    at = KW - 1 + (u % 2) * BANK
                    act.activation(xin[:, u // 2, at:at + BANK], bank(2 + u), ACT.Copy).then_inc(act_pre, 1)
                for u in range(4):
                    act.wait_ge(pe_pre, P0 + 7 + u)
                    at = (u % 2) * BANK
                    act.activation(sz[:, u // 2, at:at + BANK], bank(6 + u), ACT.Silu).then_inc(act_pre, 1)
                for c in range(NB):
                    act.wait_ge(dve_pre, D0 + 2 + KW * (c + 1))
                    act.activation(xc[:, c, :], acc[:, c, :], ACT.Silu).then_inc(act_pre, 1)
                for half in range(HALVES):
                    cols = slice(half * BANK, (half + 1) * BANK)
                    act.wait_ge(pe_pre, P0 + 11 + half)
                    act.activation(xs[0:DK, cols], bank(2 + half)[0:DK, :], ACT.Copy).then_inc(act_pre, 1)
                for u in range(4):
                    c, cols = u // 2, slice((u % 2) * BANK, (u % 2 + 1) * BANK)
                    act.wait_ge(pe_pre, P0 + 13 + u)
                    act.activation(ex[:, c, cols], bank(4 + u), ACT.Abs, bias=cv[:, c, CT:CT + 1]).then_inc(act_pre, 1)
                    act.activation(rl[:, c, cols], bank(4 + u), ACT.Relu, bias=cv[:, c, CT:CT + 1]).then_inc(act_pre, 1)
                for c in range(NB):
                    act.wait_ge(act_pre, A0 + 22 + 2 * c)
                    act.activation(ex[:, c, :], ex[:, c, :], ACT.Exp, scale=-1.0).then_inc(act_pre, 1)
                    act.wait_ge(act_pre, A0 + 23 + 2 * c)
                    act.activation(dt[:, c, :], ex[:, c, :], ACT.Ln, bias=1.0).then_inc(act_pre, 1)
                for k in range(STEPS):
                    c, n = k // NS, k % NS
                    if n == 0:
                        act.wait_ge(dve_pre, D0 + 12 + 5 * (c + 1))
                        if k == 0:
                            act.wait_ge(set_ok, 3)
                    if k >= 2:
                        act.wait_ge(scan_done, S0 + k - 1)
                    act.activation(a[:, k % 2, :], dt[:, c, :], ACT.Exp, scale=av[:, k:k + 1]).then_inc(a_done, 1)
                    act.wait_ge(cc_done, S0 + k + 1)
                    if k >= 2:
                        act.wait_ge(hc_done, S0 + k - 1)
                    act.activation(cs[:, k % 2, :], pc, ACT.Copy).then_inc(c_copied, 1)

        @block.tensor
        def _(pe):
            pe.wait_ge(c_in, 80)
            pe.wait_ge(raw_lo, 2)
            pe.wait_ge(raw_hi, 3)
            with pe.Fori(0, BATCH) as b:
                P0, A0, D0, S0 = PE_PRE * b, ACT_PRE * b, DVE_PRE * b, STEPS * b
                pe.wait_ge(xt_in, 16 * HALVES * (b + 1))
                pe.wait_ge(chain, LINKS * b)
                for t in range(NT):
                    m = pe.transpose(ps[:, t * P:(t + 1) * P], xt[:, t, :], idf[:, :])
                    if t % TILES == TILES - 1:
                        m.then_inc(pe_pre, 1)
                for u in range(8):
                    cols = slice((u // 2) * P, (u // 2 + 1) * P)
                    at = slice((u % 2) * BANK, (u % 2 + 1) * BANK)
                    pe.wait_ge(dve_pre, D0 + u % 2 + 1)
                    if u >= 6:
                        pe.wait_ge(dve_pre, D0 + 2)
                    pe.matmul(bank(2 + u), wph[:, cols], xh[:, at], start=True, stop=False)
                    pe.matmul(bank(2 + u), wph[:, cols], xl[:, at], start=False, stop=False)
                    pe.matmul(bank(2 + u), wpl[:, cols], xh[:, at], start=False, stop=True).then_inc(pe_pre, 1)
                pe.wait_ge(act_pre, A0 + 12)
                for half in range(HALVES):
                    cols = slice(half * BANK, (half + 1) * BANK)
                    for c in range(NB):
                        m = pe.matmul(bank(2 + half)[0:DK, :], wx[:, c, :], xc[:, c, cols], start=(c == 0), stop=(c == NB - 1))
                    m.then_inc(pe_pre, 1)
                for u in range(4):
                    c, half = u // 2, u % 2
                    cols = slice(half * BANK, (half + 1) * BANK)
                    pe.wait_ge(dve_pre, D0 + 11 + half)
                    pe.matmul(bank(4 + u), wdh[:, c * P:(c + 1) * P], xs[:, cols], start=True, stop=False)
                    pe.matmul(bank(4 + u), wdl[:, c * P:(c + 1) * P], xs[:, cols], start=False, stop=True).then_inc(pe_pre, 1)

                def broadcast(k):
                    n = k % NS
                    if k >= 1:
                        pe.wait_ge(bx_done, S0 + k)
                    for half in range(HALVES):
                        cols = slice(half * BANK, (half + 1) * BANK)
                        m = pe.matmul(pb[:, cols], sl[:, n, :], xs[:, cols], start=True, stop=True)
                    m.then_inc(bb_done, 1)
                    if k >= 1:
                        pe.wait_ge(c_copied, S0 + k)
                    for half in range(HALVES):
                        cols = slice(half * BANK, (half + 1) * BANK)
                        m = pe.matmul(pc[:, cols], sl[:, NS + n, :], xs[:, cols], start=True, stop=True)
                    m.then_inc(cc_done, 1)

                def add_up(k):
                    c, n = k // NS, k % NS
                    pe.wait_ge(hc_done, S0 + k + 1)
                    if k == NS:
                        pe.wait_ge(chain, LINKS * b + 1)
                    if k == 0:
                        pe.wait_ge(act_pre, A0 + 22)
                    for half in range(HALVES):
                        cols = slice(half * BANK, (half + 1) * BANK)
                        m = pe.matmul(py[:, cols], idf[:, :], hc[:, k % 2, cols], start=(n == 0), stop=(n == NS - 1))
                    m.then_inc(y_acc, 1)

                broadcast(0)
                for k in range(STEPS):
                    if k + 1 < STEPS:
                        broadcast(k + 1)
                    if k >= 1:
                        add_up(k - 1)
                add_up(STEPS - 1)
                pe.wait_ge(chain, LINKS * b + 4)
                for t in range(NT):
                    cols = slice(t * P, (t + 1) * P)
                    for c in range(NB):
                        m = pe.matmul(pb[:, cols], yz[:, c, cols], wo_s[:, c, :], start=(c == 0), stop=(c == NB - 1))
                m.then_inc(o_done, 1)

        @block.vector
        def _(dve):
            for k, (lo, hi, n) in enumerate(((wpl[:, :], wph[:, :], 4 * P), (wdl[:, :], wdh[:, :], NB * P))):
                dve.wait_ge(raw_hi, k + 1)
                dve.tensor_tensor(lo, raw[:, 0:n], hi.bitcast(F32), ALU.subtract).then_inc(raw_lo, 1)
            dve.memset(xin[:, 0, 0:KW - 1], 0.0).then_inc(set_ok, 1)
            dve.memset(xin[:, 1, 0:KW - 1], 0.0).then_inc(set_ok, 1)
            dve.wait_ge(a_exp, 1)
            dve.tensor_scalar(av[:, :], av[:, :], -1.0, None, ALU.mult).then_inc(set_ok, 1)
            with dve.Fori(0, BATCH) as b:
                P0, A0, D0, S0, L0 = PE_PRE * b, ACT_PRE * b, DVE_PRE * b, STEPS * b, LINKS * b
                for half in range(HALVES):
                    cols = slice(half * BANK, (half + 1) * BANK)
                    dve.wait_ge(act_pre, A0 + half + 1)
                    dve.tensor_tensor(xl[:, cols], bank(half), xh[:, cols].bitcast(F32), ALU.subtract).then_inc(dve_pre, 1)
                for c in range(NB):
                    dve.wait_ge(act_pre, A0 + 4 + 2 * c)
                    dve.tensor_scalar(acc[:, c, :], xin[:, c, 0:CTX], cv[:, c, 0:1], cv[:, c, CB:CB + 1], ALU.mult,
                                      ALU.add).then_inc(dve_pre, 1)
                    for k in range(1, KW):
                        dve.wait_ge(dve_pre, D0 + 2 + KW * c + k)
                        dve.scalar_tensor_tensor(acc[:, c, :], xin[:, c, k:k + CTX], cv[:, c, k:k + 1], acc[:, c, :],
                                                 ALU.mult, ALU.add).then_inc(dve_pre, 1)
                for half in range(HALVES):
                    cols = slice(half * BANK, (half + 1) * BANK)
                    dve.wait_ge(act_pre, A0 + 13 + half)
                    dve.tensor_tensor(xs[DK:P, cols], bank(2 + half)[0:DK, :], xs[0:DK, cols].bitcast(F32),
                                      ALU.subtract).then_inc(dve_pre, 1)
                for c in range(NB):
                    at = D0 + 12 + 5 * c
                    dve.wait_ge(act_pre, A0 + 24 + 2 * c)
                    dve.tensor_scalar(dtx[:, c, :], ex[:, c, :], 1.0, None, ALU.add).then_inc(dve_pre, 1)
                    dve.wait_ge(dve_pre, at + 1)
                    dve.scalar_tensor_tensor(dtx[:, c, :], dtx[:, c, :], -1.0, ex[:, c, :], ALU.add,
                                             ALU.subtract).then_inc(dve_pre, 1)
                    dve.wait_ge(dve_pre, at + 2)
                    dve.tensor_tensor(dt[:, c, :], dt[:, c, :], dtx[:, c, :], ALU.subtract).then_inc(dve_pre, 1)
                    dve.wait_ge(dve_pre, at + 3)
                    dve.tensor_tensor(dt[:, c, :], dt[:, c, :], rl[:, c, :], ALU.add).then_inc(dve_pre, 1)
                    dve.wait_ge(dve_pre, at + 4)
                    dve.tensor_tensor(dtx[:, c, :], dt[:, c, :], xc[:, c, :], ALU.mult).then_inc(dve_pre, 1)
                dve.wait_ge(dve_pre, D0 + DVE_PRE)

                def gated(c):
                    dve.wait_ge(y_acc, S0 + NS * (c + 1))
                    dve.scalar_tensor_tensor(yz[:, c, :], xc[:, c, :], cv[:, c, CD:CD + 1], py, ALU.mult,
                                             ALU.add).then_inc(chain, 1)
                    dve.wait_ge(chain, L0 + 2 * c + 1)
                    dve.tensor_tensor(yz[:, c, :], yz[:, c, :], sz[:, c, :], ALU.mult).then_inc(chain, 1)

                for k in range(STEPS):
                    c = k // NS
                    dve.wait_ge(bb_done, S0 + k + 1)
                    dve.wait_ge(scan_done, S0 + k)
                    dve.tensor_tensor(px, pb, dtx[:, c, :], ALU.mult).then_inc(bx_done, 1)
                    if k == NS + 1:
                        gated(0)
                    dve.wait_ge(bx_done, S0 + k + 1)
                    dve.wait_ge(a_done, S0 + k + 1)
                    if k >= 2:
                        dve.wait_ge(hc_done, S0 + k - 1)
                    dve.tensor_tensor_scan(hs[:, k % 2, :], a[:, k % 2, :], px, 0.0, ALU.mult,
                                           ALU.add).then_inc(scan_done, 1)
                gated(1)
                dve.wait_ge(o_done, b + 1)
                dve.tensor_tensor(r[:, :, :], pb.rearrange("p (t d) -> p t d", t=NT), xt[:, :, :], ALU.add).then_inc(chain, 1)
                dve.wait_ge(chain, L0 + 5)
                for t in range(NT):
                    m = dve.bn_stats(st[:, t, :], r[:, t, :])
                m.then_inc(chain, 1)
                dve.wait_ge(chain, L0 + 6)
                dve.sem_inc(held, 1)
                for t in range(NT):
                    m = dve.bn_aggr(mv[:, t, :], st[:, t, :])
                m.then_inc(chain, 1)
                dve.wait_ge(chain, L0 + 7)
                dve.tensor_scalar(ve[:, :], mv[:, :, 1], EPS, None, ALU.add).then_inc(chain, 1)
                dve.wait_ge(pow_done, b + 1)
                dve.wait_ge(z_out, 16 * HALVES * b)
                for t in range(NT):
                    m = dve.tensor_scalar(y3[:, t, :], r[:, t, :], mv[:, t, 0:1], rstd[:, t:t + 1], ALU.subtract, ALU.mult)
                m.then_inc(chain, 1)


def ternary_ffn(nc, z_d, w1, w2, b1, b2, ident, out):
    KC = HID // P
    LINKS = 5

    with ExitStack() as ctx:
        def sb(name, shape, dt):
            return ctx.enter_context(nc.sbuf_tensor(name, shape, dt))

        def sem(name):
            return ctx.enter_context(nc.semaphore(name))

        wr = sb("t_wr", [P, 2, HID], F32)
        above = sb("t_above", [P, 2, HID], F32)
        below = sb("t_below", [P, 2, HID], F32)
        wq = sb("t_wq", [P, 2, HID], F32R)
        asum = sb("t_asum", [P, 2], F32)
        th = sb("t_th", [P, 2, 2], F32)
        ones = sb("t_ones", [P, P], F32)
        idf = sb("t_idf", [P, P], F32)
        bv1 = sb("t_b1", [P, KC], F32)
        bv2 = sb("t_b2", [P, P], F32)
        mhalf = sb("t_mhalf", [P, TILES], F32)
        xt = sb("t_xt", [P, 2, TILES, P], F32)
        xb = sb("t_xb", [P, 2, TILES, P], F32)
        xh = sb("t_xh", [P, 2, BANK], F32R)
        xl = sb("t_xl", [P, 2, BANK], F32R)
        hf = sb("t_hf", [P, KC, BANK], F32)
        hh = sb("t_hh", [P, KC, BANK], F32R)
        hl = sb("t_hl", [P, KC, BANK], F32R)
        r = sb("t_r", [P, TILES, P], F32)
        y = sb("t_y", [P, 2, TILES, P], F32)
        st = sb("t_st", [P, TILES, 6], F32)
        mv = sb("t_mv", [P, TILES, 2], F32)
        ve = sb("t_ve", [P, TILES], F32)
        rstd = sb("t_rstd", [P, TILES], F32)
        pu = ctx.enter_context(nc.psum_tensor("t_pu", [P, KC, BANK], F32))
        pt = ctx.enter_context(nc.psum_tensor("t_pt", [P, 2, TILES, P], F32))
        pz = ctx.enter_context(nc.psum_tensor("t_pz", [P, 2, TILES, P], F32))

        held = sem("t_held")
        c_in = sem("t_c_in")
        set_ok = sem("t_set_ok")
        q_sum = sem("t_q_sum")
        q_dve = sem("t_q_dve")
        xt_in = [sem(f"t_xt_in{i}") for i in range(2)]
        tr_done = sem("t_tr_done")
        tr_hi = sem("t_tr_hi")
        tr_lo = sem("t_tr_lo")
        xb_ok = sem("t_xb_ok")
        u_done = sem("t_u_done")
        relu_ok = sem("t_relu_ok")
        hi_ok = sem("t_hi_ok")
        lo_ok = sem("t_lo_ok")
        z_done = sem("t_z_done")
        chain = sem("t_chain")
        pow_done = sem("t_pow_done")
        y_out = [sem(f"t_y_out{i}") for i in range(2)]

        ROUNDS = CHUNKS // 2
        block = ctx.enter_context(nc.Block())

        @block.sync
        def _(sp):
            for i in range(2):
                sp.dma_start(xt[:, i], z_d[i]).then_inc(xt_in[i], 16)
            for dst, src in ((wr[:, 0, :], w1), (wr[:, 1, :], w2), (idf[:, :], ident), (bv1[:, :], b1), (bv2[:, :], b2)):
                sp.dma_start(dst, src).then_inc(c_in, 16)
            with sp.Fori(0, ROUNDS) as g:
                for s in range(2):
                    sp.wait_ge(chain, LINKS * (2 * g + s + 1))
                    sp.dma_start(out[2 * g + s], y[:, s]).then_inc(y_out[s], 16)
                    sp.wait_ge(xb_ok, 2 * g + s + 1)
                    sp.dma_start(xt[:, s], z_d[(2 * g + s + 2) % CHUNKS]).then_inc(xt_in[s], 16)
            for s in range(2):
                sp.wait_ge(y_out[s], 16 * ROUNDS)
                sp.wait_ge(xt_in[s], 16 * (ROUNDS + 1))

        @block.gpsimd
        def _(pool):
            pool.memset(ones[:, :], 1.0).then_inc(set_ok, 1)
            pool.memset(mhalf[:, :], -0.5).then_inc(set_ok, 1)
            pool.wait_ge(set_ok, 2)
            pool.wait_ge(c_in, 80)
            with pool.Fori(0, ROUNDS) as g:
                for s in range(2):
                    i = 2 * g + s
                    pool.wait_ge(xt_in[s], 16 * (g + 1))
                    pool.wait_ge(tr_done, i + 1)
                    pool.tensor_tensor(xb[:, s], xt[:, s], bv2[:, :].unsqueeze(1).to_broadcast([P, TILES, P]),
                                       ALU.add).then_inc(xb_ok, 1)
                    for k in range(KC):
                        pool.wait_ge(relu_ok, KC * i + k + 1)
                        pool.sem_inc(held, 1)
                        pool.tensor_scalar(hh[:, k, :], hf[:, k, :], 1.0, 1.0, ALU.mult, ALU.mult).then_inc(hi_ok, 1)
                    pool.wait_ge(chain, LINKS * i + 4)
                    pool.tensor_tensor(rstd[:, :], ve[:, :], mhalf[:, :], ALU.pow).then_inc(pow_done, 1)

        @block.scalar
        def _(act):
            act.wait_ge(c_in, 80)
            with act.Fori(0, ROUNDS) as g:
                for s in range(2):
                    i = 2 * g + s
                    act.wait_ge(tr_done, i + 1)
                    act.activation(xh[:, s, :], pt[:, s].rearrange("p t d -> p (t d)"), ACT.Copy).then_inc(tr_hi, 1)
                    for k in range(KC):
                        act.wait_ge(u_done, KC * i + k + 1)
                        act.wait_ge(lo_ok, KC * i)
                        act.activation(hf[:, k, :], pu[:, k, :], ACT.Relu, bias=bv1[:, k:k + 1]).then_inc(relu_ok, 1)

        @block.tensor
        def _(pe):
            pe.wait_ge(c_in, 80)
            pe.wait_ge(set_ok, 2)
            pe.wait_ge(q_dve, 2)
            pe.matmul(pz[:, 0, 0, 0:2], ones[:, :], asum[:, :], start=True, stop=True).then_inc(q_sum, 1)

            def transposes(i, s, g):
                pe.wait_ge(xt_in[s], 16 * (g + 1))
                for t in range(TILES):
                    m = pe.transpose(pt[:, s, t, :], xt[:, s, t, :], idf[:, :])
                m.then_inc(tr_done, 1)

            pe.wait_ge(q_dve, 9)
            with pe.Fori(0, ROUNDS) as g:
                for s in range(2):
                    transposes(2 * g + s, s, g)
                for s in range(2):
                    i = 2 * g + s
                    pe.wait_ge(tr_lo, i + 1)
                    for k in range(KC):
                        pe.wait_ge(relu_ok, KC * i)
                        cols = slice(k * P, (k + 1) * P)
                        pe.matmul(pu[:, k, :], wq[:, 0, cols], xh[:, s, :], start=True, stop=False)
                        pe.matmul(pu[:, k, :], wq[:, 0, cols], xl[:, s, :], start=False, stop=True).then_inc(u_done, 1)
                    pe.wait_ge(lo_ok, KC * (i + 1))
                    pe.wait_ge(chain, LINKS * i)
                    for t in range(TILES):
                        cols = slice(t * P, (t + 1) * P)
                        for k in range(KC):
                            pe.matmul(pz[:, s, t, :], hh[:, k, cols], wq[:, 1, k * P:(k + 1) * P], start=(k == 0), stop=False)
                            m = pe.matmul(pz[:, s, t, :], hl[:, k, cols], wq[:, 1, k * P:(k + 1) * P], start=False, stop=(k == KC - 1))
                    m.then_inc(z_done, 1)

        @block.vector
        def _(dve):
            dve.wait_ge(c_in, 80)
            for j in range(2):
                dve.tensor_reduce(asum[:, j:j + 1], wr[:, j, :], AX.X, ALU.add, apply_absolute_value=True).then_inc(q_dve, 1)
            dve.wait_ge(q_sum, 1)
            dve.tensor_scalar(th[:, 0, :], pz[:, 0, 0, 0:2], 1.0 / (D * HID), EPS, ALU.mult, ALU.add).then_inc(q_dve, 1)
            dve.wait_ge(q_dve, 3)
            dve.tensor_scalar(th[:, 1, :], th[:, 0, :], -0.5, None, ALU.mult).then_inc(q_dve, 1)
            dve.wait_ge(q_dve, 4)
            dve.tensor_scalar(th[:, 0, :], th[:, 1, :], -1.0, None, ALU.mult).then_inc(q_dve, 1)
            dve.wait_ge(q_dve, 5)
            for j in range(2):
                dve.tensor_scalar(above[:, j, :], wr[:, j, :], th[:, 0, j:j + 1], None, ALU.is_gt)
                m = dve.tensor_scalar(below[:, j, :], wr[:, j, :], th[:, 1, j:j + 1], None, ALU.is_lt)
                m.then_inc(q_dve, 1)
            dve.wait_ge(q_dve, 7)
            for j in range(2):
                dve.tensor_tensor(wq[:, j, :], above[:, j, :], below[:, j, :], ALU.subtract).then_inc(q_dve, 1)
            with dve.Fori(0, ROUNDS) as g:
                for s in range(2):
                    i = 2 * g + s
                    at = LINKS * i
                    dve.wait_ge(tr_hi, i + 1)
                    dve.tensor_tensor(xl[:, s, :], pt[:, s].rearrange("p t d -> p (t d)"), xh[:, s, :].bitcast(F32),
                                      ALU.subtract).then_inc(tr_lo, 1)
                    for k in range(KC):
                        dve.wait_ge(hi_ok, KC * i + k + 1)
                        dve.tensor_tensor(hl[:, k, :], hf[:, k, :], hh[:, k, :].bitcast(F32), ALU.subtract).then_inc(lo_ok, 1)
                    dve.wait_ge(z_done, i + 1)
                    dve.wait_ge(xb_ok, i + 1)
                    dve.tensor_tensor(r[:, :, :], pz[:, s], xb[:, s], ALU.add).then_inc(chain, 1)
                    dve.wait_ge(chain, at + 1)
                    for t in range(TILES):
                        m = dve.bn_stats(st[:, t, :], r[:, t, :])
                    m.then_inc(chain, 1)
                    dve.wait_ge(chain, at + 2)
                    dve.sem_inc(held, 1)
                    for t in range(TILES):
                        m = dve.bn_aggr(mv[:, t, :], st[:, t, :])
                    m.then_inc(chain, 1)
                    dve.wait_ge(chain, at + 3)
                    dve.tensor_scalar(ve[:, :], mv[:, :, 1], EPS, None, ALU.add).then_inc(chain, 1)
                    dve.wait_ge(pow_done, i + 1)
                    dve.wait_ge(y_out[s], 16 * g)
                    for t in range(TILES):
                        m = dve.tensor_scalar(y[:, s, t, :], r[:, t, :], mv[:, t, 0:1], rstd[:, t:t + 1], ALU.subtract, ALU.mult)
                    m.then_inc(chain, 1)


def program(nc, x_tok, xT, wpk, mask, wo, w_in, w_hid, w_out, scales, s3, w_proj, conv, w_x, w_dt, a_log,
            w_mix, sel, w1, w2, b1, b2, ident, out):
    ot_d = nc.dram_tensor("attended", [CHUNKS, P, PAIRS, BANK], F32, kind="Internal").ap()
    y_d = nc.dram_tensor("after_gated", [CHUNKS, P, TILES, P], F32, kind="Internal").ap()
    z_d = nc.dram_tensor("after_mixer", [CHUNKS, P, TILES, P], F32, kind="Internal").ap()
    attention(nc, xT, wpk, ident, mask, ot_d)
    gated_ffn(nc, ot_d, x_tok, wo, w_in, w_hid, w_out, scales, s3, ident, y_d)
    state_space(nc, y_d, w_proj, conv, w_x, w_dt, a_log, w_mix, sel, ident, z_d)
    ternary_ffn(nc, z_d, w1, w2, b1, b2, ident, out)


def kernel(**inputs):
    import numpy as np
    import concourse.bacc as bacc
    from concourse.bass_utils import run_bass_kernel_spmd

    t = {k: np.asarray(v) for k, v in inputs.items()}

    def tiled(m):
        return np.ascontiguousarray(m.reshape(-1, P, m.shape[1]).transpose(1, 0, 2))

    def spread(vec):
        return np.ascontiguousarray(np.broadcast_to(vec, (P, vec.shape[0])))

    x = t["L0_attn_x"].reshape(TOK, D)
    wpk = np.empty((PAIRS, P, WCOLS), np.float32)
    for pair in range(PAIRS):
        both = slice(2 * DK * pair, 2 * DK * (pair + 1))
        for h in range(2):
            cols = slice(DK * (2 * pair + h), DK * (2 * pair + h + 1))
            for k in range(2):
                at = slice(P * h + DK * k, P * h + DK * (k + 1))
                rows = slice(DK * k, DK * (k + 1))
                wpk[pair, :, WQ:WQ + 256][:, at] = t["L0_attn_Wq"][:, cols]
                wpk[pair, :, WK:WK + 256][:, at] = t["L0_attn_Wk"][:, cols]
                wpk[pair, rows, WBQ + h] = t["L0_attn_bq"][cols]
                wpk[pair, rows, WBK + h] = t["L0_attn_bk"][cols]
        wpk[pair, :, WV:WV + P] = t["L0_attn_Wv"][:, both]
        wpk[pair, :, WBV:WBV + P] = t["L0_attn_bv"][both]

    key = np.arange(P)
    mask = np.where(key[None, :] <= key[:, None], 0.0, -1e30).astype(np.float32)
    per_block = lambda vec: vec.reshape(-1, P).T
    conv = np.concatenate([t["L1_attn_conv_w"].reshape(2, P, 4).transpose(1, 0, 2)] +
                          [per_block(t[n])[:, :, None] for n in ("L1_attn_conv_b", "L1_attn_D_param", "L1_attn_dt_proj_b")], 2)
    w_x = np.zeros((P, 2, DK), np.float32)
    w_x[:, :, 0:40] = tiled(t["L1_attn_x_proj_w"].T)
    w_dt = np.zeros((P, 256), np.float32)
    sel = np.zeros((P, 32, P), np.float32)
    for lo in (0, DK):
        w_dt[lo:lo + 8] = t["L1_attn_dt_proj_w"].T
        for n in range(32):
            sel[lo + 8 + n, n] = 1.0

    arrays = {
        "x_tok": x.reshape(CHUNKS, TILES, P, D).transpose(0, 2, 1, 3),
        "xT": x.T,
        "wpk": wpk,
        "mask": mask,
        "wo": tiled(t["L0_attn_Wo"]),
        "w_in": np.stack([t["L0_ffn_w1_w"].T, t["L0_ffn_w2_w"].T]),
        "w_hid": np.stack([tiled(t[n].T).reshape(P, -1) for n in ("L0_ffn_h1_w", "L0_ffn_h2_w")]),
        "w_out": tiled(t["L0_ffn_w3_w"].T).reshape(P, -1),
        "scales": np.stack([per_block(t[f"L0_ffn_{n}_s"]) for n in ("w1", "w2", "h1", "h2")], 1),
        "s3": spread(t["L0_ffn_w3_s"]),
        "w_proj": t["L1_attn_in_proj_w"].T,
        "conv": conv,
        "w_x": w_x,
        "w_dt": w_dt,
        "a_log": tiled(t["L1_attn_A_log"]).reshape(P, -1),
        "w_mix": tiled(t["L1_attn_out_proj_w"].T),
        "sel": sel.reshape(P, -1),
        "w1": t["L1_ffn_W1"].T,
        "w2": tiled(t["L1_ffn_W2"].T).reshape(P, -1),
        "b1": per_block(t["L1_ffn_b1"]),
        "b2": spread(t["L1_ffn_b2"]),
        "ident": np.eye(P, dtype=np.float32),
    }
    arrays = {f"in_{k}": np.ascontiguousarray(v) for k, v in arrays.items()}
    nc = bacc.Bacc("TRN2", target_bir_lowering=False, num_devices=1)
    args = [nc.dram_tensor(k, v.shape, mybir.dt.from_np(v.dtype), kind="ExternalInput").ap() for k, v in arrays.items()]
    out = nc.dram_tensor("tokens_out", [CHUNKS, P, TILES, P], F32, kind="ExternalOutput").ap()
    program(nc, *args, out)
    got = run_bass_kernel_spmd(nc, [arrays], core_ids=[0]).results[0]["tokens_out"]
    return got.reshape(CHUNKS, P, TILES, D).transpose(0, 2, 1, 3).reshape(BATCH, CTX, D)
```

```python
from contextlib import ExitStack

import concourse.bass as bass
from concourse import mybir

ALU = mybir.AluOpType
ACT = mybir.ActivationFunctionType
AX = mybir.AxisListType
F32 = mybir.dt.float32
F32R = mybir.dt.float32r
BF16 = mybir.dt.bfloat16

P = 128
BANK = 512
BATCH, CTX, D = 4, 1024, 128
TOK = BATCH * CTX
HEADS, DK = 16, 64
PAIRS = HEADS // 2
CHUNKS = TOK // BANK
TILES = BANK // P
HID = 512
EPS = 1e-5

WQ, WK, WV = 0, 256, 512
WBQ, WBK, WBV = 640, 642, 644
WCOLS = 772


def attention(nc, xT, wpk, ident, masks, pick, ot_d):
    ITERS = BATCH * PAIRS
    NT = CTX // P
    UNITS = 8
    JOBS = UNITS + 2
    EXPS = 4 + NT
    ADDS = EXPS - 2
    SCORES = EXPS + 2
    MAXES = 8 + 16 + 2
    EARLY = 4
    ESLOTS = 4

    PAIR = """
        score 0 0 0, max 1 4, max 1 5, score 0 0 1, max 1 6, max 1 7
        score 0 1 0, score 0 1 1, max 1 8, max 1 9, unit 0, pv 0 0, max 1 10, max 1 11, sum -1
        score 0 2 0, score 0 2 1, max 1 12, max 1 13, unit 1, pv 0 1, max 1 14, max 1 15, fold
        score 0 3 0, score 0 3 1, unit 2, pv 0 2, turn 1, pv 0 3, drain 0, unit 3, invert -1 0, invert -1 1
        score 1 0 0, score 1 0 1
        score 1 1 0, score 1 1 1, max 0 0, pv 1 0, scale -1, sum 0, unit 4, max 0 1
        score 1 2 0, score 1 2 1, max 0 2, unit 5, max 0 3, pv 1 1
        score 1 3 0, score 1 3 1, max 0 4, unit 6, max 0 5
        score 1 4 0, max 0 6, score 1 4 1
        score 1 5 0, unit 7, pv 1 2, max 0 7, invert 0 0, pv 1 3, pv 1 4, values 0, turn 0, max 1 0, score 1 5 1
        score 1 6 0, score 1 6 1, values 1, pv 1 5, max 1 1, split, max 1 2
        score 1 7 0, max 1 3, score 1 7 1, invert 0 1, pv 1 6, pv 1 7, scale 0, drain 1
    """

    def read(text):
        words = (step.split() for step in text.replace("\n", ",").split(",") if step.strip())
        return [(kind, *map(int, at)) for kind, *at in words]

    def ahead(kind, *at):
        return kind in ("unit", "values", "split") or (kind, *at) == ("turn", 0) or (
            kind == "max" and (at[0] == 0 or at[1] < EARLY))

    def pair_steps(first, last):
        return [s for s in read(PAIR) if not (last and ahead(*s)) and not (first and s[1:2] == (-1,))]

    START = [(kind, *at) for kind, *at in (
        [("unit", n) for n in range(UNITS)] + [("values", n) for n in range(2)] +
        [("max", 0, n) for n in range(8)] + [("turn", 0)] + [("max", 1, n) for n in range(EARLY)])]
    END = read("sum -1, invert -1 0, invert -1 1, scale -1")

    def first_lo(c, j):
        return max(0, j - 4) * P if c else 0

    def exp_no(g, c, j):
        return EXPS * g + 4 * c + j

    def adds_with(g, c, j):
        return ADDS * g + 3 * c + max(j, 1)

    SCORE_ORDER = [(0, 0), (0, 1), "prev", (0, 2), (0, 3), (1, 0), (1, 1), "own"] + [(1, j) for j in range(2, NT)]

    def score_turn(g, what):
        pos = SCORE_ORDER.index(what)
        if isinstance(g, int) and g == ITERS:
            return SCORES * g - 1
        return pos if isinstance(g, int) and g == 0 and pos < 2 else SCORES * g + pos - 1

    def score_slot(g, what):
        pos = SCORE_ORDER.index(what)
        return (pos if isinstance(g, int) and g == 0 and pos < 2 else pos - 1) % 2

    assert SCORES % 2 == 0 and MAXES % 2 == 0 and EXPS % ESLOTS == 0

    def max_pos(kind, c, n=0):
        late = 16 - EARLY
        if kind == "turn":
            return late if c else late + 1 + 8
        if c == 0:
            return late + 1 + n
        return n - EARLY if n >= EARLY else late + 2 + 8 + n

    def max_turn(g, kind, c, n=0):
        return 8 + 1 + EARLY + MAXES * g + max_pos(kind, c, n)

    def turn_slot(c, n=None):
        return max_turn(0, "turn" if n is None else "max", c, n or 0) % 2

    def target(g, kind, c, n=0):
        return g if c and (kind == "turn" or n >= EARLY) else g + 1

    def sum_no(g, c):
        return 2 * g + c

    def unit(n):
        return n // 4, (n // 2) % 2, n % 2 == 1

    with ExitStack() as ctx:
        def sb(name, shape, dt):
            return ctx.enter_context(nc.sbuf_tensor(name, shape, dt))

        def sem(name):
            return ctx.enter_context(nc.semaphore(name))

        xh = sb("a_xh", [P, TOK], F32R)
        xl = sb("a_xl", [P, TOK], F32R)
        xb = sb("a_xb", [P, 2, CTX], F32)
        w = sb("a_w", [P, 2, WCOLS], F32)
        wh = sb("a_wh", [P, 2, 512], F32R)
        wl = sb("a_wl", [P, 2, 512], F32R)
        qa = sb("a_qa", [P, 2, 2, CTX], F32R)
        ka = sb("a_ka", [P, 2, 2, CTX], F32R)
        qb = sb("a_qb", [P, 2, 2, CTX], F32R)
        kb = sb("a_kb", [P, 2, 2, CTX], F32R)
        v = sb("a_v", [P, 2, NT, P], F32)
        e = sb("a_e", [P, ESLOTS, 2, BANK], F32)
        acc = sb("a_acc", [P, 2, 2, BANK], F32)
        rs = sb("a_rs", [P, 2, BANK], F32)
        ou = sb("a_ou", [P, 2, BANK], F32)
        ots = sb("a_ots", [P, 2, BANK], F32)
        part = sb("a_part", [P, 8, 2], F32)
        nmc = sb("a_nmc", [P, 2, P], F32)
        ones = sb("a_ones", [P, DK], F32)
        pk = sb("a_pick", [P, 8], F32)
        col = sb("a_col", [P, 1], F32)
        idf = sb("a_idf", [P, P], F32)
        mkf = sb("a_mkf", [P, 2, P], F32)
        idb = sb("a_idb", [P, P], BF16)
        mkb = sb("a_mkb", [P, 2, P], BF16)

        ps = ctx.enter_context(nc.psum_tensor("a_ps", [P, 2, 2, BANK], F32))
        pm = ctx.enter_context(nc.psum_tensor("a_pm", [P, 2, BANK], F32))
        po = ctx.enter_context(nc.psum_tensor("a_po", [P, BANK], F32))
        pj = ctx.enter_context(nc.psum_tensor("a_pj", [P, BANK], F32))

        held = sem("a_held")
        const_in = sem("a_const_in")
        const_dve = sem("a_const_dve")
        const_pool = sem("a_const_pool")
        xin = [sem(f"a_xin{i}") for i in range(2)]
        x_hi = sem("a_x_hi")
        x_lo = sem("a_x_lo")
        w_in = [sem(f"a_w_in{i}") for i in range(2)]
        xb_in = [sem(f"a_xb_in{i}") for i in range(2)]
        w_scaled = sem("a_w_scaled")
        w_split = sem("a_w_split")
        pj_done = sem("a_pj_done")
        pj_hi = sem("a_pj_hi")
        pj_free = sem("a_pj_free")
        mx_done = sem("a_mx_done")
        mx_free = sem("a_mx_free")
        folded = sem("a_folded")
        s_done = sem("a_s_done")
        s_free = sem("a_s_free")
        add_done = sem("a_add_done")
        pv_done = sem("a_pv_done")
        po_free = sem("a_po_free")
        inverted = sem("a_inverted")
        scaled = sem("a_scaled")
        o_out = [sem(f"a_o_out{i}") for i in range(2)]
        sent = sem("a_sent")

        CONSTS = 9
        block = ctx.enter_context(nc.Block())

        def pairs(engine, steps):
            steps(-1, 1, START)
            steps(0, 0, pair_steps(True, False))
            with engine.Fori(0, (ITERS - 2) // 2) as i:
                for k in (1, 2):
                    steps(2 * i + k, k % 2, pair_steps(False, False))
            steps(ITERS - 1, 1, pair_steps(False, True))
            steps(ITERS, 0, END)

        @block.sync
        def _(sp):
            for dst, src in ((idf[:, :], ident), (mkf[:, :, :], masks), (pk[:, :], pick)):
                sp.dma_start(dst, src).then_inc(const_in, 16)
            for i in range(2):
                sp.dma_start(w[:, i, :], wpk[i]).then_inc(w_in[i], 16)
            for b in range(BATCH):
                if b >= 2:
                    sp.wait_ge(x_lo, b - 1)
                sp.dma_start(xb[:, b % 2, :], xT[:, b * CTX:(b + 1) * CTX]).then_inc(xin[b % 2], 16)
            for i in range(2):
                sp.wait_ge(x_lo, BATCH)
                sp.dma_start(xb[:, i, :], xT[:, 0:CTX]).then_inc(xb_in[i], 16)

            def load(g, slot):
                sp.wait_ge(pj_free, JOBS * (g + 1) + 1)
                at = g + 2
                sp.dma_start(w[:, slot, :], wpk[at % PAIRS]).then_inc(w_in[slot], 16)
                sp.dma_start(xb[:, slot, :], xT[:, bass.ds(((at // PAIRS) % BATCH) * CTX, CTX)]).then_inc(xb_in[slot], 16)

            def send(g, c):
                sp.wait_ge(scaled, sum_no(g, c) + 3)
                sp.dma_start(ot_d[2 * (g // PAIRS) + c, :, g % PAIRS, :], ots[:, c, :]).then_inc(o_out[c], 16)
                sp.wait_ge(o_out[c], 16 * (g + 1))
                sp.sem_inc(sent, 1)

            sp.sem_inc(sent, 2)
            load(0, 0)
            send(0, 0)
            with sp.Fori(0, (ITERS - 2) // 2) as i:
                for k in (1, 2):
                    g = 2 * i + k
                    load(g, k % 2)
                    send(g - 1, 1)
                    send(g, 0)
            send(ITERS - 2, 1)
            send(ITERS - 1, 0)
            send(ITERS - 1, 1)
            for c in range(2):
                sp.wait_ge(w_in[c], 16 * (ITERS // 2 + 1 - c))
                sp.wait_ge(xb_in[c], 16 * (ITERS // 2 + 1 - c))

        @block.gpsimd
        def _(pool):
            def split_weights(g, slot):
                pool.wait_ge(w_in[slot], 8 * (g - slot) + 16)
                pool.sem_inc(held, 1)
                pool.tensor_scalar(w[:, slot, WQ:WQ + 256], w[:, slot, WQ:WQ + 256], 0.125, 1.0, ALU.mult,
                                   ALU.mult).then_inc(w_scaled, 1)
                pool.tensor_scalar(w[:, slot, WBQ:WBQ + 2], w[:, slot, WBQ:WBQ + 2], 0.125, 1.0, ALU.mult,
                                   ALU.mult).then_inc(w_scaled, 1)
                pool.wait_ge(w_scaled, 3 * g + 2)
                pool.sem_inc(held, 1)
                pool.tensor_scalar(wh[:, slot, :], w[:, slot, 0:512], 1.0, 1.0, ALU.mult, ALU.mult).then_inc(w_scaled, 1)
                pool.wait_ge(w_scaled, 3 * g + 3)
                pool.tensor_tensor(wl[:, slot, :], w[:, slot, 0:512], wh[:, slot, :].bitcast(F32),
                                   ALU.subtract).then_inc(w_split, 1)

            def add(g, c, j):
                lo = first_lo(c, j)
                slot = exp_no(0, c, j) % ESLOTS
                pool.wait_ge(s_free, score_turn(g, (c, j)) + 1 + 2)
                if j == 1:
                    if not isinstance(g, int) or g > 0:
                        pool.wait_ge(s_done, (score_turn(g, "prev") if c else score_turn(g - 1, "own")) + 1)
                else:
                    pool.wait_ge(add_done, adds_with(g, c, j) - 1 + ESLOTS)
                before = e[:, (slot - 1) % ESLOTS] if j == 1 else acc[:, c]
                pool.tensor_tensor(acc[:, c, :, lo:BANK], before[:, :, lo:BANK], e[:, slot, :, lo:BANK],
                                   ALU.add).then_inc(add_done, 1)

            def scale(g, c):
                n = sum_no(g, c)
                pool.wait_ge(inverted, 2 * (n + 1))
                pool.wait_ge(po_free, n + 2)
                pool.wait_ge(sent, n + 1)
                pool.tensor_tensor(ots[:, c % 2, :], ou[:, c % 2, :], rs[:, c % 2, :], ALU.mult).then_inc(scaled, 1)

            def steps(g, slot, items):
                for kind, *at in items:
                    if kind == "score" and at[2] == 1 and at[1] > 0:
                        add(g, at[0], at[1])
                    elif kind == "scale":
                        scale(g, at[0])
                    elif kind == "split":
                        split_weights(g + 2, slot)

            pool.sem_inc(add_done, ESLOTS)
            pool.sem_inc(scaled, 2)
            pool.memset(ones[:, :], 1.0).then_inc(const_pool, 1)
            split_weights(0, 0)
            split_weights(1, 1)
            pairs(pool, steps)

        @block.scalar
        def _(act):
            def project_hi(g, slot, n):
                half, h, query = unit(n)
                cols = slice(half * BANK, (half + 1) * BANK)
                at = (WBQ if query else WBK) + h
                act.wait_ge(pj_done, JOBS * g + n + 1)
                if query:
                    act.activation(qb[0:DK, slot, h, cols], pj[0:DK, :], ACT.Identity, bias=w[0:DK, slot, at:at + 1])
                act.activation((qa if query else ka)[:, slot, h, cols], pj[:, :], ACT.Identity,
                               bias=w[:, slot, at:at + 1]).then_inc(pj_hi, 1)

            def exponentials(g, c, j):
                lo = first_lo(c, j)
                n = exp_no(g, c, j)
                slot = exp_no(0, c, j) % ESLOTS
                act.wait_ge(pv_done, n + 1)
                if c == 0:
                    act.wait_ge(add_done, adds_with(g - 1, 1, 4 + j) + ESLOTS)
                elif j < 4:
                    act.wait_ge(add_done, adds_with(g, 0, j) + ESLOTS)
                else:
                    act.wait_ge(add_done, adds_with(g, 1, j - 4) + ESLOTS)
                act.wait_ge(s_done, score_turn(g, (c, j)) + 1)
                s = score_slot(g, (c, j))
                act.activation(e[:, slot, :, lo:BANK], ps[:, s, :, lo:BANK], ACT.Exp).then_inc(s_free, 1)

            def copy_sums(g, c):
                act.wait_ge(scaled, sum_no(g, c) + 1)
                act.wait_ge(s_done, score_turn(g, "prev" if c < 0 else "own") + 1)
                act.activation(rs[:, c % 2, :], ps[:, score_slot(g, "prev" if c < 0 else "own"), 0, :],
                               ACT.Copy).then_inc(s_free, 1)

            def drain(g, c):
                act.wait_ge(scaled, sum_no(g, c) + 1)
                act.wait_ge(pv_done, exp_no(g, c, NT - 1 if c else 3) + 1 + ESLOTS)
                act.activation(ou[:, c, :], po[:, :], ACT.Copy).then_inc(po_free, 1)

            def steps(g, slot, items):
                for kind, *at in items:
                    if kind == "score" and at[2] == 1:
                        exponentials(g, at[0], at[1])
                    elif kind == "unit":
                        project_hi(g + 1, 1 - slot, at[0])
                    elif kind == "sum":
                        copy_sums(g, at[0])
                    elif kind == "drain":
                        drain(g, at[0])

            act.sem_inc(s_free, 2)
            act.sem_inc(po_free, 1)
            for b in range(BATCH):
                act.wait_ge(xin[b % 2], 16 * (b // 2 + 1))
                act.activation(xh[:, b * CTX:(b + 1) * CTX], xb[:, b % 2, :], ACT.Identity).then_inc(x_hi, 1)
            pairs(act, steps)

        @block.tensor
        def _(pe):
            def project(g, slot, n):
                half, h, query = unit(n)
                cols = slice((WQ if query else WK) + P * h, (WQ if query else WK) + P * (h + 1))
                if n == 0:
                    pe.wait_ge(w_split, g + 1)
                pe.wait_ge(pj_free, JOBS * g + n + 1)
                at = (g // PAIRS) * CTX + half * BANK
                hi, lo = (x[:, bass.ds(at, BANK)] for x in (xh, xl))
                pe.matmul(pj[:, :], wh[:, slot, cols], hi, start=True, stop=False)
                pe.matmul(pj[:, :], wh[:, slot, cols], lo, start=False, stop=False)
                pe.matmul(pj[:, :], wl[:, slot, cols], hi, start=False, stop=True).then_inc(pj_done, 1)

            def values(g, slot, half):
                pe.wait_ge(xb_in[slot], 8 * (g - slot) + 16)
                pe.wait_ge(pj_free, JOBS * g + UNITS + half + 1)
                for k in range(4):
                    t = 4 * half + k
                    m = pe.matmul(pj[:, k * P:(k + 1) * P], xb[:, slot, t * P:(t + 1) * P],
                                  w[:, slot, WV:WV + P], start=True, stop=True)
                m.then_inc(pj_done, 1)

            def score_max(g, slot, turn, c, n):
                h, t, k = (n % 2, n // 2, 0) if c == 0 else ((n // 2) % 2, n // 4, n % 2)
                if n == 0:
                    pe.wait_ge(pj_free, JOBS * g + (UNITS if c else 4) + 1)
                pe.wait_ge(mx_free, turn + 1)
                width = P * (t + 1) if k else BANK
                q = qa[:, slot, h, c * BANK + t * P:c * BANK + (t + 1) * P]
                m = pe.matmul(pm[:, turn_slot(c, n), 0:width], q, ka[:, slot, h, k * BANK:k * BANK + width],
                              start=True, stop=k == 0)
                if k:
                    m = pe.matmul(pm[:, turn_slot(c, n), width - P:width], idb[:, :], mkb[:, 0, :],
                                  start=False, stop=True)
                m.then_inc(mx_done, 1)

            def turn_max(g, turn, c):
                pe.wait_ge(mx_free, turn + 2)
                if c:
                    pe.wait_ge(folded, g + 1)
                pe.transpose(pm[:, turn_slot(c), 0:P], nmc[:, c, :], idf[:, :]).then_inc(mx_done, 1)

            def score(g, slot, c, j, h):
                lo = first_lo(c, j)
                at = score_slot(g, (c, j))
                if h == 0:
                    pe.wait_ge(s_free, score_turn(g, (c, j)) + 1)
                    if j == 0:
                        pe.wait_ge(mx_free, max_turn(g if c else g - 1, "turn", c) + 1 + 2)
                dst = ps[:, at, h, lo:BANK]
                keys = slice(j * P, (j + 1) * P)
                queries = slice(c * BANK + lo, (c + 1) * BANK)
                diag = c == 1 and j >= 4
                pe.matmul(dst, ka[:, slot, h, keys], qa[:, slot, h, queries], start=True, stop=False)
                m = pe.matmul(dst, kb[:, slot, h, keys], qb[:, slot, h, queries], start=False, stop=not diag)
                if diag:
                    m = pe.matmul(ps[:, at, h, lo:lo + P], idb[:, :], mkb[:, 1, :], start=False, stop=True)
                if h == 1:
                    m.then_inc(s_done, 1)

            def weigh(g, slot, c, j):
                lo = first_lo(c, j)
                pe.wait_ge(s_free, score_turn(g, (c, j)) + 1 + 2)
                if j == 0:
                    pe.wait_ge(po_free, sum_no(g, c) + 1)
                    if c == 0:
                        pe.wait_ge(pj_free, JOBS * (g + 1) + 1)
                for h in range(2):
                    m = pe.matmul(po[h * DK:(h + 1) * DK, lo:BANK], v[:, slot, j, h * DK:(h + 1) * DK],
                                  e[:, exp_no(0, c, j) % ESLOTS, h, lo:BANK], start=(j == 0),
                                  stop=(j == (NT - 1 if c else 3)))
                m.then_inc(pv_done, 1)

            def sums(g, c):
                what = "prev" if c < 0 else "own"
                pe.wait_ge(s_free, score_turn(g, what) + 1)
                pe.wait_ge(add_done, (ADDS * g if c < 0 else adds_with(g, 0, 3)) + ESLOTS)
                for h in range(2):
                    m = pe.matmul(ps[h * DK:(h + 1) * DK, score_slot(g, what), 0, :], ones[:, :],
                                  acc[:, c % 2, h, :], start=True, stop=True)
                m.then_inc(s_done, 1)

            def steps(g, slot, items):
                for kind, *at in items:
                    if kind == "unit":
                        project(g + 1, 1 - slot, at[0])
                    elif kind == "values":
                        values(g + 1, 1 - slot, at[0])
                    elif kind == "max":
                        own = target(0, "max", *at) == 0
                        score_max(g if own else g + 1, slot if own else 1 - slot, max_turn(g, "max", *at), *at)
                    elif kind == "turn":
                        turn_max(g, max_turn(g, "turn", at[0]), at[0])
                    elif kind == "score":
                        score(g, slot, *at)
                    elif kind == "pv":
                        weigh(g, slot, *at)
                    elif kind == "sum":
                        sums(g, at[0])

            pe.sem_inc(pv_done, ESLOTS)
            pe.wait_ge(x_lo, BATCH)
            pe.wait_ge(const_dve, CONSTS)
            pe.wait_ge(const_pool, 1)
            pairs(pe, steps)

        @block.vector
        def _(dve):
            def project_lo(g, slot, n):
                half, h, query = unit(n)
                cols = slice(half * BANK, (half + 1) * BANK)
                at = (WBQ if query else WBK) + h
                rows = slice(DK, P) if query else slice(0, DK)
                dst = (qa if query else kb)[rows, slot, h, cols]
                hi = (qa if query else ka)[rows, slot, h, cols].bitcast(F32)
                dve.wait_ge(pj_hi, UNITS * g + n + 1)
                dve.scalar_tensor_tensor(dst, pj[rows, :], w[rows, slot, at:at + 1], hi, ALU.add,
                                         ALU.subtract).then_inc(pj_free, 1)

            def values(g, slot, half):
                dve.wait_ge(pj_done, JOBS * g + UNITS + half + 1)
                bias = w[:, slot, WBV:WBV + P].unsqueeze(1).to_broadcast([P, 4, P])
                dve.tensor_tensor(v[:, slot, 4 * half:4 * half + 4, :], pj[:, :].rearrange("p (t d) -> p t d", t=4),
                                  bias, ALU.add).then_inc(pj_free, 1)

            def maximum(turn, c, n):
                h, t, k = (n % 2, n // 2, 0) if c == 0 else ((n // 2) % 2, n // 4, n % 2)
                width = P * (t + 1) if k else BANK
                at = 4 * h + t
                dst = part[:, at, k:k + 1] if c else nmc[:, 0, DK + at:DK + at + 1]
                dve.wait_ge(mx_done, turn + 1)
                dve.tensor_reduce(dst, pm[:, turn_slot(c, n), 0:width], AX.X, ALU.max, negate=True).then_inc(mx_free, 1)

            def fold(g):
                dve.wait_ge(mx_free, max_turn(g, "turn", 1) + 2)
                dve.tensor_reduce(nmc[:, 1, DK:DK + 8], part[:, :, :], AX.X, ALU.min).then_inc(folded, 1)

            def place(slot, turn, c):
                dve.wait_ge(mx_done, turn + 1)
                src = pm[DK:P, turn_slot(c), 0:P].unsqueeze(1).to_broadcast([DK, 8, P])
                dst = qb[DK:P, slot, :, c * BANK:(c + 1) * BANK].rearrange("p h (t q) -> p h t q", t=4)
                sel = pk[DK:P, :].unsqueeze(2).to_broadcast([DK, 8, P])
                split = "p (h t) q -> p h t q"
                dve.tensor_tensor(dst, src.rearrange(split, h=2), sel.rearrange(split, h=2), ALU.mult).then_inc(mx_free, 1)

            def invert(g, c, k):
                if k == 0:
                    dve.wait_ge(s_free, score_turn(g, "prev" if c < 0 else "own") + 1 + 2)
                piece = rs[:, c % 2, k * BANK // 2:(k + 1) * BANK // 2]
                dve.reciprocal(piece, piece).then_inc(inverted, 1)

            def steps(g, slot, items):
                for kind, *at in items:
                    if kind == "unit":
                        project_lo(g + 1, 1 - slot, at[0])
                    elif kind == "values":
                        values(g + 1, 1 - slot, at[0])
                    elif kind == "max":
                        maximum(max_turn(g, "max", *at), *at)
                    elif kind == "fold":
                        fold(g)
                    elif kind == "turn":
                        place(slot if at[0] else 1 - slot, max_turn(g, "turn", at[0]), at[0])
                    elif kind == "invert":
                        invert(g, *at)

            dve.sem_inc(pj_free, 1)
            dve.sem_inc(mx_free, 2)
            dve.memset(nmc[:, :, :], 0.0).then_inc(const_dve, 1)
            dve.memset(acc[:, 0, :, :], 0.0).then_inc(const_dve, 1)
            dve.wait_ge(const_in, 48)
            dve.tensor_copy(idb[:, :], idf[:, :]).then_inc(const_dve, 1)
            dve.tensor_copy(mkb[:, :, :], mkf[:, :, :]).then_inc(const_dve, 1)
            dve.tensor_reduce(col[:, :], pk[:, :], AX.X, ALU.add).then_inc(const_dve, 1)
            dve.wait_ge(const_dve, 5)
            for slot in range(2):
                for h in range(2):
                    dve.tensor_scalar(kb[DK:P, slot, h, :], acc[DK:P, 0, :, :].rearrange("p h q -> p (h q)"),
                                      col[DK:P, :], None, ALU.add).then_inc(const_dve, 1)
            for b in range(BATCH):
                dve.wait_ge(x_hi, b + 1)
                cols = slice(b * CTX, (b + 1) * CTX)
                dve.tensor_tensor(xl[:, cols], xb[:, b % 2, :], xh[:, cols].bitcast(F32),
                                  ALU.subtract).then_inc(x_lo, 1)
            pairs(dve, steps)


def gated_ffn(nc, ot_d, x_tok, wo, w_in, w_hid, w_out, scales, s3, ident, y_d):
    KC = HID // P
    UN = 4 * KC
    LN1, LN2 = 5, 6
    LINKS = LN1 + LN2
    LATE = 3 * KC - 2

    with ExitStack() as ctx:
        def sb(name, shape, dt):
            return ctx.enter_context(nc.sbuf_tensor(name, shape, dt))

        def sem(name):
            return ctx.enter_context(nc.semaphore(name))

        ot = sb("f_ot", [P, PAIRS, BANK], F32)
        xt = sb("f_xt", [P, TILES, P], F32)
        wo_s = sb("f_wo", [P, PAIRS, P], F32)
        raw = sb("f_raw", [P, 2 * HID + 2 * KC * HID + KC * P], F32)
        w12h = sb("f_w12h", [P, 2, HID], F32R)
        w12l = sb("f_w12l", [P, 2, HID], F32R)
        hh = sb("f_hh", [P, 2, KC, HID], F32R)
        hl = sb("f_hl", [P, 2, KC, HID], F32R)
        w3h = sb("f_w3h", [P, KC, P], F32R)
        w3l = sb("f_w3l", [P, KC, P], F32R)
        sc = sb("f_sc", [P, 4, KC], F32)
        s3b = sb("f_s3b", [P, P], F32)
        idf = sb("f_idf", [P, P], F32)
        half = sb("f_half", [P, TILES], F32)
        r1 = sb("f_r1", [P, TILES, P], F32)
        r2 = sb("f_r2", [P, TILES, P], F32)
        x1n = sb("f_x1n", [P, TILES, P], F32)
        x1 = sb("f_x1", [P, TILES, P], F32)
        x1h = sb("f_x1h", [P, BANK], F32R)
        x1l = sb("f_x1l", [P, BANK], F32R)
        gate = sb("f_gate", [P, 2, BANK], F32)
        act_f = sb("f_act", [P, 4, BANK], F32)
        ah = sb("f_ah", [P, 3, KC, BANK], F32R)
        al = sb("f_al", [P, 3, KC, BANK], F32R)
        y2 = sb("f_y2", [P, TILES, P], F32)
        st = sb("f_st", [P, TILES, 6], F32)
        mv = sb("f_mv", [P, TILES, 2], F32)
        ve = sb("f_ve", [P, TILES], F32)
        rstd = sb("f_rstd", [P, TILES], F32)

        pu = ctx.enter_context(nc.psum_tensor("f_pu", [P, 4, BANK], F32))
        py = ctx.enter_context(nc.psum_tensor("f_py", [P, TILES, P], F32))
        pz = ctx.enter_context(nc.psum_tensor("f_pz", [P, TILES, P], F32))

        held = sem("f_held")
        c_in = sem("f_c_in")
        raw_in = [sem(f"f_raw_in{k}") for k in range(5)]
        raw_hi = sem("f_raw_hi")
        raw_lo = sem("f_raw_lo")
        half_ok = sem("f_half_ok")
        ot_in = sem("f_ot_in")
        xt_in = sem("f_xt_in")
        wo_done = sem("f_wo_done")
        chain = sem("f_chain")
        pow_done = sem("f_pow_done")
        tr_done = sem("f_tr_done")
        tr_hi = sem("f_tr_hi")
        tr_lo = sem("f_tr_lo")
        u_done = sem("f_u_done")
        gate_ok = sem("f_gate_ok")
        prod_ok = sem("f_prod_ok")
        gelu_ok = sem("f_gelu_ok")
        hi_ok = sem("f_hi_ok")
        lo_ok = sem("f_lo_ok")
        z_done = sem("f_z_done")
        x1_ok = sem("f_x1_ok")
        y_out = sem("f_y_out")

        WEIGHTS = [(w12h[:, 0, :], w12l[:, 0, :], HID), (w12h[:, 1, :], w12l[:, 1, :], HID),
                   (hh[:, 0], hl[:, 0], KC * HID), (hh[:, 1], hl[:, 1], KC * HID),
                   (w3h[:, :, :], w3l[:, :, :], KC * P)]
        SOURCES = [w_in[0], w_in[1], w_hid[0], w_hid[1], w_out]
        RAW, at = [], 0
        for _, _, n in WEIGHTS:
            RAW.append(raw[:, at:at + n])
            at += n

        def flat(ap):
            return ap if len(ap.shape) == 2 else ap.rearrange("p a b -> p (a b)")

        block = ctx.enter_context(nc.Block())

        @block.sync
        def _(sp):
            sp.dma_start(wo_s[:, :, :], wo).then_inc(c_in, 16)
            sp.dma_start(ot[:, :, :], ot_d[0]).then_inc(ot_in, 16)
            sp.dma_start(xt[:, :, :], x_tok[0]).then_inc(xt_in, 16)
            sp.dma_start(idf[:, :], ident).then_inc(c_in, 16)
            sp.dma_start(sc[:, :, :], scales).then_inc(c_in, 16)
            sp.dma_start(s3b[:, :], s3).then_inc(c_in, 16)
            for k, (src, dst) in enumerate(zip(SOURCES, RAW)):
                sp.dma_start(dst, src).then_inc(raw_in[k], 16)
            sp.sem_inc(y_out, 16)
            sp.wait_ge(wo_done, 1)
            sp.dma_start(ot[:, :, :], ot_d[1]).then_inc(ot_in, 16)
            sp.wait_ge(chain, 1)
            sp.dma_start(xt[:, :, :], x_tok[1]).then_inc(xt_in, 16)
            with sp.Fori(0, CHUNKS - 2) as i:
                sp.wait_ge(wo_done, i + 2)
                sp.dma_start(ot[:, :, :], ot_d[i + 2]).then_inc(ot_in, 16)
                sp.wait_ge(chain, LINKS * i + LN1 + 1)
                sp.dma_start(xt[:, :, :], x_tok[i + 2]).then_inc(xt_in, 16)
                sp.wait_ge(chain, LINKS * i + LN1 + LINKS)
                sp.dma_start(y_d[i], y2[:, :, :]).then_inc(y_out, 16)
            for i in (CHUNKS - 2, CHUNKS - 1):
                sp.wait_ge(chain, LN1 + LINKS * (i + 1) - (LN1 if i == CHUNKS - 1 else 0))
                sp.dma_start(y_d[i], y2[:, :, :]).then_inc(y_out, 16)
            sp.wait_ge(y_out, 16 * (CHUNKS + 1))

        @block.gpsimd
        def _(pool):
            def power(n, at):
                pool.wait_ge(chain, at)
                pool.tensor_tensor(rstd[:, :], ve[:, :], half[:, :], ALU.pow).then_inc(pow_done, 1)

            def split(i, k):
                layer = k // KC
                if layer == 0:
                    pool.wait_ge(prod_ok, KC * i + k + 1)
                else:
                    pool.wait_ge(gelu_ok, 2 * KC * i + k - KC + 1)
                pool.sem_inc(held, 1)
                pool.tensor_scalar(ah[:, layer, k % KC, :], act_f[:, k % 4, :], 1.0, 1.0, ALU.mult,
                                   ALU.mult).then_inc(hi_ok, 1)

            def keep(at):
                pool.wait_ge(chain, at)
                pool.sem_inc(held, 1)
                pool.tensor_scalar(x1[:, :, :], x1n[:, :, :], 1.0, 1.0, ALU.mult, ALU.mult).then_inc(x1_ok, 1)

            def body(i, last):
                for k in range(KC, 2 * KC):
                    split(i, k)
                if not last:
                    power(2 * i + 1, LINKS * i + LN1 + 4)
                for k in range(2 * KC, 3 * KC):
                    split(i, k)
                if not last:
                    for k in range(KC):
                        split(i + 1, k)
                    keep(LINKS * i + 2 * LN1 + 2)
                power(2 * i + (1 if last else 2), LINKS * i + LN1 + (0 if last else LN1) + 5)

            pool.memset(half[:, :], -0.5).then_inc(half_ok, 1)
            pool.wait_ge(half_ok, 1)
            power(0, 4)
            keep(LN1)
            for k in range(KC):
                split(0, k)
            with pool.Fori(0, CHUNKS - 1) as i:
                body(i, False)
            body(CHUNKS - 1, True)

        @block.scalar
        def _(act):
            def weights_hi(k):
                act.wait_ge(raw_in[k], 16)
                act.activation(flat(WEIGHTS[k][0]), RAW[k], ACT.Copy).then_inc(raw_hi, 1)

            def tokens_hi(n):
                act.wait_ge(tr_done, n + 1)
                act.activation(x1h[:, :], py[:, :, :].rearrange("p t d -> p (t d)"), ACT.Copy).then_inc(tr_hi, 1)

            def gates(i):
                for m in range(KC):
                    act.wait_ge(u_done, UN * i + 2 * m + 1)
                    if m >= 2:
                        act.wait_ge(prod_ok, KC * i + m - 1)
                    act.activation(gate[:, m % 2, :], pu[:, (2 * m) % 4, :], ACT.Silu,
                                   scale=sc[:, 0, m:m + 1]).then_inc(gate_ok, 1)

            def body(i, last):
                for k in range(KC, 3 * KC):
                    act.wait_ge(u_done, UN * i + KC + k + 1)
                    act.wait_ge(lo_ok, 3 * KC * i + k - 3)
                    act.activation(act_f[:, k % 4, :], pu[:, (KC + k) % 4, :], ACT.Gelu,
                                   scale=sc[:, 1 + k // KC, k % KC:k % KC + 1]).then_inc(gelu_ok, 1)
                    if k == LATE and not last:
                        tokens_hi(i + 1)
                if not last:
                    gates(i + 1)

            for k in range(3):
                weights_hi(k)
            tokens_hi(0)
            for k in (3, 4):
                weights_hi(k)
            gates(0)
            with act.Fori(0, CHUNKS - 1) as i:
                body(i, False)
            body(CHUNKS - 1, True)

        @block.tensor
        def _(pe):
            def project(n):
                pe.wait_ge(ot_in, 16 * (n + 1))
                if not isinstance(n, int):
                    pe.wait_ge(tr_lo, n)
                for t in range(TILES):
                    for r in range(PAIRS):
                        m = pe.matmul(py[:, t, :], ot[:, r, t * P:(t + 1) * P], wo_s[:, r, :],
                                      start=(r == 0), stop=(r == PAIRS - 1))
                m.then_inc(wo_done, 1)

            def transposes(n, at):
                pe.wait_ge(chain, at)
                for t in range(TILES):
                    m = pe.transpose(py[:, t, :], x1n[:, t, :], idf[:, :])
                m.then_inc(tr_done, 1)

            def unit(i, u, wh, wl, xh, xl):
                dst = pu[:, u % 4, :]
                n = len(wh)
                for k in range(n):
                    pe.matmul(dst, wh[k], xh[k], start=(k == 0), stop=False)
                    pe.matmul(dst, wh[k], xl[k], start=False, stop=False)
                    m = pe.matmul(dst, wl[k], xh[k], start=False, stop=(k == n - 1))
                m.then_inc(u_done, 1)

            def gated(i, first):
                pe.wait_ge(tr_lo, i + 1)
                for u in range(2 * KC):
                    m, second = u // 2, u % 2
                    if u >= 4:
                        if second:
                            pe.wait_ge(prod_ok, KC * i + m - 1)
                        else:
                            pe.wait_ge(gate_ok, KC * i + m - 1)
                    elif not first:
                        pe.wait_ge(gelu_ok, 2 * KC * (i - 1) + KC + u + 1)
                    cols = slice(m * P, (m + 1) * P)
                    unit(i, u, [w12h[:, second, cols]], [w12l[:, second, cols]], [x1h[:, :]], [x1l[:, :]])

            def body(i, last):
                for k in range(KC, 3 * KC):
                    layer, m = k // KC, k % KC
                    if layer == 1:
                        pe.wait_ge(prod_ok, KC * i + 2 + m // 2 + 1)
                        pe.wait_ge(lo_ok, 3 * KC * i + KC)
                    else:
                        pe.wait_ge(gelu_ok, 2 * KC * i + m + 1)
                        pe.wait_ge(lo_ok, 3 * KC * i + 2 * KC)
                    cols = slice(m * P, (m + 1) * P)
                    unit(i, KC + k, [hh[:, layer - 1, j, cols] for j in range(KC)],
                         [hl[:, layer - 1, j, cols] for j in range(KC)],
                         [ah[:, layer - 1, j, :] for j in range(KC)], [al[:, layer - 1, j, :] for j in range(KC)])
                    if k == 2 * KC - 1 and not last:
                        project(i + 1)
                    if k == LATE and not last:
                        transposes(i + 1, LINKS * i + 2 * LN1)
                if not last:
                    gated(i + 1, False)
                pe.wait_ge(lo_ok, 3 * KC * (i + 1))
                if last:
                    pe.wait_ge(chain, LINKS * i)
                for t in range(TILES):
                    cols = slice(t * P, (t + 1) * P)
                    for j in range(KC):
                        pe.matmul(pz[:, t, :], ah[:, 2, j, cols], w3h[:, j, :], start=(j == 0), stop=False)
                        pe.matmul(pz[:, t, :], al[:, 2, j, cols], w3h[:, j, :], start=False, stop=False)
                        m = pe.matmul(pz[:, t, :], ah[:, 2, j, cols], w3l[:, j, :], start=False, stop=(j == KC - 1))
                m.then_inc(z_done, 1)

            pe.wait_ge(c_in, 64)
            project(0)
            transposes(0, LN1)
            pe.wait_ge(raw_lo, 2)
            gated(0, True)
            pe.wait_ge(raw_lo, len(WEIGHTS))
            with pe.Fori(0, CHUNKS - 1) as i:
                body(i, False)
            body(CHUNKS - 1, True)

        @block.vector
        def _(dve):
            def weights_lo(k):
                hi, lo, _ = WEIGHTS[k]
                dve.wait_ge(raw_hi, k + 1)
                dve.tensor_tensor(flat(lo), RAW[k], flat(hi).bitcast(F32), ALU.subtract).then_inc(raw_lo, 1)

            def norm(r, dst, n, at):
                dve.wait_ge(chain, at)
                for t in range(TILES):
                    m = dve.bn_stats(st[:, t, :], r[:, t, :])
                m.then_inc(chain, 1)
                dve.wait_ge(chain, at + 1)
                dve.sem_inc(held, 1)
                for t in range(TILES):
                    m = dve.bn_aggr(mv[:, t, :], st[:, t, :])
                m.then_inc(chain, 1)
                dve.wait_ge(chain, at + 2)
                dve.tensor_scalar(ve[:, :], mv[:, :, 1], EPS, None, ALU.add).then_inc(chain, 1)
                dve.wait_ge(pow_done, n + 1)
                for t in range(TILES):
                    m = dve.tensor_scalar(dst[:, t, :], r[:, t, :], mv[:, t, 0:1], rstd[:, t:t + 1],
                                          ALU.subtract, ALU.mult)
                m.then_inc(chain, 1)

            def norm1(i, n, at):
                dve.wait_ge(wo_done, i + 1)
                dve.wait_ge(xt_in, 16 * (i + 1))
                dve.tensor_tensor(r1[:, :, :], py[:, :, :], xt[:, :, :], ALU.add).then_inc(chain, 1)
                norm(r1, x1n, n, at + 1)

            def tokens_lo(n):
                dve.wait_ge(tr_hi, n + 1)
                dve.tensor_tensor(x1l[:, :], py[:, :, :].rearrange("p t d -> p (t d)"), x1h[:, :].bitcast(F32),
                                  ALU.subtract).then_inc(tr_lo, 1)

            def split(i, k):
                dve.wait_ge(hi_ok, 3 * KC * i + k + 1)
                dve.tensor_tensor(al[:, k // KC, k % KC, :], act_f[:, k % 4, :],
                                  ah[:, k // KC, k % KC, :].bitcast(F32), ALU.subtract).then_inc(lo_ok, 1)

            def products(i, first):
                for m in range(KC):
                    dve.wait_ge(u_done, UN * i + 2 * m + 2)
                    dve.wait_ge(gate_ok, KC * i + m + 1)
                    if not first:
                        dve.wait_ge(lo_ok, 3 * KC * i - KC + m + 1)
                    dve.scalar_tensor_tensor(act_f[:, m % 4, :], pu[:, (2 * m + 1) % 4, :], sc[:, 1, m:m + 1],
                                             gate[:, m % 2, :], ALU.mult, ALU.mult).then_inc(prod_ok, 1)
                    if m:
                        split(i, m - 1)
                split(i, KC - 1)

            def body(i, last):
                at = LINKS * i + LN1
                for k in range(KC, 2 * KC):
                    split(i, k)
                if not last:
                    dve.wait_ge(x1_ok, i + 1)
                    norm1(i + 1, 2 * i + 1, at)
                    at = at + LN1
                for k in range(2 * KC, 3 * KC):
                    split(i, k)
                    if k == LATE and not last:
                        tokens_lo(i + 1)
                if not last:
                    products(i + 1, False)
                dve.wait_ge(z_done, i + 1)
                dve.tensor_tensor(r2[:, :, :], pz[:, :, :], s3b[:, :].unsqueeze(1).to_broadcast([P, TILES, P]),
                                  ALU.mult).then_inc(chain, 1)
                dve.wait_ge(chain, at + 1)
                dve.tensor_tensor(r2[:, :, :], r2[:, :, :], x1[:, :, :], ALU.add).then_inc(chain, 1)
                dve.wait_ge(y_out, 16 * (i + 1))
                norm(r2, y2, 2 * i + (1 if last else 2), at + 2)

            weights_lo(0)
            weights_lo(1)
            norm1(0, 0, 0)
            weights_lo(2)
            tokens_lo(0)
            weights_lo(3)
            products(0, True)
            weights_lo(4)
            with dve.Fori(0, CHUNKS - 1) as i:
                body(i, False)
            body(CHUNKS - 1, True)


def state_space(nc, y_d, w_proj, conv, w_x, w_dt, a_log, w_out, sel, ident, z_d):
    NB = 2
    NS = 16
    STEPS = NB * NS
    NT = CTX // P
    HALVES = CTX // BANK
    KW = 4
    CB, CD, CT = KW, KW + 1, KW + 2
    LINKS = 9
    PIECE = 1024
    BX, HS, AS, HC = 4, 4, 3, 3

    BOTH = [(c, half) for half in range(HALVES) for c in range(NB)]
    PE_ORDER = ["tr0", "tr1"] + [("x", *u) for u in BOTH] + [("z", 0, 0), ("z", 1, 0), ("dbl", 0), ("z", 0, 1), ("z", 1, 1)]
    PE_ORDER += [("dt", 0, 0), ("dt", 1, 0), ("dbl", 1), ("dt", 0, 1), ("dt", 1, 1)]
    ACT_ORDER = ["xh0", "xh1"] + [("xin", *u) for u in BOTH] + [("xc", 0, 0), ("xc", 1, 0), ("z", 0, 0), ("z", 1, 0)]
    ACT_ORDER += [("xs", 0), ("z", 0, 1), ("z", 1, 1), ("xc", 0, 1), ("xc", 1, 1)]
    ACT_ORDER += [("abs", 0, 0), ("abs", 1, 0), ("xs", 1), ("abs", 0, 1), ("abs", 1, 1)]
    ACT_ORDER += [("exp", 0), ("exp", 1), ("ln", 0), ("ln", 1)]
    DVE_ORDER = ["xl0", "xl1"] + [("conv", c, half, k) for c, half in BOTH for k in range(KW)] + [("xs", 0), ("xs", 1)]
    DVE_ORDER += [("relu", *u) for u in BOTH] + [("soft", c, k) for k in range(3) for c in range(NB)]
    DVE_ORDER += [("soft", c, k) for k in (3, 4) for c in range(NB)]

    def pe_at(b, *name):
        return len(PE_ORDER) * b + PE_ORDER.index(name if len(name) > 1 else name[0]) + 1

    def act_at(b, *name):
        return len(ACT_ORDER) * b + ACT_ORDER.index(name if len(name) > 1 else name[0]) + 1

    def dve_at(b, *name):
        return len(DVE_ORDER) * b + DVE_ORDER.index(name if len(name) > 1 else name[0]) + 1

    with ExitStack() as ctx:
        def sb(name, shape, dt):
            return ctx.enter_context(nc.sbuf_tensor(name, shape, dt))

        def sem(name):
            return ctx.enter_context(nc.semaphore(name))

        xt = sb("m_xt", [P, NT, P], F32)
        xres = sb("m_xres", [P, NT, P], F32)
        xh = sb("m_xh", [P, CTX], F32R)
        xl = sb("m_xl", [P, CTX], F32R)
        raw = sb("m_raw", [P, 2, PIECE], F32)
        wph = sb("m_wph", [P, 4 * P], F32R)
        wpl = sb("m_wpl", [P, 4 * P], F32R)
        cv = sb("m_cv", [P, NB, KW + 3], F32)
        wx = sb("m_wx", [P, NB, DK], F32)
        wdh = sb("m_wdh", [P, NB * P], F32R)
        wdl = sb("m_wdl", [P, NB * P], F32R)
        av = sb("m_av", [P, NB * NS], F32)
        wo_s = sb("m_wo", [P, NB, P], F32)
        sl = sb("m_sl", [P, 2 * NS * P], F32R)
        idf = sb("m_idf", [P, P], F32)
        xin = sb("m_xin", [P, NB, KW - 1 + CTX], F32)
        xc = sb("m_xc", [P, NB, CTX], F32)
        sz = sb("m_sz", [P, NB, CTX], F32)
        xs = sb("m_xs", [P, CTX], F32R)
        dt = sb("m_dt", [P, NB, CTX], F32)
        dtx = sb("m_dtx", [P, NB, CTX], F32)
        ex = sb("m_ex", [P, NB, CTX], F32)
        rl = sb("m_rl", [P, NB, CTX], F32)
        px = sb("m_px", [P, BX, CTX], F32)
        a = sb("m_a", [P, AS, CTX], F32)
        cs = sb("m_cs", [P, 2, CTX], F32)
        hs = sb("m_hs", [P, HS, CTX], F32)
        hc = sb("m_hc", [P, HC, CTX], F32)
        yz = sb("m_yz", [P, NB, CTX], F32)
        r = sb("m_r", [P, NT, P], F32)
        y3 = sb("m_y3", [P, NT, P], F32)
        st = sb("m_st", [P, NT, 6], F32)
        mv = sb("m_mv", [P, NT, 2], F32)
        ve = sb("m_ve", [P, NT], F32)
        rstd = sb("m_rstd", [P, NT], F32)
        mhalf = sb("m_mhalf", [P, NT], F32)

        ps = ctx.enter_context(nc.psum_tensor("m_ps", [P, 8 * BANK], F32))
        pb, pc, py0, py1 = (ps[:, k * CTX:(k + 1) * CTX] for k in range(4))
        py = (py0, py1)

        def bank(k):
            return ps[:, k * BANK:(k + 1) * BANK]

        TR_BANK = (2, 3)
        X_BANK = {(0, 0): 4, (1, 0): 5, (0, 1): 6, (1, 1): 7}
        Z_BANK = {(0, 0): 2, (1, 0): 3, (0, 1): 4, (1, 1): 5}
        DBL_BANK = (6, 7)
        DT_BANK = {(0, 0): 2, (1, 0): 3, (0, 1): 4, (1, 1): 5}

        held = sem("m_held")
        c_in = sem("m_c_in")
        raw_in = [sem(f"m_raw_in{i}") for i in range(2)]
        raw_hi = sem("m_raw_hi")
        raw_lo = sem("m_raw_lo")
        a_exp = sem("m_a_exp")
        set_ok = sem("m_set_ok")
        mh_ok = sem("m_mh_ok")
        xt_in = sem("m_xt_in")
        res_ok = sem("m_res_ok")
        pe_pre = sem("m_pe_pre")
        act_pre = sem("m_act_pre")
        dve_pre = sem("m_dve_pre")
        bb_done = sem("m_bb_done")
        cc_done = sem("m_cc_done")
        a_done = sem("m_a_done")
        c_copied = sem("m_c_copied")
        bx_done = sem("m_bx_done")
        scan_done = sem("m_scan_done")
        hc_done = sem("m_hc_done")
        y_acc = sem("m_y_acc")
        chain = sem("m_chain")
        o_done = sem("m_o_done")
        pow_done = sem("m_pow_done")
        z_out = sem("m_z_out")

        STAGED = [(w_proj, wph[:, :]), (w_dt, wdh[:, :])]
        STAGED += [(sel[:, k:k + PIECE], sl[:, k:k + PIECE]) for k in range(0, 2 * NS * P, PIECE)]

        block = ctx.enter_context(nc.Block())

        def sequences(engine, body, end):
            body(0, True)
            with engine.Fori(1, BATCH) as b:
                body(b, False)
            end(BATCH - 1)

        @block.sync
        def _(sp):
            def load(b):
                for half in range(HALVES):
                    sp.dma_start(xt[:, half * TILES:(half + 1) * TILES, :], y_d[HALVES * b + half]).then_inc(xt_in, 16)

            def store(b):
                sp.wait_ge(chain, LINKS * (b + 1))
                for half in range(HALVES):
                    sp.dma_start(z_d[HALVES * b + half], y3[:, half * TILES:(half + 1) * TILES, :]).then_inc(z_out, 16)

            load(0)
            sp.dma_start(idf[:, :], ident).then_inc(c_in, 16)
            sp.dma_start(cv[:, :, :], conv).then_inc(c_in, 16)
            sp.dma_start(wx[:, :, :], w_x).then_inc(c_in, 16)
            sp.dma_start(av[:, :], a_log).then_inc(c_in, 16)
            sp.dma_start(wo_s[:, :, :], w_out).then_inc(c_in, 16)
            for k, (src, dst) in enumerate(STAGED):
                if k >= 2:
                    sp.wait_ge(raw_hi, k - 1)
                    sp.wait_ge(raw_lo, min(k - 1, 2))
                sp.dma_start(raw[:, k % 2, 0:dst.shape[1]], src).then_inc(raw_in[k % 2], 16)
            sp.sem_inc(z_out, 16 * HALVES)
            with sp.Fori(0, BATCH - 1) as b:
                sp.wait_ge(res_ok, b + 1)
                load(b + 1)
                store(b)
            store(BATCH - 1)
            sp.wait_ge(z_out, 16 * HALVES * (BATCH + 1))

        @block.gpsimd
        def _(pool):
            def keep(b, first):
                pool.wait_ge(xt_in, 16 * HALVES * (b + 1))
                pool.wait_ge(pe_pre, pe_at(b, "tr1"))
                if not first:
                    pool.wait_ge(chain, LINKS * (b - 1) + 5)
                pool.sem_inc(held, 1)
                pool.tensor_scalar(xres[:, :, :], xt[:, :, :], 1.0, 1.0, ALU.mult, ALU.mult).then_inc(res_ok, 1)

            def power(b):
                pool.wait_ge(chain, LINKS * b + 8)
                pool.tensor_tensor(rstd[:, :], ve[:, :], mhalf[:, :], ALU.pow).then_inc(pow_done, 1)

            def body(b, first):
                keep(b, first)
                if not first:
                    power(b - 1)
                for k in range(STEPS):
                    pool.wait_ge(scan_done, STEPS * b + k + 1)
                    pool.wait_ge(c_copied, NS * b + k // 2 + 1)
                    if k >= HC:
                        pool.wait_ge(y_acc, STEPS * b + k - HC + 1)
                    pool.tensor_tensor(hc[:, k % HC, :], hs[:, k % HS, :], cs[:, (k // 2) % 2, :],
                                       ALU.mult).then_inc(hc_done, 1)

            pool.memset(mhalf[:, :], -0.5).then_inc(mh_ok, 1)
            pool.wait_ge(mh_ok, 1)
            sequences(pool, body, power)

        @block.scalar
        def _(act):
            for k, (_, dst) in enumerate(STAGED):
                act.wait_ge(raw_in[k % 2], 16 * (k // 2 + 1))
                act.activation(dst, raw[:, k % 2, 0:dst.shape[1]], ACT.Copy).then_inc(raw_hi, 1)
            act.wait_ge(c_in, 80)
            act.activation(av[:, :], av[:, :], ACT.Exp).then_inc(a_exp, 1)

            def prepare(b):
                def xc_part(c, half):
                    cols = slice(half * BANK, (half + 1) * BANK)
                    act.wait_ge(dve_pre, dve_at(b, "conv", c, half, KW - 1))
                    act.activation(xc[:, c, cols], dtx[:, c, cols], ACT.Silu).then_inc(act_pre, 1)

                def sz_part(c, half):
                    at = half * BANK
                    act.wait_ge(pe_pre, pe_at(b, "z", c, half))
                    act.activation(sz[:, c, at:at + BANK], bank(Z_BANK[c, half]), ACT.Silu).then_inc(act_pre, 1)

                def xs_part(half):
                    cols = slice(half * BANK, (half + 1) * BANK)
                    act.wait_ge(pe_pre, pe_at(b, "dbl", half))
                    act.activation(xs[0:DK, cols], bank(DBL_BANK[half])[0:DK, :], ACT.Copy).then_inc(act_pre, 1)

                def dt_part(c, half):
                    cols = slice(half * BANK, (half + 1) * BANK)
                    src = bank(DT_BANK[c, half])
                    act.wait_ge(pe_pre, pe_at(b, "dt", c, half))
                    act.activation(ex[:, c, cols], src, ACT.Abs, bias=cv[:, c, CT:CT + 1]).then_inc(act_pre, 1)

                for half in range(HALVES):
                    act.wait_ge(pe_pre, pe_at(b, f"tr{half}"))
                    act.activation(xh[:, half * BANK:(half + 1) * BANK], bank(TR_BANK[half]), ACT.Copy).then_inc(act_pre, 1)
                for c, half in BOTH:
                    at = KW - 1 + half * BANK
                    act.wait_ge(pe_pre, pe_at(b, "x", c, half))
                    act.activation(xin[:, c, at:at + BANK], bank(X_BANK[c, half]), ACT.Copy).then_inc(act_pre, 1)
                xc_part(0, 0)
                xc_part(1, 0)
                sz_part(0, 0)
                sz_part(1, 0)
                xs_part(0)
                sz_part(0, 1)
                sz_part(1, 1)
                xc_part(0, 1)
                xc_part(1, 1)
                dt_part(0, 0)
                dt_part(1, 0)
                xs_part(1)
                dt_part(0, 1)
                dt_part(1, 1)
                for c in range(NB):
                    act.wait_ge(act_pre, act_at(b, "abs", c, 1))
                    act.activation(ex[:, c, :], ex[:, c, :], ACT.Exp, scale=-1.0).then_inc(act_pre, 1)
                for c in range(NB):
                    act.wait_ge(act_pre, act_at(b, "exp", c))
                    act.activation(dt[:, c, :], ex[:, c, :], ACT.Ln, bias=1.0).then_inc(act_pre, 1)

            def body(b, first):
                prepare(b)
                S0 = STEPS * b
                for k in range(STEPS):
                    n, c = k // 2, k % 2
                    if n == 0:
                        act.wait_ge(dve_pre, dve_at(b, "soft", c, 3))
                    if k >= AS:
                        act.wait_ge(scan_done, S0 + k - AS + 1)
                    act.activation(a[:, k % AS, :], dt[:, c, :], ACT.Exp, scale=av[:, c * NS + n:c * NS + n + 1]).then_inc(a_done, 1)
                    if c == 0:
                        act.wait_ge(cc_done, NS * b + n + 1)
                        if n >= 2:
                            act.wait_ge(hc_done, S0 + 2 * n - 2)
                        act.activation(cs[:, n % 2, :], pc, ACT.Copy).then_inc(c_copied, 1)

            act.wait_ge(set_ok, 3)
            sequences(act, body, lambda b: None)

        @block.tensor
        def _(pe):
            def project(b, name, base, banks, c, half, waits):
                cols = slice(base + c * P, base + (c + 1) * P)
                at = slice(half * BANK, (half + 1) * BANK)
                dst = bank(banks[c, half])
                for semaphore, count in waits:
                    pe.wait_ge(semaphore, count)
                pe.matmul(dst, wph[:, cols], xh[:, at], start=True, stop=False)
                pe.matmul(dst, wph[:, cols], xl[:, at], start=False, stop=False)
                pe.matmul(dst, wpl[:, cols], xh[:, at], start=False, stop=True).then_inc(pe_pre, 1)

            def finish(b):
                pe.wait_ge(chain, LINKS * b + 4)
                for t in range(NT):
                    cols = slice(t * P, (t + 1) * P)
                    for c in range(NB):
                        m = pe.matmul(pb[:, cols], yz[:, c, cols], wo_s[:, c, :], start=(c == 0), stop=(c == NB - 1))
                m.then_inc(o_done, 1)

            def prepare(b, first):
                pe.wait_ge(xt_in, 16 * HALVES * (b + 1))
                if not first:
                    pe.wait_ge(c_copied, NS * b)
                for t in range(NT):
                    m = pe.transpose(pc[:, t * P:(t + 1) * P], xt[:, t, :], idf[:, :])
                    if t % TILES == TILES - 1:
                        m.then_inc(pe_pre, 1)
                for half in range(HALVES):
                    project_x = [(c, half) for c in range(NB)]
                    for u in project_x:
                        project(b, "x", 0, X_BANK, *u, [(dve_pre, dve_at(b, f"xl{half}"))])
                    if half == 0 and not first:
                        finish(b - 1)

                def project_z(half):
                    for c in range(NB):
                        before = (dve_pre, dve_at(b, "xl1")) if half == 0 else (act_pre, act_at(b, "xin", c, 0))
                        project(b, "z", 2 * P, Z_BANK, c, half, [before])

                def double(half):
                    cols = slice(half * BANK, (half + 1) * BANK)
                    pe.wait_ge(act_pre, act_at(b, "xc", 1, half))
                    for c in range(NB):
                        m = pe.matmul(bank(DBL_BANK[half])[0:DK, :], wx[:, c, :], xc[:, c, cols], start=(c == 0), stop=(c == NB - 1))
                    m.then_inc(pe_pre, 1)

                def widen(half):
                    cols = slice(half * BANK, (half + 1) * BANK)
                    pe.wait_ge(dve_pre, dve_at(b, "xs", half))
                    for c in range(NB):
                        dst = bank(DT_BANK[c, half])
                        pe.wait_ge(act_pre, act_at(b, "z", c, half))
                        pe.matmul(dst, wdh[:, c * P:(c + 1) * P], xs[:, cols], start=True, stop=False)
                        pe.matmul(dst, wdl[:, c * P:(c + 1) * P], xs[:, cols], start=False, stop=True).then_inc(pe_pre, 1)

                project_z(0)
                double(0)
                project_z(1)
                widen(0)
                double(1)
                widen(1)

            def body(b, first):
                prepare(b, first)
                S0 = STEPS * b

                def broadcast_b(n):
                    if n:
                        pe.wait_ge(bx_done, S0 + 2 * n)
                    elif not first:
                        pe.wait_ge(chain, LINKS * (b - 1) + 5)
                    for half in range(HALVES):
                        cols = slice(half * BANK, (half + 1) * BANK)
                        m = pe.matmul(pb[:, cols], sl[:, n * P:(n + 1) * P], xs[:, cols], start=True, stop=True)
                    m.then_inc(bb_done, 1)

                def broadcast_c(n):
                    if n:
                        pe.wait_ge(c_copied, NS * b + n)
                    else:
                        pe.wait_ge(act_pre, act_at(b, "abs", 1, 1))
                        pe.wait_ge(dve_pre, dve_at(b, "relu", 1, 1))
                    for half in range(HALVES):
                        cols = slice(half * BANK, (half + 1) * BANK)
                        m = pe.matmul(pc[:, cols], sl[:, (NS + n) * P:(NS + n + 1) * P], xs[:, cols], start=True, stop=True)
                    m.then_inc(cc_done, 1)

                def add_up(k):
                    n, c = k // 2, k % 2
                    pe.wait_ge(hc_done, S0 + k + 1)
                    for half in range(HALVES):
                        cols = slice(half * BANK, (half + 1) * BANK)
                        m = pe.matmul(py[c][:, cols], idf[:, :], hc[:, k % HC, cols], start=(n == 0), stop=(n == NS - 1))
                    m.then_inc(y_acc, 1)

                broadcast_b(0)
                broadcast_c(0)
                broadcast_b(1)
                broadcast_c(1)
                broadcast_b(2)
                for k in range(STEPS):
                    n = k // 2
                    if k % 2 == 0 and n + 2 < NS:
                        broadcast_c(n + 2)
                    if k % 2 == 1 and n + 3 < NS:
                        broadcast_b(n + 3)
                    add_up(k)

            pe.wait_ge(c_in, 80)
            pe.wait_ge(raw_lo, 2)
            pe.wait_ge(raw_hi, len(STAGED))
            sequences(pe, body, finish)

        @block.vector
        def _(dve):
            for k, (lo, hi) in enumerate(((wpl[:, :], wph[:, :]), (wdl[:, :], wdh[:, :]))):
                dve.wait_ge(raw_hi, k + 1)
                dve.tensor_tensor(lo, raw[:, k, 0:lo.shape[1]], hi.bitcast(F32), ALU.subtract).then_inc(raw_lo, 1)
            dve.memset(xin[:, 0, 0:KW - 1], 0.0).then_inc(set_ok, 1)
            dve.memset(xin[:, 1, 0:KW - 1], 0.0).then_inc(set_ok, 1)
            dve.wait_ge(a_exp, 1)
            dve.tensor_scalar(av[:, :], av[:, :], -1.0, None, ALU.mult).then_inc(set_ok, 1)
            dve.wait_ge(set_ok, 2)

            def gated(b, c):
                dve.wait_ge(y_acc, STEPS * b + STEPS)
                dve.scalar_tensor_tensor(yz[:, c, :], xc[:, c, :], cv[:, c, CD:CD + 1], py[c], ALU.mult,
                                         ALU.add).then_inc(chain, 1)

            def gate(b, c):
                dve.wait_ge(chain, LINKS * b + c + 1)
                dve.tensor_tensor(yz[:, c, :], yz[:, c, :], sz[:, c, :], ALU.mult).then_inc(chain, 1)

            def residual(b):
                dve.wait_ge(o_done, b + 1)
                dve.wait_ge(res_ok, b + 1)
                dve.tensor_tensor(r[:, :, :], pb.rearrange("p (t d) -> p t d", t=NT), xres[:, :, :], ALU.add).then_inc(chain, 1)

            def moments(b):
                dve.wait_ge(chain, LINKS * b + 5)
                for t in range(NT):
                    m = dve.bn_stats(st[:, t, :], r[:, t, :])
                m.then_inc(chain, 1)
                dve.wait_ge(chain, LINKS * b + 6)
                dve.sem_inc(held, 1)
                for t in range(NT):
                    m = dve.bn_aggr(mv[:, t, :], st[:, t, :])
                m.then_inc(chain, 1)
                dve.wait_ge(chain, LINKS * b + 7)
                dve.tensor_scalar(ve[:, :], mv[:, :, 1], EPS, None, ALU.add).then_inc(chain, 1)

            def normed(b):
                dve.wait_ge(pow_done, b + 1)
                dve.wait_ge(z_out, 16 * HALVES * (b + 1))
                for t in range(NT):
                    m = dve.tensor_scalar(y3[:, t, :], r[:, t, :], mv[:, t, 0:1], rstd[:, t:t + 1], ALU.subtract, ALU.mult)
                m.then_inc(chain, 1)

            def prepare(b, first):
                def convolve(c, half):
                    at = half * BANK
                    acc = dtx[:, c, at:at + BANK]
                    dve.wait_ge(act_pre, act_at(b, "xin", c, half))
                    dve.tensor_scalar(acc, xin[:, c, at:at + BANK], cv[:, c, 0:1], cv[:, c, CB:CB + 1], ALU.mult,
                                      ALU.add).then_inc(dve_pre, 1)
                    for k in range(1, KW):
                        dve.wait_ge(dve_pre, dve_at(b, "conv", c, half, k - 1))
                        dve.scalar_tensor_tensor(acc, xin[:, c, at + k:at + k + BANK], cv[:, c, k:k + 1], acc,
                                                 ALU.mult, ALU.add).then_inc(dve_pre, 1)

                def xs_part(half):
                    cols = slice(half * BANK, (half + 1) * BANK)
                    dve.wait_ge(act_pre, act_at(b, "xs", half))
                    dve.tensor_tensor(xs[DK:P, cols], bank(DBL_BANK[half])[0:DK, :], xs[0:DK, cols].bitcast(F32),
                                      ALU.subtract).then_inc(dve_pre, 1)

                if not first:
                    for c in range(NB):
                        gated(b - 1, c)
                for half in range(HALVES):
                    cols = slice(half * BANK, (half + 1) * BANK)
                    dve.wait_ge(act_pre, act_at(b, f"xh{half}"))
                    dve.tensor_tensor(xl[:, cols], bank(TR_BANK[half]), xh[:, cols].bitcast(F32), ALU.subtract).then_inc(dve_pre, 1)
                if not first:
                    for c in range(NB):
                        gate(b - 1, c)
                for c, half in BOTH:
                    convolve(c, half)
                xs_part(0)
                if not first:
                    residual(b - 1)
                xs_part(1)
                for c, half in BOTH:
                    cols = slice(half * BANK, (half + 1) * BANK)
                    dve.wait_ge(pe_pre, pe_at(b, "dt", c, half))
                    dve.wait_ge(act_pre, act_at(b, "abs", c, half))
                    dve.tensor_scalar(rl[:, c, cols], bank(DT_BANK[c, half]), cv[:, c, CT:CT + 1], 0.0, ALU.add,
                                      ALU.max).then_inc(dve_pre, 1)
                if not first:
                    moments(b - 1)
                for c in range(NB):
                    dve.wait_ge(act_pre, act_at(b, "exp", c))
                    dve.tensor_scalar(dtx[:, c, :], ex[:, c, :], 1.0, None, ALU.add).then_inc(dve_pre, 1)
                for c in range(NB):
                    dve.wait_ge(dve_pre, dve_at(b, "soft", c, 0))
                    dve.scalar_tensor_tensor(dtx[:, c, :], dtx[:, c, :], -1.0, ex[:, c, :], ALU.add,
                                             ALU.subtract).then_inc(dve_pre, 1)
                for c in range(NB):
                    dve.wait_ge(dve_pre, dve_at(b, "soft", c, 1))
                    dve.tensor_tensor(rl[:, c, :], rl[:, c, :], dtx[:, c, :], ALU.subtract).then_inc(dve_pre, 1)
                for c in range(NB):
                    dve.wait_ge(act_pre, act_at(b, "ln", c))
                    dve.wait_ge(dve_pre, dve_at(b, "soft", c, 2))
                    dve.tensor_tensor(dt[:, c, :], dt[:, c, :], rl[:, c, :], ALU.add).then_inc(dve_pre, 1)
                for c in range(NB):
                    dve.wait_ge(dve_pre, dve_at(b, "soft", c, 3))
                    dve.tensor_tensor(dtx[:, c, :], dt[:, c, :], xc[:, c, :], ALU.mult).then_inc(dve_pre, 1)

            def body(b, first):
                prepare(b, first)
                S0 = STEPS * b

                def inputs(n):
                    dve.wait_ge(bb_done, NS * b + n + 1)
                    for c in range(NB):
                        k = 2 * n + c
                        if n == 0:
                            dve.wait_ge(dve_pre, dve_at(b, "soft", c, 4))
                        if k >= BX:
                            dve.wait_ge(scan_done, S0 + k - BX + 1)
                        dve.tensor_tensor(px[:, k % BX, :], pb, dtx[:, c, :], ALU.mult).then_inc(bx_done, 1)

                inputs(0)
                if not first:
                    normed(b - 1)
                for n in range(NS):
                    if n + 1 < NS:
                        inputs(n + 1)
                    for k in (2 * n, 2 * n + 1):
                        dve.wait_ge(bx_done, S0 + k + 1)
                        dve.wait_ge(a_done, S0 + k + 1)
                        if k >= HS:
                            dve.wait_ge(hc_done, S0 + k - HS + 1)
                        dve.tensor_tensor_scan(hs[:, k % HS, :], a[:, k % AS, :], px[:, k % BX, :], 0.0, ALU.mult,
                                               ALU.add).then_inc(scan_done, 1)

            def end(b):
                for c in range(NB):
                    gated(b, c)
                for c in range(NB):
                    gate(b, c)
                residual(b)
                moments(b)
                normed(b)

            sequences(dve, body, end)


def ternary_ffn(nc, z_d, w1, w2, b1, b2, ident, out):
    KC = HID // P
    ROUNDS = CHUNKS // 2
    LINKS = 7

    with ExitStack() as ctx:
        def sb(name, shape, dt):
            return ctx.enter_context(nc.sbuf_tensor(name, shape, dt))

        def sem(name):
            return ctx.enter_context(nc.semaphore(name))

        wr = sb("t_wr", [P, 2, HID], F32)
        above = sb("t_above", [P, 2, HID], F32)
        below = sb("t_below", [P, 2, HID], F32)
        wq = sb("t_wq", [P, 2, HID], F32R)
        asum = sb("t_asum", [P, 2], F32)
        th = sb("t_th", [P, 2, 2], F32)
        ones = sb("t_ones", [P, P], F32)
        idf = sb("t_idf", [P, P], F32)
        bv1 = sb("t_b1", [P, KC], F32)
        bv2 = sb("t_b2", [P, P], F32)
        mhalf = sb("t_mhalf", [P, 2 * TILES], F32)
        xt = sb("t_xt", [P, 2, TILES, P], F32)
        xb = sb("t_xb", [P, 2, TILES, P], F32)
        xh = sb("t_xh", [P, 2, BANK], F32R)
        xl = sb("t_xl", [P, 2, BANK], F32R)
        hf = sb("t_hf", [P, 2, KC, BANK], F32)
        hh = sb("t_hh", [P, 2, KC, BANK], F32R)
        hl = sb("t_hl", [P, 2, KC, BANK], F32R)
        r = sb("t_r", [P, 2, TILES, P], F32)
        y = sb("t_y", [P, 2, TILES, P], F32)
        st = sb("t_st", [P, 2 * TILES, 6], F32)
        mv = sb("t_mv", [P, 2 * TILES, 2], F32)
        ve = sb("t_ve", [P, 2 * TILES], F32)
        rstd = sb("t_rstd", [P, 2 * TILES], F32)
        pu = ctx.enter_context(nc.psum_tensor("t_pu", [P, KC, BANK], F32))
        pt = ctx.enter_context(nc.psum_tensor("t_pt", [P, 2, TILES, P], F32))
        pz = ctx.enter_context(nc.psum_tensor("t_pz", [P, 2, TILES, P], F32))

        held = sem("t_held")
        c_in = sem("t_c_in")
        set_ok = sem("t_set_ok")
        q_sum = sem("t_q_sum")
        q_dve = sem("t_q_dve")
        xt_in = [sem(f"t_xt_in{i}") for i in range(2)]
        tr_done = sem("t_tr_done")
        tr_hi = sem("t_tr_hi")
        tr_lo = sem("t_tr_lo")
        xb_ok = sem("t_xb_ok")
        u_done = sem("t_u_done")
        relu_ok = sem("t_relu_ok")
        hi_ok = sem("t_hi_ok")
        lo_ok = sem("t_lo_ok")
        z_done = sem("t_z_done")
        chain = sem("t_chain")
        pow_done = sem("t_pow_done")
        y_out = [sem(f"t_y_out{i}") for i in range(2)]

        block = ctx.enter_context(nc.Block())

        def rounds(engine, body):
            with engine.Fori(0, ROUNDS - 1) as g:
                body(g, False)
            body(ROUNDS - 1, True)

        @block.sync
        def _(sp):
            for dst, src in ((wr[:, 0, :], w1), (wr[:, 1, :], w2), (idf[:, :], ident), (bv1[:, :], b1), (bv2[:, :], b2)):
                sp.dma_start(dst, src).then_inc(c_in, 16)
            for s in range(2):
                sp.dma_start(xt[:, s], z_d[s]).then_inc(xt_in[s], 16)
                sp.sem_inc(y_out[s], 16)

            def body(g, last):
                for s in range(2):
                    if not last:
                        sp.wait_ge(xb_ok, 2 * g + s + 1)
                        sp.dma_start(xt[:, s], z_d[2 * g + 2 + s]).then_inc(xt_in[s], 16)
                for s in range(2):
                    sp.wait_ge(chain, LINKS * (g + 1) + 6 + s)
                    sp.dma_start(out[2 * g + s], y[:, s]).then_inc(y_out[s], 16)

            rounds(sp, body)
            for s in range(2):
                sp.wait_ge(y_out[s], 16 * (ROUNDS + 1))

        @block.gpsimd
        def _(pool):
            def residual(g, s, first):
                pool.wait_ge(xt_in[s], 16 * (g + 1))
                pool.wait_ge(tr_done, 2 * g + s + 1)
                if not first:
                    pool.wait_ge(chain, LINKS * g + s + 1)
                pool.tensor_tensor(xb[:, s], xt[:, s], bv2[:, :].unsqueeze(1).to_broadcast([P, TILES, P]),
                                   ALU.add).then_inc(xb_ok, 1)

            def body(g, last):
                for s in range(2):
                    for k in range(KC):
                        pool.wait_ge(relu_ok, KC * (2 * g + s) + k + 1 + KC)
                        pool.sem_inc(held, 1)
                        pool.tensor_scalar(hh[:, s, k, :], hf[:, s, k, :], 1.0, 1.0, ALU.mult, ALU.mult).then_inc(hi_ok, 1)
                for s in range(2):
                    if not last:
                        residual(g + 1, s, False)
                pool.wait_ge(chain, LINKS * (g + 1) + 5)
                pool.tensor_tensor(rstd[:, :], ve[:, :], mhalf[:, :], ALU.pow).then_inc(pow_done, 1)

            pool.memset(ones[:, :], 1.0).then_inc(set_ok, 1)
            pool.memset(mhalf[:, :], -0.5).then_inc(set_ok, 1)
            pool.wait_ge(set_ok, 2)
            pool.wait_ge(c_in, 80)
            for s in range(2):
                residual(0, s, True)
            rounds(pool, body)

        @block.scalar
        def _(act):
            def tokens_hi(i, s):
                act.wait_ge(tr_done, i + 1)
                act.activation(xh[:, s, :], pt[:, s].rearrange("p t d -> p (t d)"), ACT.Copy).then_inc(tr_hi, 1)

            def body(g, last):
                for s in range(2):
                    for k in range(KC):
                        act.wait_ge(u_done, KC * (2 * g + s) + k + 1)
                        act.activation(hf[:, s, k, :], pu[:, k, :], ACT.Relu, bias=bv1[:, k:k + 1]).then_inc(relu_ok, 1)
                for s in range(2):
                    if not last:
                        tokens_hi(2 * g + 2 + s, s)

            act.sem_inc(relu_ok, KC)
            act.wait_ge(c_in, 80)
            for s in range(2):
                tokens_hi(s, s)
            rounds(act, body)

        @block.tensor
        def _(pe):
            def transposes(g, s):
                pe.wait_ge(xt_in[s], 16 * (g + 1))
                for t in range(TILES):
                    m = pe.transpose(pt[:, s, t, :], xt[:, s, t, :], idf[:, :])
                m.then_inc(tr_done, 1)

            def body(g, last):
                for s in range(2):
                    i = 2 * g + s
                    pe.wait_ge(tr_lo, i + 1)
                    for k in range(KC):
                        pe.wait_ge(relu_ok, KC * i + k + 1)
                        cols = slice(k * P, (k + 1) * P)
                        pe.matmul(pu[:, k, :], wq[:, 0, cols], xh[:, s, :], start=True, stop=False)
                        pe.matmul(pu[:, k, :], wq[:, 0, cols], xl[:, s, :], start=False, stop=True).then_inc(u_done, 1)
                for s in range(2):
                    if not last:
                        transposes(g + 1, s)
                for s in range(2):
                    pe.wait_ge(lo_ok, KC * (2 * g + s + 1))
                    pe.wait_ge(chain, LINKS * g + s + 1)
                    for t in range(TILES):
                        cols = slice(t * P, (t + 1) * P)
                        for k in range(KC):
                            pe.matmul(pz[:, s, t, :], hh[:, s, k, cols], wq[:, 1, k * P:(k + 1) * P], start=(k == 0), stop=False)
                            m = pe.matmul(pz[:, s, t, :], hl[:, s, k, cols], wq[:, 1, k * P:(k + 1) * P], start=False, stop=(k == KC - 1))
                    m.then_inc(z_done, 1)

            pe.wait_ge(c_in, 80)
            pe.wait_ge(set_ok, 2)
            for s in range(2):
                transposes(0, s)
            pe.wait_ge(q_dve, 2)
            pe.matmul(pz[:, 0, 0, 0:2], ones[:, :], asum[:, :], start=True, stop=True).then_inc(q_sum, 1)
            pe.wait_ge(q_dve, 9)
            rounds(pe, body)

        @block.vector
        def _(dve):
            def tokens_lo(i, s):
                dve.wait_ge(tr_hi, i + 1)
                dve.tensor_tensor(xl[:, s, :], pt[:, s].rearrange("p t d -> p (t d)"), xh[:, s, :].bitcast(F32),
                                  ALU.subtract).then_inc(tr_lo, 1)

            def body(g, last):
                for s in range(2):
                    for k in range(KC):
                        dve.wait_ge(hi_ok, KC * (2 * g + s) + k + 1)
                        dve.tensor_tensor(hl[:, s, k, :], hf[:, s, k, :], hh[:, s, k, :].bitcast(F32),
                                          ALU.subtract).then_inc(lo_ok, 1)
                for s in range(2):
                    if not last:
                        tokens_lo(2 * g + 2 + s, s)
                at = LINKS * (g + 1)
                for s in range(2):
                    dve.wait_ge(z_done, 2 * g + s + 1)
                    dve.wait_ge(xb_ok, 2 * g + s + 1)
                    dve.tensor_tensor(r[:, s], pz[:, s], xb[:, s], ALU.add).then_inc(chain, 1)
                for s in range(2):
                    dve.wait_ge(chain, at + 1 + s)
                    for t in range(TILES):
                        m = dve.bn_stats(st[:, TILES * s + t, :], r[:, s, t, :])
                m.then_inc(chain, 1)
                dve.wait_ge(chain, at + 3)
                dve.sem_inc(held, 1)
                for t in range(2 * TILES):
                    m = dve.bn_aggr(mv[:, t, :], st[:, t, :])
                m.then_inc(chain, 1)
                dve.wait_ge(chain, at + 4)
                dve.tensor_scalar(ve[:, :], mv[:, :, 1], EPS, None, ALU.add).then_inc(chain, 1)
                dve.wait_ge(pow_done, g + 1)
                for s in range(2):
                    dve.wait_ge(y_out[s], 16 * (g + 1))
                    for t in range(TILES):
                        at_t = TILES * s + t
                        m = dve.tensor_scalar(y[:, s, t, :], r[:, s, t, :], mv[:, at_t, 0:1],
                                              rstd[:, at_t:at_t + 1], ALU.subtract, ALU.mult)
                    m.then_inc(chain, 1)

            dve.sem_inc(chain, LINKS)
            dve.wait_ge(c_in, 80)
            for j in range(2):
                dve.tensor_reduce(asum[:, j:j + 1], wr[:, j, :], AX.X, ALU.add, apply_absolute_value=True).then_inc(q_dve, 1)
            dve.wait_ge(q_sum, 1)
            dve.tensor_scalar(th[:, 0, :], pz[:, 0, 0, 0:2], 1.0 / (D * HID), EPS, ALU.mult, ALU.add).then_inc(q_dve, 1)
            dve.wait_ge(q_dve, 3)
            dve.tensor_scalar(th[:, 1, :], th[:, 0, :], -0.5, None, ALU.mult).then_inc(q_dve, 1)
            dve.wait_ge(q_dve, 4)
            dve.tensor_scalar(th[:, 0, :], th[:, 1, :], -1.0, None, ALU.mult).then_inc(q_dve, 1)
            dve.wait_ge(q_dve, 5)
            for j in range(2):
                dve.tensor_scalar(above[:, j, :], wr[:, j, :], th[:, 0, j:j + 1], None, ALU.is_gt)
                m = dve.tensor_scalar(below[:, j, :], wr[:, j, :], th[:, 1, j:j + 1], None, ALU.is_lt)
                m.then_inc(q_dve, 1)
            dve.wait_ge(q_dve, 7)
            for j in range(2):
                dve.tensor_tensor(wq[:, j, :], above[:, j, :], below[:, j, :], ALU.subtract).then_inc(q_dve, 1)
            for s in range(2):
                tokens_lo(s, s)
            rounds(dve, body)


def program(nc, x_tok, xT, wpk, masks, pick, wo, w_in, w_hid, w_out, scales, s3, w_proj, conv, w_x, w_dt, a_log,
            w_mix, sel, w1, w2, b1, b2, ident, out):
    ot_d = nc.dram_tensor("attended", [CHUNKS, P, PAIRS, BANK], F32, kind="Internal").ap()
    y_d = nc.dram_tensor("after_gated", [CHUNKS, P, TILES, P], F32, kind="Internal").ap()
    z_d = nc.dram_tensor("after_mixer", [CHUNKS, P, TILES, P], F32, kind="Internal").ap()
    attention(nc, xT, wpk, ident, masks, pick, ot_d)
    gated_ffn(nc, ot_d, x_tok, wo, w_in, w_hid, w_out, scales, s3, ident, y_d)
    state_space(nc, y_d, w_proj, conv, w_x, w_dt, a_log, w_mix, sel, ident, z_d)
    ternary_ffn(nc, z_d, w1, w2, b1, b2, ident, out)


def kernel(**inputs):
    import numpy as np
    import concourse.bacc as bacc
    from concourse.bass_utils import run_bass_kernel_spmd

    t = {k: np.asarray(v) for k, v in inputs.items()}

    def tiled(m):
        return np.ascontiguousarray(m.reshape(-1, P, m.shape[1]).transpose(1, 0, 2))

    def spread(vec):
        return np.ascontiguousarray(np.broadcast_to(vec, (P, vec.shape[0])))

    x = t["L0_attn_x"].reshape(TOK, D)
    wpk = np.empty((PAIRS, P, WCOLS), np.float32)
    for pair in range(PAIRS):
        both = slice(2 * DK * pair, 2 * DK * (pair + 1))
        for h in range(2):
            cols = slice(DK * (2 * pair + h), DK * (2 * pair + h + 1))
            for k in range(2):
                at = slice(P * h + DK * k, P * h + DK * (k + 1))
                rows = slice(DK * k, DK * (k + 1))
                wpk[pair, :, WQ:WQ + 256][:, at] = t["L0_attn_Wq"][:, cols]
                wpk[pair, :, WK:WK + 256][:, at] = t["L0_attn_Wk"][:, cols]
                wpk[pair, rows, WBQ + h] = t["L0_attn_bq"][cols]
                wpk[pair, rows, WBK + h] = t["L0_attn_bk"][cols]
        wpk[pair, :, WV:WV + P] = t["L0_attn_Wv"][:, both]
        wpk[pair, :, WBV:WBV + P] = t["L0_attn_bv"][both]

    key = np.arange(P)
    mask = np.where(key[None, :] <= key[:, None], 0.0, -1e30).astype(np.float32)
    pick = np.zeros((P, 8), np.float32)
    pick[DK + np.arange(8), np.arange(8)] = 1.0
    per_block = lambda vec: vec.reshape(-1, P).T
    conv = np.concatenate([t["L1_attn_conv_w"].reshape(2, P, 4).transpose(1, 0, 2)] +
                          [per_block(t[n])[:, :, None] for n in ("L1_attn_conv_b", "L1_attn_D_param", "L1_attn_dt_proj_b")], 2)
    w_x = np.zeros((P, 2, DK), np.float32)
    w_x[:, :, 0:40] = tiled(t["L1_attn_x_proj_w"].T)
    w_dt = np.zeros((P, 256), np.float32)
    sel = np.zeros((P, 32, P), np.float32)
    for lo in (0, DK):
        w_dt[lo:lo + 8] = t["L1_attn_dt_proj_w"].T
        for n in range(32):
            sel[lo + 8 + n, n] = 1.0

    arrays = {
        "x_tok": x.reshape(CHUNKS, TILES, P, D).transpose(0, 2, 1, 3),
        "xT": x.T,
        "wpk": wpk,
        "masks": np.stack([mask, mask.T], 1),
        "pick": pick,
        "wo": tiled(t["L0_attn_Wo"]),
        "w_in": np.stack([t["L0_ffn_w1_w"].T, t["L0_ffn_w2_w"].T]),
        "w_hid": np.stack([tiled(t[n].T).reshape(P, -1) for n in ("L0_ffn_h1_w", "L0_ffn_h2_w")]),
        "w_out": tiled(t["L0_ffn_w3_w"].T).reshape(P, -1),
        "scales": np.stack([per_block(t[f"L0_ffn_{n}_s"]) for n in ("w1", "w2", "h1", "h2")], 1),
        "s3": spread(t["L0_ffn_w3_s"]),
        "w_proj": t["L1_attn_in_proj_w"].T,
        "conv": conv,
        "w_x": w_x,
        "w_dt": w_dt,
        "a_log": tiled(t["L1_attn_A_log"]).reshape(P, -1),
        "w_mix": tiled(t["L1_attn_out_proj_w"].T),
        "sel": sel.reshape(P, -1),
        "w1": t["L1_ffn_W1"].T,
        "w2": tiled(t["L1_ffn_W2"].T).reshape(P, -1),
        "b1": per_block(t["L1_ffn_b1"]),
        "b2": spread(t["L1_ffn_b2"]),
        "ident": np.eye(P, dtype=np.float32),
    }
    arrays = {f"in_{k}": np.ascontiguousarray(v) for k, v in arrays.items()}
    nc = bacc.Bacc("TRN2", target_bir_lowering=False, num_devices=1)
    args = [nc.dram_tensor(k, v.shape, mybir.dt.from_np(v.dtype), kind="ExternalInput").ap() for k, v in arrays.items()]
    out = nc.dram_tensor("tokens_out", [CHUNKS, P, TILES, P], F32, kind="ExternalOutput").ap()
    program(nc, *args, out)
    got = run_bass_kernel_spmd(nc, [arrays], core_ids=[0]).results[0]["tokens_out"]
    return got.reshape(CHUNKS, P, TILES, D).transpose(0, 2, 1, 3).reshape(BATCH, CTX, D)
```

```python
from contextlib import ExitStack

import concourse.bass as bass
from concourse import mybir

ALU = mybir.AluOpType
ACT = mybir.ActivationFunctionType
AX = mybir.AxisListType
F32 = mybir.dt.float32
F32R = mybir.dt.float32r
BF16 = mybir.dt.bfloat16

P = 128
BANK = 512
BATCH, CTX, D = 4, 1024, 128
TOK = BATCH * CTX
HEADS, DK = 16, 64
PAIRS = HEADS // 2
CHUNKS = TOK // BANK
TILES = BANK // P
HID = 512
EPS = 1e-5

WQ, WK, WV = 0, P, 2 * P
WBQ, WBK, WBV = 3 * P, 3 * P + 1, 3 * P + 2
WCOLS = 4 * P + 2


def attention(nc, xT, wpk, ident, masks, pick, ot_d, following):
    ITERS = BATCH * PAIRS
    NT = CTX // P
    UNITS = 4
    JOBS = UNITS + 2
    EXPS = 4 + NT
    ADDS = EXPS - 2
    SCORES = EXPS + 2
    MAXES = 8 + 16 + 2
    EARLY = 4
    ESLOTS = 4

    PAIR = """
        score 0 0 0, max 1 4, score 0 0 1
        score 0 1 0, max 1 5, max 1 6, max 1 7, score 0 1 1, max 1 8, max 1 9, unit 0, sum -1, max 1 10, max 1 11, pv 0 0, pv 0 1
        score 0 2 0, max 1 12, max 1 13, score 0 2 1, max 1 14, max 1 15, fold, invert -1 0
        score 0 3 0, score 0 3 1, turn 1, unit 1, pv 0 2, pv 0 3, drain 0
        score 1 0 0, score 1 0 1
        score 1 1 0, invert -1 1, scale -1, score 1 1 1, max 0 0, max 0 1, unit 2, sum 0
        score 1 2 0, max 0 2, max 0 3, score 1 2 1, pv 1 0
        score 1 3 0, score 1 3 1
        score 1 4 0, max 0 4, max 0 5, unit 3, score 1 4 1
        score 1 5 0, max 0 6, max 0 7, pv 1 1, pv 1 2, invert 0 0, pv 1 3, values 0, turn 0, max 1 0, pv 1 4, score 1 5 1
        score 1 6 0, score 1 6 1, values 1, pv 1 5, max 1 1, max 1 2
        score 1 7 0, score 1 7 1, pv 1 6, split, invert 0 1, scale 0, pv 1 7, drain 1, max 1 3
    """

    def read(text):
        words = (step.split() for step in text.replace("\n", ",").split(",") if step.strip())
        return [(kind, *map(int, at)) for kind, *at in words]

    def ahead(kind, *at):
        return kind in ("unit", "values", "split") or (kind, *at) == ("turn", 0) or (
            kind == "max" and (at[0] == 0 or at[1] < EARLY))

    def pair_steps(first, last):
        return [s for s in read(PAIR) if not (last and ahead(*s)) and not (first and s[1:2] == (-1,))]

    START = read("""
        unit 0, unit 1, max 0 0, max 0 1, unit 2, max 0 2, max 0 3, unit 3, max 0 4, max 0 5
        values 0, max 0 6, max 0 7, turn 0, values 1, max 1 0, max 1 1, max 1 2, max 1 3
    """) + [("stage", b) for b in range(1, BATCH)]
    END = read("sum -1, invert -1 0, invert -1 1, scale -1")

    def first_lo(c, j):
        return max(0, j - 4) * P if c else 0

    def exp_no(g, c, j):
        return EXPS * g + 4 * c + j

    def adds_with(g, c, j):
        return ADDS * g + 3 * c + max(j, 1)

    SCORE_ORDER = [(0, 0), (0, 1), "prev", (0, 2), (0, 3), (1, 0), (1, 1), "own"] + [(1, j) for j in range(2, NT)]

    def score_turn(g, what):
        pos = SCORE_ORDER.index(what)
        if isinstance(g, int) and g == ITERS:
            return SCORES * g - 1
        return pos if isinstance(g, int) and g == 0 and pos < 2 else SCORES * g + pos - 1

    def score_slot(g, what):
        pos = SCORE_ORDER.index(what)
        return (pos if isinstance(g, int) and g == 0 and pos < 2 else pos - 1) % 2

    assert SCORES % 2 == 0 and MAXES % 2 == 0 and EXPS % ESLOTS == 0

    def max_pos(kind, c, n=0):
        late = 16 - EARLY
        if kind == "turn":
            return late if c else late + 1 + 8
        if c == 0:
            return late + 1 + n
        return n - EARLY if n >= EARLY else late + 2 + 8 + n

    def max_turn(g, kind, c, n=0):
        return 8 + 1 + EARLY + MAXES * g + max_pos(kind, c, n)

    def turn_slot(c, n=None):
        return max_turn(0, "turn" if n is None else "max", c, n or 0) % 2

    def target(g, kind, c, n=0):
        return g if c and (kind == "turn" or n >= EARLY) else g + 1

    def sum_no(g, c):
        return 2 * g + c

    def unit(n):
        return n // 2, n % 2 == 1

    with ExitStack() as ctx:
        def sb(name, shape, dt):
            return ctx.enter_context(nc.sbuf_tensor(name, shape, dt))

        def sem(name):
            return ctx.enter_context(nc.semaphore(name))

        xh = sb("a_xh", [P, TOK], F32R)
        xl = sb("a_xl", [P, TOK], F32R)
        xb = sb("a_xb", [P, 2, CTX], F32)
        w = sb("a_w", [P, 2, WCOLS], F32)
        wh = sb("a_wh", [P, 2, 256], F32R)
        wl = sb("a_wl", [P, 2, 256], F32R)
        qa = sb("a_qa", [P, 2, 2, CTX], F32R)
        ka = sb("a_ka", [P, 2, 2, CTX], F32R)
        qb = sb("a_qb", [P, 2, 2, CTX], F32R)
        kb = sb("a_kb", [P, 2, 2, CTX], F32R)
        v = sb("a_v", [P, 2, NT, P], F32)
        e = sb("a_e", [P, ESLOTS, 2, BANK], F32)
        acc = sb("a_acc", [P, 2, 2, BANK], F32)
        rs = sb("a_rs", [P, 2, BANK], F32)
        ou = sb("a_ou", [P, 2, BANK], F32)
        ots = sb("a_ots", [P, 2, BANK], F32)
        part = sb("a_part", [P, 8, 2], F32)
        nmc = sb("a_nmc", [P, 2, P], F32)
        ones = sb("a_ones", [P, DK], F32)
        pk = sb("a_pick", [P, 8], F32)
        col = sb("a_col", [P, 1], F32)
        idf = sb("a_idf", [P, P], F32)
        mkf = sb("a_mkf", [P, 2, P], F32)
        idb = sb("a_idb", [P, P], BF16)
        mkb = sb("a_mkb", [P, 2, P], BF16)

        ps = ctx.enter_context(nc.psum_tensor("a_ps", [P, 2, 2, BANK], F32))
        pm = ctx.enter_context(nc.psum_tensor("a_pm", [P, 2, BANK], F32))
        po = ctx.enter_context(nc.psum_tensor("a_po", [P, BANK], F32))
        pj = ctx.enter_context(nc.psum_tensor("a_pj", [P, BANK], F32))

        held = sem("a_held")
        const_in = sem("a_const_in")
        const_dve = sem("a_const_dve")
        const_pool = sem("a_const_pool")
        xin = [sem(f"a_xin{b}") for b in range(BATCH)]
        x_hi = sem("a_x_hi")
        x_lo = sem("a_x_lo")
        w_in = [sem(f"a_w_in{i}") for i in range(2)]
        xb_in = [sem(f"a_xb_in{i}") for i in range(2)]
        w_scaled = sem("a_w_scaled")
        w_split = sem("a_w_split")
        pj_done = sem("a_pj_done")
        pj_hi = sem("a_pj_hi")
        pj_free = sem("a_pj_free")
        mx_done = sem("a_mx_done")
        mx_free = sem("a_mx_free")
        folded = sem("a_folded")
        s_done = sem("a_s_done")
        s_free = sem("a_s_free")
        add_done = sem("a_add_done")
        pv_done = sem("a_pv_done")
        po_free = sem("a_po_free")
        inverted = sem("a_inverted")
        scaled = sem("a_scaled")
        o_out = [sem(f"a_o_out{i}") for i in range(2)]
        sent = sem("a_sent")

        CONSTS = 9
        block = ctx.enter_context(nc.Block())

        def pairs(engine, steps):
            steps(-1, 1, START)
            steps(0, 0, pair_steps(True, False))
            with engine.Fori(0, (ITERS - 2) // 2) as i:
                for k in (1, 2):
                    steps(2 * i + k, k % 2, pair_steps(False, False))
            steps(ITERS - 1, 1, pair_steps(False, True))
            steps(ITERS, 0, END)

        @block.sync
        def _(sp):
            sp.dma_start(e[:, 0], xT[:, 0:CTX]).then_inc(xin[0], 16)
            sp.dma_start(w[:, 0, :], wpk[0]).then_inc(w_in[0], 16)
            for dst, src in ((idf[:, :], ident), (mkf[:, :, :], masks), (pk[:, :], pick)):
                sp.dma_start(dst, src).then_inc(const_in, 16)
            sp.dma_start(xb[:, 0, :], xT[:, 0:CTX]).then_inc(xb_in[0], 16)
            sp.dma_start(w[:, 1, :], wpk[1]).then_inc(w_in[1], 16)
            sp.dma_start(xb[:, 1, :], xT[:, 0:CTX]).then_inc(xb_in[1], 16)
            for b in range(1, BATCH):
                sp.dma_start(e[:, b], xT[:, b * CTX:(b + 1) * CTX]).then_inc(xin[b], 16)

            def load(g, slot):
                sp.wait_ge(pj_free, JOBS * (g + 1) + 1)
                at = g + 2
                sp.dma_start(w[:, slot, :], wpk[at % PAIRS]).then_inc(w_in[slot], 16)
                sp.dma_start(xb[:, slot, :], xT[:, bass.ds(((at // PAIRS) % BATCH) * CTX, CTX)]).then_inc(xb_in[slot], 16)

            def send(g, c):
                sp.wait_ge(scaled, sum_no(g, c) + 3)
                sp.dma_start(ot_d[2 * (g // PAIRS) + c, :, g % PAIRS, :], ots[:, c, :]).then_inc(o_out[c], 16)
                sp.wait_ge(o_out[c], 16 * (g + 1))
                sp.sem_inc(sent, 1)

            sp.sem_inc(sent, 2)
            load(0, 0)
            send(0, 0)
            following.weights(sp)
            with sp.Fori(0, (ITERS - 2) // 2) as i:
                for k in (1, 2):
                    g = 2 * i + k
                    load(g, k % 2)
                    send(g - 1, 1)
                    send(g, 0)
            if BATCH > 1:
                following.outputs(sp)
            send(ITERS - 2, 1)
            send(ITERS - 1, 0)
            send(ITERS - 1, 1)
            if BATCH == 1:
                following.outputs(sp)
            for c in range(2):
                sp.wait_ge(w_in[c], 16 * (ITERS // 2 + 1 - c))
                sp.wait_ge(xb_in[c], 16 * (ITERS // 2 + 1 - c))

        @block.gpsimd
        def _(pool):
            def split_weights(g, slot):
                pool.wait_ge(w_in[slot], 8 * (g - slot) + 16)
                pool.sem_inc(held, 1)
                pool.tensor_scalar(w[:, slot, WQ:WQ + P], w[:, slot, WQ:WQ + P], 0.125, 1.0, ALU.mult,
                                   ALU.mult).then_inc(w_scaled, 1)
                pool.tensor_scalar(w[:, slot, WBQ:WBQ + 1], w[:, slot, WBQ:WBQ + 1], 0.125, 1.0, ALU.mult,
                                   ALU.mult).then_inc(w_scaled, 1)
                pool.wait_ge(w_scaled, 3 * g + 2)
                pool.sem_inc(held, 1)
                pool.tensor_scalar(wh[:, slot, :], w[:, slot, 0:2 * P], 1.0, 1.0, ALU.mult, ALU.mult).then_inc(w_scaled, 1)
                pool.wait_ge(w_scaled, 3 * g + 3)
                pool.tensor_tensor(wl[:, slot, :], w[:, slot, 0:2 * P], wh[:, slot, :].bitcast(F32),
                                   ALU.subtract).then_inc(w_split, 1)

            def add(g, c, j):
                lo = first_lo(c, j)
                slot = exp_no(0, c, j) % ESLOTS
                pool.wait_ge(s_free, score_turn(g, (c, j)) + 1 + 2)
                if j == 1:
                    if not isinstance(g, int) or g > 0:
                        pool.wait_ge(s_done, (score_turn(g, "prev") if c else score_turn(g - 1, "own")) + 1)
                else:
                    pool.wait_ge(add_done, adds_with(g, c, j) - 1 + ESLOTS)
                before = e[:, (slot - 1) % ESLOTS] if j == 1 else acc[:, c]
                pool.tensor_tensor(acc[:, c, :, lo:BANK], before[:, :, lo:BANK], e[:, slot, :, lo:BANK],
                                   ALU.add).then_inc(add_done, 1)

            def scale(g, c):
                n = sum_no(g, c)
                pool.wait_ge(inverted, 2 * (n + 1))
                pool.wait_ge(po_free, n + 2)
                pool.wait_ge(sent, n + 1)
                pool.tensor_tensor(ots[:, c % 2, :], ou[:, c % 2, :], rs[:, c % 2, :], ALU.mult).then_inc(scaled, 1)

            def steps(g, slot, items):
                for kind, *at in items:
                    if kind == "score" and at[2] == 1 and at[1] > 0:
                        add(g, at[0], at[1])
                    elif kind == "scale":
                        scale(g, at[0])
                    elif kind == "split":
                        split_weights(g + 2, slot)

            pool.sem_inc(add_done, ESLOTS)
            pool.sem_inc(scaled, 2)
            pool.memset(ones[:, :], 1.0).then_inc(const_pool, 1)
            split_weights(0, 0)
            split_weights(1, 1)
            pairs(pool, steps)

        @block.scalar
        def _(act):
            def tokens_hi(b):
                act.wait_ge(xin[b], 16)
                act.activation(xh[:, b * CTX:(b + 1) * CTX], e[:, b].rearrange("p h q -> p (h q)"),
                               ACT.Identity).then_inc(x_hi, 1)
                if b == BATCH - 1:
                    act.wait_ge(x_lo, BATCH)

            def project_hi(g, slot, n):
                half, query = unit(n)
                cols = slice(half * BANK, (half + 1) * BANK)
                at = WBQ if query else WBK
                act.wait_ge(pj_done, JOBS * g + n + 1)
                for h in range(2):
                    own = slice(h * DK, (h + 1) * DK)
                    other = slice((1 - h) * DK, (2 - h) * DK)
                    if query:
                        dsts = [qb[0:DK, slot, h, cols], qa[0:DK, slot, h, cols]] + [qa[own, slot, h, cols]] * h
                    else:
                        dsts = [ka[other, slot, h, cols], ka[own, slot, h, cols]]
                    for dst in dsts:
                        m = act.activation(dst, pj[own, :], ACT.Identity, bias=w[own, slot, at:at + 1])
                    m.then_inc(pj_hi, 1)

            def exponentials(g, c, j):
                lo = first_lo(c, j)
                n = exp_no(g, c, j)
                slot = exp_no(0, c, j) % ESLOTS
                act.wait_ge(pv_done, n + 1)
                if c == 0:
                    act.wait_ge(add_done, adds_with(g - 1, 1, 4 + j) + ESLOTS)
                elif j < 4:
                    act.wait_ge(add_done, adds_with(g, 0, j) + ESLOTS)
                else:
                    act.wait_ge(add_done, adds_with(g, 1, j - 4) + ESLOTS)
                act.wait_ge(s_done, score_turn(g, (c, j)) + 1)
                s = score_slot(g, (c, j))
                act.activation(e[:, slot, :, lo:BANK], ps[:, s, :, lo:BANK], ACT.Exp).then_inc(s_free, 1)

            def copy_sums(g, c):
                act.wait_ge(scaled, sum_no(g, c) + 1)
                act.wait_ge(s_done, score_turn(g, "prev" if c < 0 else "own") + 1)
                act.activation(rs[:, c % 2, :], ps[:, score_slot(g, "prev" if c < 0 else "own"), 0, :],
                               ACT.Copy).then_inc(s_free, 1)

            def drain(g, c):
                act.wait_ge(scaled, sum_no(g, c) + 1)
                act.wait_ge(pv_done, exp_no(g, c, NT - 1 if c else 3) + 1 + ESLOTS)
                act.activation(ou[:, c, :], po[:, :], ACT.Copy).then_inc(po_free, 1)

            def steps(g, slot, items):
                for kind, *at in items:
                    if kind == "score" and at[2] == 1:
                        exponentials(g, at[0], at[1])
                    elif kind == "stage":
                        tokens_hi(at[0])
                    elif kind == "unit":
                        project_hi(g + 1, 1 - slot, at[0])
                    elif kind == "sum":
                        copy_sums(g, at[0])
                    elif kind == "drain":
                        drain(g, at[0])

            act.sem_inc(s_free, 2)
            act.sem_inc(po_free, 1)
            tokens_hi(0)
            pairs(act, steps)

        @block.tensor
        def _(pe):
            def project(g, slot, n):
                half, query = unit(n)
                cols = slice(WQ, WQ + P) if query else slice(WK, WK + P)
                if n == 0:
                    pe.wait_ge(w_split, g + 1)
                pe.wait_ge(pj_free, JOBS * g + n + 1)
                at = (g // PAIRS) * CTX + half * BANK
                hi, lo = (x[:, bass.ds(at, BANK)] for x in (xh, xl))
                pe.matmul(pj[:, :], wh[:, slot, cols], hi, start=True, stop=False)
                pe.matmul(pj[:, :], wh[:, slot, cols], lo, start=False, stop=False)
                pe.matmul(pj[:, :], wl[:, slot, cols], hi, start=False, stop=True).then_inc(pj_done, 1)

            def values(g, slot, half):
                pe.wait_ge(xb_in[slot], 8 * (g - slot) + 16)
                pe.wait_ge(pj_free, JOBS * g + UNITS + half + 1)
                for k in range(4):
                    t = 4 * half + k
                    m = pe.matmul(pj[:, k * P:(k + 1) * P], xb[:, slot, t * P:(t + 1) * P],
                                  w[:, slot, WV:WV + P], start=True, stop=True)
                m.then_inc(pj_done, 1)

            def score_max(g, slot, turn, c, n):
                h, t, k = (n % 2, n // 2, 0) if c == 0 else ((n // 2) % 2, n // 4, n % 2)
                if n == 0:
                    pe.wait_ge(pj_free, JOBS * g + (UNITS if c else 2) + 1)
                pe.wait_ge(mx_free, turn + 1)
                width = P * (t + 1) if k else BANK
                q = qa[:, slot, h, c * BANK + t * P:c * BANK + (t + 1) * P]
                m = pe.matmul(pm[:, turn_slot(c, n), 0:width], q, ka[:, slot, h, k * BANK:k * BANK + width],
                              start=True, stop=k == 0)
                if k:
                    m = pe.matmul(pm[:, turn_slot(c, n), width - P:width], idb[:, :], mkb[:, 0, :],
                                  start=False, stop=True)
                m.then_inc(mx_done, 1)

            def turn_max(g, turn, c):
                pe.wait_ge(mx_free, turn + 2)
                if c:
                    pe.wait_ge(folded, g + 1)
                pe.transpose(pm[:, turn_slot(c), 0:P], nmc[:, c, :], idf[:, :]).then_inc(mx_done, 1)

            def score(g, slot, c, j, h):
                lo = first_lo(c, j)
                at = score_slot(g, (c, j))
                if h == 0:
                    pe.wait_ge(s_free, score_turn(g, (c, j)) + 1)
                    if j == 0:
                        pe.wait_ge(mx_free, max_turn(g if c else g - 1, "turn", c) + 1 + 2)
                dst = ps[:, at, h, lo:BANK]
                keys = slice(j * P, (j + 1) * P)
                queries = slice(c * BANK + lo, (c + 1) * BANK)
                diag = c == 1 and j >= 4
                pe.matmul(dst, ka[:, slot, h, keys], qa[:, slot, h, queries], start=True, stop=False)
                m = pe.matmul(dst, kb[:, slot, h, keys], qb[:, slot, h, queries], start=False, stop=not diag)
                if diag:
                    m = pe.matmul(ps[:, at, h, lo:lo + P], idb[:, :], mkb[:, 1, :], start=False, stop=True)
                if h == 1:
                    m.then_inc(s_done, 1)

            def weigh(g, slot, c, j):
                lo = first_lo(c, j)
                pe.wait_ge(s_free, score_turn(g, (c, j)) + 1 + 2)
                if j == 0:
                    pe.wait_ge(po_free, sum_no(g, c) + 1)
                    if c == 0:
                        pe.wait_ge(pj_free, JOBS * (g + 1) + 1)
                for h in range(2):
                    m = pe.matmul(po[h * DK:(h + 1) * DK, lo:BANK], v[:, slot, j, h * DK:(h + 1) * DK],
                                  e[:, exp_no(0, c, j) % ESLOTS, h, lo:BANK], start=(j == 0),
                                  stop=(j == (NT - 1 if c else 3)))
                m.then_inc(pv_done, 1)

            def sums(g, c):
                what = "prev" if c < 0 else "own"
                pe.wait_ge(s_free, score_turn(g, what) + 1)
                pe.wait_ge(add_done, (ADDS * g if c < 0 else adds_with(g, 0, 3)) + ESLOTS)
                for h in range(2):
                    m = pe.matmul(ps[h * DK:(h + 1) * DK, score_slot(g, what), 0, :], ones[:, :],
                                  acc[:, c % 2, h, :], start=True, stop=True)
                m.then_inc(s_done, 1)

            def steps(g, slot, items):
                for kind, *at in items:
                    if kind == "stage":
                        pe.wait_ge(x_lo, at[0] + 1)
                    elif kind == "unit":
                        project(g + 1, 1 - slot, at[0])
                    elif kind == "values":
                        values(g + 1, 1 - slot, at[0])
                    elif kind == "max":
                        own = target(0, "max", *at) == 0
                        score_max(g if own else g + 1, slot if own else 1 - slot, max_turn(g, "max", *at), *at)
                    elif kind == "turn":
                        turn_max(g, max_turn(g, "turn", at[0]), at[0])
                    elif kind == "score":
                        score(g, slot, *at)
                    elif kind == "pv":
                        weigh(g, slot, *at)
                    elif kind == "sum":
                        sums(g, at[0])

            pe.sem_inc(pv_done, ESLOTS)
            pe.wait_ge(x_lo, 1)
            pe.wait_ge(const_dve, CONSTS)
            pe.wait_ge(const_pool, 1)
            pairs(pe, steps)

        @block.vector
        def _(dve):
            def tokens_lo(b):
                dve.wait_ge(x_hi, b + 1)
                cols = slice(b * CTX, (b + 1) * CTX)
                dve.tensor_tensor(xl[:, cols], e[:, b].rearrange("p h q -> p (h q)"), xh[:, cols].bitcast(F32),
                                  ALU.subtract).then_inc(x_lo, 1)

            def project_lo(g, slot, n):
                half, query = unit(n)
                cols = slice(half * BANK, (half + 1) * BANK)
                at = WBQ if query else WBK
                for h in range(2):
                    own = slice(h * DK, (h + 1) * DK)
                    dst = qa[DK:P, slot, h, cols] if query else kb[0:DK, slot, h, cols]
                    hi = (qa if query else ka)[own, slot, h, cols].bitcast(F32)
                    dve.wait_ge(pj_hi, 2 * (UNITS * g + n) + h + 1)
                    m = dve.scalar_tensor_tensor(dst, pj[own, :], w[own, slot, at:at + 1], hi, ALU.add, ALU.subtract)
                m.then_inc(pj_free, 1)

            def values(g, slot, half):
                dve.wait_ge(pj_done, JOBS * g + UNITS + half + 1)
                bias = w[:, slot, WBV:WBV + P].unsqueeze(1).to_broadcast([P, 4, P])
                dve.tensor_tensor(v[:, slot, 4 * half:4 * half + 4, :], pj[:, :].rearrange("p (t d) -> p t d", t=4),
                                  bias, ALU.add).then_inc(pj_free, 1)

            def maximum(turn, c, n):
                h, t, k = (n % 2, n // 2, 0) if c == 0 else ((n // 2) % 2, n // 4, n % 2)
                width = P * (t + 1) if k else BANK
                at = 4 * h + t
                dst = part[:, at, k:k + 1] if c else nmc[:, 0, DK + at:DK + at + 1]
                dve.wait_ge(mx_done, turn + 1)
                dve.tensor_reduce(dst, pm[:, turn_slot(c, n), 0:width], AX.X, ALU.max, negate=True).then_inc(mx_free, 1)

            def fold(g):
                dve.wait_ge(mx_free, max_turn(g, "turn", 1) + 2)
                dve.tensor_reduce(nmc[:, 1, DK:DK + 8], part[:, :, :], AX.X, ALU.min).then_inc(folded, 1)

            def place(slot, turn, c):
                dve.wait_ge(mx_done, turn + 1)
                src = pm[DK:P, turn_slot(c), 0:P].unsqueeze(1).to_broadcast([DK, 8, P])
                dst = qb[DK:P, slot, :, c * BANK:(c + 1) * BANK].rearrange("p h (t q) -> p h t q", t=4)
                sel = pk[DK:P, :].unsqueeze(2).to_broadcast([DK, 8, P])
                split = "p (h t) q -> p h t q"
                dve.tensor_tensor(dst, src.rearrange(split, h=2), sel.rearrange(split, h=2), ALU.mult).then_inc(mx_free, 1)

            def invert(g, c, k):
                if k == 0:
                    dve.wait_ge(s_free, score_turn(g, "prev" if c < 0 else "own") + 1 + 2)
                piece = rs[:, c % 2, k * BANK // 2:(k + 1) * BANK // 2]
                dve.reciprocal(piece, piece).then_inc(inverted, 1)

            def steps(g, slot, items):
                for kind, *at in items:
                    if kind == "stage":
                        tokens_lo(at[0])
                    elif kind == "unit":
                        project_lo(g + 1, 1 - slot, at[0])
                    elif kind == "values":
                        values(g + 1, 1 - slot, at[0])
                    elif kind == "max":
                        maximum(max_turn(g, "max", *at), *at)
                    elif kind == "fold":
                        fold(g)
                    elif kind == "turn":
                        place(slot if at[0] else 1 - slot, max_turn(g, "turn", at[0]), at[0])
                    elif kind == "invert":
                        invert(g, *at)

            dve.sem_inc(pj_free, 1)
            dve.sem_inc(mx_free, 2)
            dve.memset(nmc[:, :, :], 0.0).then_inc(const_dve, 1)
            dve.memset(acc[:, 0, :, :], 0.0).then_inc(const_dve, 1)
            dve.wait_ge(const_in, 48)
            dve.tensor_copy(idb[:, :], idf[:, :]).then_inc(const_dve, 1)
            dve.tensor_copy(mkb[:, :, :], mkf[:, :, :]).then_inc(const_dve, 1)
            dve.tensor_reduce(col[:, :], pk[:, :], AX.X, ALU.add).then_inc(const_dve, 1)
            dve.wait_ge(const_dve, 5)
            for slot in range(2):
                for h in range(2):
                    dve.tensor_scalar(kb[DK:P, slot, h, :], acc[DK:P, 0, :, :].rearrange("p h q -> p (h q)"),
                                      col[DK:P, :], None, ALU.add).then_inc(const_dve, 1)
            tokens_lo(0)
            pairs(dve, steps)


class GatedInputs:

    def __init__(self, nc, ctx, ot_d, x_tok, wo, w_in, w_hid, w_out):
        def sb(name, columns):
            return ctx.enter_context(nc.sbuf_tensor(name, [P, *columns], F32))

        self.ot = sb("f_ot", [PAIRS, BANK])
        self.xt = sb("f_xt", [TILES, P])
        self.wo = sb("f_wo", [PAIRS, P])
        self.sources = [w_in[0], w_in[1], w_hid[0], w_hid[1], w_out]
        self.raw = [sb(f"f_raw{k}", [source.shape[1]]) for k, source in enumerate(self.sources)]
        self.sources += [wo, x_tok[0], ot_d[0]]
        self.ot_in, self.xt_in, self.wo_in, *self.raw_in = (
            ctx.enter_context(nc.semaphore(f"f_{name}_in")) for name in ("ot", "xt", "wo", "raw0", "raw1", "raw2", "raw3", "raw4"))

    def weights(self, sp):
        *sources, wo, x_tok, _ = self.sources
        sp.dma_start(self.wo[:, :, :], wo).then_inc(self.wo_in, 16)
        sp.dma_start(self.xt[:, :, :], x_tok).then_inc(self.xt_in, 16)
        for raw, source, raw_in in zip(self.raw, sources, self.raw_in):
            sp.dma_start(raw[:, :], source).then_inc(raw_in, 16)

    def outputs(self, sp):
        sp.dma_start(self.ot[:, :, :], self.sources[-1]).then_inc(self.ot_in, 16)


def gated_ffn(nc, given, ot_d, x_tok, scales, s3, ident, y_d):
    KC = HID // P
    UN = 4 * KC
    LN1, LN2 = 5, 6
    LINKS = LN1 + LN2
    LATE = 3 * KC - 2

    with ExitStack() as ctx:
        def sb(name, shape, dt):
            return ctx.enter_context(nc.sbuf_tensor(name, shape, dt))

        def sem(name):
            return ctx.enter_context(nc.semaphore(name))

        ot, xt, wo_s = given.ot, given.xt, given.wo
        w12h = sb("f_w12h", [P, 2, HID], F32R)
        w12l = sb("f_w12l", [P, 2, HID], F32R)
        hh = sb("f_hh", [P, 2, KC, HID], F32R)
        hl = sb("f_hl", [P, 2, KC, HID], F32R)
        w3h = sb("f_w3h", [P, KC, P], F32R)
        w3l = sb("f_w3l", [P, KC, P], F32R)
        sc = sb("f_sc", [P, 4, KC], F32)
        s3b = sb("f_s3b", [P, P], F32)
        idf = sb("f_idf", [P, P], F32)
        half = sb("f_half", [P, TILES], F32)
        r1 = sb("f_r1", [P, TILES, P], F32)
        r2 = sb("f_r2", [P, TILES, P], F32)
        x1n = sb("f_x1n", [P, TILES, P], F32)
        x1 = sb("f_x1", [P, TILES, P], F32)
        x1h = sb("f_x1h", [P, BANK], F32R)
        x1l = sb("f_x1l", [P, BANK], F32R)
        gate = sb("f_gate", [P, 2, BANK], F32)
        act_f = sb("f_act", [P, 4, BANK], F32)
        ah = sb("f_ah", [P, 3, KC, BANK], F32R)
        al = sb("f_al", [P, 3, KC, BANK], F32R)
        y2 = sb("f_y2", [P, TILES, P], F32)
        st = sb("f_st", [P, TILES, 6], F32)
        mv = sb("f_mv", [P, TILES, 2], F32)
        ve = sb("f_ve", [P, TILES], F32)
        rstd = sb("f_rstd", [P, TILES], F32)

        pu = ctx.enter_context(nc.psum_tensor("f_pu", [P, 4, BANK], F32))
        py = ctx.enter_context(nc.psum_tensor("f_py", [P, TILES, P], F32))
        pz = ctx.enter_context(nc.psum_tensor("f_pz", [P, TILES, P], F32))

        held = sem("f_held")
        c_in = sem("f_c_in")
        raw_hi = sem("f_raw_hi")
        raw_lo = sem("f_raw_lo")
        half_ok = sem("f_half_ok")
        wo_done = sem("f_wo_done")
        chain = sem("f_chain")
        pow_done = sem("f_pow_done")
        tr_done = sem("f_tr_done")
        tr_hi = sem("f_tr_hi")
        tr_lo = sem("f_tr_lo")
        u_done = sem("f_u_done")
        gate_ok = sem("f_gate_ok")
        prod_ok = sem("f_prod_ok")
        gelu_ok = sem("f_gelu_ok")
        hi_ok = sem("f_hi_ok")
        lo_ok = sem("f_lo_ok")
        z_done = sem("f_z_done")
        x1_ok = sem("f_x1_ok")
        y_out = sem("f_y_out")

        WEIGHTS = [(w12h[:, 0, :], w12l[:, 0, :]), (w12h[:, 1, :], w12l[:, 1, :]), (hh[:, 0], hl[:, 0]),
                   (hh[:, 1], hl[:, 1]), (w3h[:, :, :], w3l[:, :, :])]

        def flat(ap):
            return ap if len(ap.shape) == 2 else ap.rearrange("p a b -> p (a b)")

        block = ctx.enter_context(nc.Block())

        @block.sync
        def _(sp):
            sp.dma_start(idf[:, :], ident).then_inc(c_in, 16)
            sp.dma_start(sc[:, :, :], scales).then_inc(c_in, 16)
            sp.dma_start(s3b[:, :], s3).then_inc(c_in, 16)
            sp.sem_inc(y_out, 16)
            sp.wait_ge(wo_done, 1)
            sp.dma_start(ot[:, :, :], ot_d[1]).then_inc(given.ot_in, 16)
            sp.wait_ge(chain, 1)
            sp.dma_start(xt[:, :, :], x_tok[1]).then_inc(given.xt_in, 16)
            with sp.Fori(0, CHUNKS - 2) as i:
                sp.wait_ge(wo_done, i + 2)
                sp.dma_start(ot[:, :, :], ot_d[i + 2]).then_inc(given.ot_in, 16)
                sp.wait_ge(chain, LINKS * i + LN1 + 1)
                sp.dma_start(xt[:, :, :], x_tok[i + 2]).then_inc(given.xt_in, 16)
                sp.wait_ge(chain, LINKS * i + LN1 + LINKS)
                sp.dma_start(y_d[i], y2[:, :, :]).then_inc(y_out, 16)
            for i in (CHUNKS - 2, CHUNKS - 1):
                sp.wait_ge(chain, LN1 + LINKS * (i + 1) - (LN1 if i == CHUNKS - 1 else 0))
                sp.dma_start(y_d[i], y2[:, :, :]).then_inc(y_out, 16)
            sp.wait_ge(y_out, 16 * (CHUNKS + 1))

        @block.gpsimd
        def _(pool):
            def power(at):
                pool.wait_ge(chain, at)
                pool.tensor_tensor(rstd[:, :], ve[:, :], half[:, :], ALU.pow).then_inc(pow_done, 1)

            def split(i, k):
                layer = k // KC
                if layer == 0:
                    pool.wait_ge(prod_ok, KC * i + k + 1)
                else:
                    pool.wait_ge(gelu_ok, 2 * KC * i + k - KC + 1)
                pool.sem_inc(held, 1)
                pool.tensor_scalar(ah[:, layer, k % KC, :], act_f[:, k % 4, :], 1.0, 1.0, ALU.mult,
                                   ALU.mult).then_inc(hi_ok, 1)

            def keep(at):
                pool.wait_ge(chain, at)
                pool.sem_inc(held, 1)
                pool.tensor_scalar(x1[:, :, :], x1n[:, :, :], 1.0, 1.0, ALU.mult, ALU.mult).then_inc(x1_ok, 1)

            def body(i, last):
                for k in range(KC, 2 * KC):
                    split(i, k)
                if not last:
                    power(LINKS * i + LN1 + 4)
                for k in range(2 * KC, 3 * KC):
                    split(i, k)
                if not last:
                    for k in range(KC):
                        split(i + 1, k)
                    keep(LINKS * i + 2 * LN1 + 2)
                power(LINKS * i + LN1 + (0 if last else LN1) + 5)

            pool.memset(half[:, :], -0.5).then_inc(half_ok, 1)
            pool.wait_ge(half_ok, 1)
            power(4)
            keep(LN1)
            for k in range(KC):
                split(0, k)
            with pool.Fori(0, CHUNKS - 1) as i:
                body(i, False)
            body(CHUNKS - 1, True)

        @block.scalar
        def _(act):
            def weights_hi(k):
                act.wait_ge(given.raw_in[k], 16)
                act.activation(flat(WEIGHTS[k][0]), given.raw[k][:, :], ACT.Copy).then_inc(raw_hi, 1)

            def tokens_hi(n):
                act.wait_ge(tr_done, n + 1)
                act.activation(x1h[:, :], py[:, :, :].rearrange("p t d -> p (t d)"), ACT.Copy).then_inc(tr_hi, 1)

            def gates(i):
                for m in range(KC):
                    act.wait_ge(u_done, UN * i + 2 * m + 1)
                    if m >= 2:
                        act.wait_ge(prod_ok, KC * i + m - 1)
                    act.activation(gate[:, m % 2, :], pu[:, (2 * m) % 4, :], ACT.Silu,
                                   scale=sc[:, 0, m:m + 1]).then_inc(gate_ok, 1)

            def body(i, last):
                for k in range(KC, 3 * KC):
                    act.wait_ge(u_done, UN * i + KC + k + 1)
                    act.wait_ge(lo_ok, 3 * KC * i + k - 3)
                    act.activation(act_f[:, k % 4, :], pu[:, (KC + k) % 4, :], ACT.Gelu,
                                   scale=sc[:, 1 + k // KC, k % KC:k % KC + 1]).then_inc(gelu_ok, 1)
                    if k == LATE and not last:
                        tokens_hi(i + 1)
                if not last:
                    gates(i + 1)

            for k in range(3):
                weights_hi(k)
            tokens_hi(0)
            for k in (3, 4):
                weights_hi(k)
            act.wait_ge(c_in, 48)
            gates(0)
            with act.Fori(0, CHUNKS - 1) as i:
                body(i, False)
            body(CHUNKS - 1, True)

        @block.tensor
        def _(pe):
            def project(n):
                pe.wait_ge(given.ot_in, 16 * (n + 1))
                if not isinstance(n, int):
                    pe.wait_ge(tr_lo, n)
                for t in range(TILES):
                    for r in range(PAIRS):
                        m = pe.matmul(py[:, t, :], ot[:, r, t * P:(t + 1) * P], wo_s[:, r, :],
                                      start=(r == 0), stop=(r == PAIRS - 1))
                m.then_inc(wo_done, 1)

            def transposes(at):
                pe.wait_ge(chain, at)
                for t in range(TILES):
                    m = pe.transpose(py[:, t, :], x1n[:, t, :], idf[:, :])
                m.then_inc(tr_done, 1)

            def unit(u, wh, wl, xh, xl):
                dst = pu[:, u % 4, :]
                n = len(wh)
                for k in range(n):
                    pe.matmul(dst, wh[k], xh[k], start=(k == 0), stop=False)
                    pe.matmul(dst, wh[k], xl[k], start=False, stop=False)
                    m = pe.matmul(dst, wl[k], xh[k], start=False, stop=(k == n - 1))
                m.then_inc(u_done, 1)

            def gated(i, first):
                pe.wait_ge(tr_lo, i + 1)
                for u in range(2 * KC):
                    m, second = u // 2, u % 2
                    if u >= 4:
                        if second:
                            pe.wait_ge(prod_ok, KC * i + m - 1)
                        else:
                            pe.wait_ge(gate_ok, KC * i + m - 1)
                    elif not first:
                        pe.wait_ge(gelu_ok, 2 * KC * (i - 1) + KC + u + 1)
                    cols = slice(m * P, (m + 1) * P)
                    unit(u, [w12h[:, second, cols]], [w12l[:, second, cols]], [x1h[:, :]], [x1l[:, :]])

            def body(i, last):
                for k in range(KC, 3 * KC):
                    layer, m = k // KC, k % KC
                    if layer == 1:
                        pe.wait_ge(prod_ok, KC * i + 2 + m // 2 + 1)
                        pe.wait_ge(lo_ok, 3 * KC * i + KC)
                    else:
                        pe.wait_ge(gelu_ok, 2 * KC * i + m + 1)
                        pe.wait_ge(lo_ok, 3 * KC * i + 2 * KC)
                    cols = slice(m * P, (m + 1) * P)
                    unit(KC + k, [hh[:, layer - 1, j, cols] for j in range(KC)],
                         [hl[:, layer - 1, j, cols] for j in range(KC)],
                         [ah[:, layer - 1, j, :] for j in range(KC)], [al[:, layer - 1, j, :] for j in range(KC)])
                    if k == 2 * KC - 1 and not last:
                        project(i + 1)
                    if k == LATE and not last:
                        transposes(LINKS * i + 2 * LN1)
                if not last:
                    gated(i + 1, False)
                pe.wait_ge(lo_ok, 3 * KC * (i + 1))
                if last:
                    pe.wait_ge(chain, LINKS * i)
                for t in range(TILES):
                    cols = slice(t * P, (t + 1) * P)
                    for j in range(KC):
                        pe.matmul(pz[:, t, :], ah[:, 2, j, cols], w3h[:, j, :], start=(j == 0), stop=False)
                        pe.matmul(pz[:, t, :], al[:, 2, j, cols], w3h[:, j, :], start=False, stop=False)
                        m = pe.matmul(pz[:, t, :], ah[:, 2, j, cols], w3l[:, j, :], start=False, stop=(j == KC - 1))
                m.then_inc(z_done, 1)

            pe.wait_ge(given.wo_in, 16)
            project(0)
            pe.wait_ge(c_in, 48)
            transposes(LN1)
            pe.wait_ge(raw_lo, 2)
            gated(0, True)
            pe.wait_ge(raw_lo, len(WEIGHTS))
            with pe.Fori(0, CHUNKS - 1) as i:
                body(i, False)
            body(CHUNKS - 1, True)

        @block.vector
        def _(dve):
            def weights_lo(k):
                hi, lo = WEIGHTS[k]
                dve.wait_ge(raw_hi, k + 1)
                dve.tensor_tensor(flat(lo), given.raw[k][:, :], flat(hi).bitcast(F32), ALU.subtract).then_inc(raw_lo, 1)

            def norm(r, dst, n, at):
                dve.wait_ge(chain, at)
                for t in range(TILES):
                    m = dve.bn_stats(st[:, t, :], r[:, t, :])
                m.then_inc(chain, 1)
                dve.wait_ge(chain, at + 1)
                dve.sem_inc(held, 1)
                for t in range(TILES):
                    m = dve.bn_aggr(mv[:, t, :], st[:, t, :])
                m.then_inc(chain, 1)
                dve.wait_ge(chain, at + 2)
                dve.tensor_scalar(ve[:, :], mv[:, :, 1], EPS, None, ALU.add).then_inc(chain, 1)
                dve.wait_ge(pow_done, n + 1)
                for t in range(TILES):
                    m = dve.tensor_scalar(dst[:, t, :], r[:, t, :], mv[:, t, 0:1], rstd[:, t:t + 1],
                                          ALU.subtract, ALU.mult)
                m.then_inc(chain, 1)

            def norm1(i, n, at):
                dve.wait_ge(wo_done, i + 1)
                dve.wait_ge(given.xt_in, 16 * (i + 1))
                dve.tensor_tensor(r1[:, :, :], py[:, :, :], xt[:, :, :], ALU.add).then_inc(chain, 1)
                norm(r1, x1n, n, at + 1)

            def tokens_lo(n):
                dve.wait_ge(tr_hi, n + 1)
                dve.tensor_tensor(x1l[:, :], py[:, :, :].rearrange("p t d -> p (t d)"), x1h[:, :].bitcast(F32),
                                  ALU.subtract).then_inc(tr_lo, 1)

            def split(i, k):
                dve.wait_ge(hi_ok, 3 * KC * i + k + 1)
                dve.tensor_tensor(al[:, k // KC, k % KC, :], act_f[:, k % 4, :],
                                  ah[:, k // KC, k % KC, :].bitcast(F32), ALU.subtract).then_inc(lo_ok, 1)

            def products(i, first):
                for m in range(KC):
                    dve.wait_ge(u_done, UN * i + 2 * m + 2)
                    dve.wait_ge(gate_ok, KC * i + m + 1)
                    if not first:
                        dve.wait_ge(lo_ok, 3 * KC * i - KC + m + 1)
                    dve.scalar_tensor_tensor(act_f[:, m % 4, :], pu[:, (2 * m + 1) % 4, :], sc[:, 1, m:m + 1],
                                             gate[:, m % 2, :], ALU.mult, ALU.mult).then_inc(prod_ok, 1)
                    if m:
                        split(i, m - 1)
                split(i, KC - 1)

            def body(i, last):
                at = LINKS * i + LN1
                for k in range(KC, 2 * KC):
                    split(i, k)
                if not last:
                    dve.wait_ge(x1_ok, i + 1)
                    norm1(i + 1, 2 * i + 1, at)
                    at = at + LN1
                for k in range(2 * KC, 3 * KC):
                    split(i, k)
                    if k == LATE and not last:
                        tokens_lo(i + 1)
                if not last:
                    products(i + 1, False)
                dve.wait_ge(z_done, i + 1)
                dve.tensor_tensor(r2[:, :, :], pz[:, :, :], s3b[:, :].unsqueeze(1).to_broadcast([P, TILES, P]),
                                  ALU.mult).then_inc(chain, 1)
                dve.wait_ge(chain, at + 1)
                dve.tensor_tensor(r2[:, :, :], r2[:, :, :], x1[:, :, :], ALU.add).then_inc(chain, 1)
                dve.wait_ge(y_out, 16 * (i + 1))
                norm(r2, y2, 2 * i + (1 if last else 2), at + 2)

            weights_lo(0)
            weights_lo(1)
            norm1(0, 0, 0)
            weights_lo(2)
            tokens_lo(0)
            weights_lo(3)
            dve.wait_ge(c_in, 48)
            products(0, True)
            weights_lo(4)
            with dve.Fori(0, CHUNKS - 1) as i:
                body(i, False)
            body(CHUNKS - 1, True)


class TernaryInputs:

    def __init__(self, nc, ctx, w1, w2, b1, b2, ident):
        def sb(name, columns):
            return ctx.enter_context(nc.sbuf_tensor(name, [P, *columns], F32))

        self.wr = sb("t_wr", [2, HID])
        self.idf = sb("t_idf", [P])
        self.b1 = sb("t_b1", [HID // P])
        self.b2 = sb("t_b2", [P])
        self.loads = [(self.wr[:, 0, :], w1), (self.wr[:, 1, :], w2), (self.idf[:, :], ident), (self.b1[:, :], b1),
                      (self.b2[:, :], b2)]
        self.c_in = ctx.enter_context(nc.semaphore("t_c_in"))

    def load(self, sp):
        for dst, src in self.loads:
            sp.dma_start(dst, src).then_inc(self.c_in, 16)


def state_space(nc, y_d, w_proj, conv, w_x, w_dt, a_log, w_out, sel, ident, z_d, following):
    NB = 2
    NS = 16
    STEPS = NB * NS
    POOLED = STEPS - NB
    ADDED = STEPS - NB - 1
    NT = CTX // P
    HALVES = CTX // BANK
    KW = 4
    CB, CD, CT = KW, KW + 1, KW + 2
    LINKS = 6
    PIECE = 1024
    BX, HS, AS, HC = 4, 4, 3, 3

    BOTH = [(c, half) for half in range(HALVES) for c in range(NB)]
    PE_ORDER = ["tr0", "tr1"] + [("x", *u) for u in BOTH] + [("z", 0, 0), ("z", 1, 0), ("dbl", 0), ("z", 0, 1), ("z", 1, 1)]
    PE_ORDER += [("dt", 0, 0), ("dt", 1, 0), ("dbl", 1), ("dt", 0, 1), ("dt", 1, 1)]
    ACT_ORDER = ["xh0", "xh1"] + [(what, *u) for u in BOTH for what in ("xin", "tap")] + [("xc", 0, 0), ("xc", 1, 0), ("z", 0, 0), ("z", 1, 0)]
    ACT_ORDER += [("xs", 0), ("z", 0, 1), ("z", 1, 1), ("xc", 0, 1), ("xc", 1, 1)]
    ACT_ORDER += [("abs", 0, 0), ("abs", 1, 0), ("xs", 1), ("abs", 0, 1), ("abs", 1, 1)]
    ACT_ORDER += [("exp", 0), ("exp", 1), ("ln", 0), ("ln", 1)]
    DVE_ORDER = ["xl0", "xl1"] + [("conv", c, half, k) for c, half in BOTH for k in range(1, KW)] + [("xs", 0), ("xs", 1)]
    DVE_ORDER += [("relu", *u) for u in BOTH] + [("soft", c, k) for k in range(2) for c in range(NB)] + [("soft", 0, 2)]
    DVE_ORDER += [("soft", 0, k) for k in (3, 4)]
    SOFT = 3

    def pe_at(b, *name):
        return len(PE_ORDER) * b + PE_ORDER.index(name if len(name) > 1 else name[0]) + 1

    def act_at(b, *name):
        return len(ACT_ORDER) * b + ACT_ORDER.index(name if len(name) > 1 else name[0]) + 1

    def dve_at(b, *name):
        return len(DVE_ORDER) * b + DVE_ORDER.index(name if len(name) > 1 else name[0]) + 1

    with ExitStack() as ctx:
        def sb(name, shape, dt):
            return ctx.enter_context(nc.sbuf_tensor(name, shape, dt))

        def sem(name):
            return ctx.enter_context(nc.semaphore(name))

        xt = sb("m_xt", [P, NT, P], F32)
        xres = sb("m_xres", [P, NT, P], F32)
        xh = sb("m_xh", [P, CTX], F32R)
        xl = sb("m_xl", [P, CTX], F32R)
        raw = sb("m_raw", [P, 2, PIECE], F32)
        wph = sb("m_wph", [P, 4 * P], F32R)
        wpl = sb("m_wpl", [P, 4 * P], F32R)
        cv = sb("m_cv", [P, NB, KW + 3], F32)
        wx = sb("m_wx", [P, NB, DK], F32)
        wdh = sb("m_wdh", [P, NB * P], F32R)
        wdl = sb("m_wdl", [P, NB * P], F32R)
        av = sb("m_av", [P, NB * NS], F32)
        wo_s = sb("m_wo", [P, NB, P], F32)
        sl = sb("m_sl", [P, 2 * NS * P], F32R)
        idf = sb("m_idf", [P, P], F32)
        xin = sb("m_xin", [P, NB, KW - 1 + CTX], F32)
        xc = sb("m_xc", [P, NB, CTX], F32)
        sz = sb("m_sz", [P, NB, CTX], F32)
        xs = sb("m_xs", [P, CTX], F32R)
        dt = sb("m_dt", [P, NB, CTX], F32)
        dtx = sb("m_dtx", [P, NB, CTX], F32)
        ex = sb("m_ex", [P, NB, CTX], F32)
        rl = sb("m_rl", [P, NB, CTX], F32)
        px = sb("m_px", [P, BX, CTX], F32)
        a = sb("m_a", [P, AS, CTX], F32)
        cs = sb("m_cs", [P, 2, CTX], F32)
        hs = sb("m_hs", [P, HS, CTX], F32)
        hc = sb("m_hc", [P, HC, CTX], F32)
        yz = sb("m_yz", [P, NB, CTX], F32)
        r = sb("m_r", [P, NT, P], F32)
        y3 = sb("m_y3", [P, NT, P], F32)
        st = sb("m_st", [P, NT, 6], F32)
        mv = sb("m_mv", [P, NT, 2], F32)
        ve = sb("m_ve", [P, NT], F32)
        rstd = sb("m_rstd", [P, NT], F32)
        mhalf = sb("m_mhalf", [P, NT], F32)

        ps = ctx.enter_context(nc.psum_tensor("m_ps", [P, 8 * BANK], F32))
        pb, pc, py0, py1 = (ps[:, k * CTX:(k + 1) * CTX] for k in range(4))
        py = (py0, py1)

        def bank(k):
            return ps[:, k * BANK:(k + 1) * BANK]

        TR_BANK = (2, 3)
        X_BANK = {(0, 0): 4, (1, 0): 5, (0, 1): 6, (1, 1): 7}
        Z_BANK = {(0, 0): 2, (1, 0): 3, (0, 1): 4, (1, 1): 5}
        DBL_BANK = (6, 7)
        DT_BANK = {(0, 0): 2, (1, 0): 3, (0, 1): 4, (1, 1): 5}

        held = sem("m_held")
        id_in = sem("m_id_in")
        c_in = sem("m_c_in")
        raw_in = [sem(f"m_raw_in{i}") for i in range(2)]
        raw_hi = sem("m_raw_hi")
        raw_lo = sem("m_raw_lo")
        sel_ok = sem("m_sel_ok")
        a_exp = sem("m_a_exp")
        set_ok = sem("m_set_ok")
        mh_ok = sem("m_mh_ok")
        xt_in = sem("m_xt_in")
        res_ok = sem("m_res_ok")
        pe_pre = sem("m_pe_pre")
        act_pre = sem("m_act_pre")
        dve_pre = sem("m_dve_pre")
        soft = sem("m_soft")
        bb_done = sem("m_bb_done")
        cc_done = sem("m_cc_done")
        a_done = sem("m_a_done")
        c_copied = sem("m_c_copied")
        bx_done = sem("m_bx_done")
        scan_done = sem("m_scan_done")
        hc_done = sem("m_hc_done")
        hc_last = sem("m_hc_last")
        y_acc = sem("m_y_acc")
        chain = sem("m_chain")
        gate_ok = sem("m_gate_ok")
        y_ok = sem("m_y_ok")
        o_done = sem("m_o_done")
        pow_done = sem("m_pow_done")
        z_out = sem("m_z_out")

        STAGED = [(w_proj, wph[:, :]), (w_dt, wdh[:, :])]
        WEIGHTS = len(STAGED)
        STAGED += [(sel[:, k:k + PIECE], sl[:, k:k + PIECE]) for k in range(0, 2 * NS * P, PIECE)]

        block = ctx.enter_context(nc.Block())

        def sequences(engine, body, end):
            body(0, True)
            with engine.Fori(1, BATCH) as b:
                body(b, False)
            end(BATCH - 1)

        @block.sync
        def _(sp):
            def load(b):
                for half in range(HALVES):
                    sp.dma_start(xt[:, half * TILES:(half + 1) * TILES, :], y_d[HALVES * b + half]).then_inc(xt_in, 16)

            def store(b):
                sp.wait_ge(y_ok, b + 1)
                for half in range(HALVES):
                    sp.dma_start(z_d[HALVES * b + half], y3[:, half * TILES:(half + 1) * TILES, :]).then_inc(z_out, 16)

            def stage(k):
                src, dst = STAGED[k]
                sp.dma_start(raw[:, k % 2, 0:dst.shape[1]], src).then_inc(raw_in[k % 2], 16)

            load(0)
            sp.dma_start(idf[:, :], ident).then_inc(id_in, 16)
            for k in range(WEIGHTS):
                stage(k)
            sp.dma_start(av[:, :], a_log).then_inc(c_in, 16)
            sp.dma_start(cv[:, :, :], conv).then_inc(c_in, 16)
            sp.dma_start(wx[:, :, :], w_x).then_inc(c_in, 16)
            sp.dma_start(wo_s[:, :, :], w_out).then_inc(c_in, 16)
            for k in range(WEIGHTS, len(STAGED)):
                if k - 2 < WEIGHTS:
                    sp.wait_ge(raw_lo, k - 1)
                else:
                    sp.wait_ge(sel_ok, k - 1 - WEIGHTS)
                stage(k)
            following.load(sp)
            sp.sem_inc(z_out, 16 * HALVES)
            with sp.Fori(0, BATCH - 1) as b:
                sp.wait_ge(res_ok, b + 1)
                load(b + 1)
                store(b)
            store(BATCH - 1)
            sp.wait_ge(z_out, 16 * HALVES * (BATCH + 1))

        @block.gpsimd
        def _(pool):
            def keep(b, first):
                pool.wait_ge(xt_in, 16 * HALVES * (b + 1))
                pool.wait_ge(pe_pre, pe_at(b, "tr1"))
                if not first:
                    pool.wait_ge(chain, LINKS * (b - 1) + 3)
                pool.sem_inc(held, 1)
                pool.tensor_scalar(xres[:, :, :], xt[:, :, :], 1.0, 1.0, ALU.mult, ALU.mult).then_inc(res_ok, 1)

            def gates(b, blocks=range(NB)):
                for c in blocks:
                    pool.wait_ge(chain, LINKS * b + c + 1)
                    pool.tensor_tensor(yz[:, c, :], yz[:, c, :], sz[:, c, :], ALU.mult).then_inc(gate_ok, 1)

            def power(b):
                pool.wait_ge(chain, LINKS * b + 6)
                pool.tensor_tensor(rstd[:, :], ve[:, :], mhalf[:, :], ALU.pow).then_inc(pow_done, 1)

            def softplus(b):
                pool.wait_ge(dve_pre, dve_at(b, "soft", 1, 1))
                pool.tensor_tensor(rl[:, 1, :], rl[:, 1, :], dtx[:, 1, :], ALU.subtract).then_inc(soft, 1)
                pool.wait_ge(soft, SOFT * b + 1)
                pool.wait_ge(act_pre, act_at(b, "ln", 1))
                pool.tensor_tensor(dt[:, 1, :], dt[:, 1, :], rl[:, 1, :], ALU.add).then_inc(soft, 1)
                pool.wait_ge(soft, SOFT * b + 2)
                pool.tensor_tensor(dtx[:, 1, :], dt[:, 1, :], xc[:, 1, :], ALU.mult).then_inc(soft, 1)

            def body(b, first):
                if not first:
                    gates(b - 1)
                keep(b, first)
                if not first:
                    power(b - 1)
                softplus(b)
                for k in range(POOLED):
                    pool.wait_ge(scan_done, STEPS * b + k + 1)
                    pool.wait_ge(c_copied, NS * b + k // 2 + 1)
                    if k >= HC:
                        pool.wait_ge(y_acc, STEPS * b + k - HC + 1)
                    pool.tensor_tensor(hc[:, k % HC, :], hs[:, k % HS, :], cs[:, (k // 2) % 2, :],
                                       ALU.mult).then_inc(hc_done, 1)

            pool.memset(mhalf[:, :], -0.5).then_inc(mh_ok, 1)
            pool.wait_ge(mh_ok, 1)
            for k in range(WEIGHTS, len(STAGED)):
                dst = STAGED[k][1]
                pool.wait_ge(raw_in[k % 2], 16 * (k // 2 + 1))
                pool.sem_inc(held, 1)
                pool.tensor_scalar(dst, raw[:, k % 2, 0:dst.shape[1]], 1.0, 1.0, ALU.mult, ALU.mult).then_inc(sel_ok, 1)

            def end(b):
                gates(b, range(NB - 1))
                power(b)

            sequences(pool, body, end)

        @block.scalar
        def _(act):
            for k, (_, dst) in enumerate(STAGED[:WEIGHTS]):
                act.wait_ge(raw_in[k % 2], 16)
                act.activation(dst, raw[:, k % 2, 0:dst.shape[1]], ACT.Copy).then_inc(raw_hi, 1)
            act.wait_ge(c_in, 64)
            act.activation(av[:, :], av[:, :], ACT.Exp).then_inc(a_exp, 1)

            def prepare(b):
                def xc_part(c, half):
                    cols = slice(half * BANK, (half + 1) * BANK)
                    act.wait_ge(dve_pre, dve_at(b, "conv", c, half, KW - 1))
                    act.activation(xc[:, c, cols], dtx[:, c, cols], ACT.Silu).then_inc(act_pre, 1)

                def sz_part(c, half):
                    at = half * BANK
                    act.wait_ge(pe_pre, pe_at(b, "z", c, half))
                    act.activation(sz[:, c, at:at + BANK], bank(Z_BANK[c, half]), ACT.Silu).then_inc(act_pre, 1)

                def xs_part(half):
                    cols = slice(half * BANK, (half + 1) * BANK)
                    act.wait_ge(pe_pre, pe_at(b, "dbl", half))
                    act.activation(xs[0:DK, cols], bank(DBL_BANK[half])[0:DK, :], ACT.Copy).then_inc(act_pre, 1)

                def dt_part(c, half):
                    cols = slice(half * BANK, (half + 1) * BANK)
                    src = bank(DT_BANK[c, half])
                    act.wait_ge(pe_pre, pe_at(b, "dt", c, half))
                    act.activation(ex[:, c, cols], src, ACT.Abs, bias=cv[:, c, CT:CT + 1]).then_inc(act_pre, 1)

                for half in range(HALVES):
                    act.wait_ge(pe_pre, pe_at(b, f"tr{half}"))
                    act.activation(xh[:, half * BANK:(half + 1) * BANK], bank(TR_BANK[half]), ACT.Copy).then_inc(act_pre, 1)
                for c, half in BOTH:
                    at = half * BANK
                    act.wait_ge(pe_pre, pe_at(b, "x", c, half))
                    act.activation(xin[:, c, KW - 1 + at:KW - 1 + at + BANK], bank(X_BANK[c, half]), ACT.Copy).then_inc(act_pre, 1)
                    act.wait_ge(act_pre, act_at(b, "xin", c, half))
                    act.activation(dtx[:, c, at:at + BANK], xin[:, c, at:at + BANK], ACT.Identity, scale=cv[:, c, 0:1],
                                   bias=cv[:, c, CB:CB + 1]).then_inc(act_pre, 1)
                xc_part(0, 0)
                xc_part(1, 0)
                sz_part(0, 0)
                sz_part(1, 0)
                xs_part(0)
                sz_part(0, 1)
                sz_part(1, 1)
                xc_part(0, 1)
                xc_part(1, 1)
                dt_part(0, 0)
                dt_part(1, 0)
                xs_part(1)
                dt_part(0, 1)
                dt_part(1, 1)
                for c in range(NB):
                    act.wait_ge(act_pre, act_at(b, "abs", c, 1))
                    act.activation(ex[:, c, :], ex[:, c, :], ACT.Exp, scale=-1.0).then_inc(act_pre, 1)
                for c in range(NB):
                    act.wait_ge(act_pre, act_at(b, "exp", c))
                    act.activation(dt[:, c, :], ex[:, c, :], ACT.Ln, bias=1.0).then_inc(act_pre, 1)

            def body(b, _):
                prepare(b)
                S0 = STEPS * b
                for k in range(STEPS):
                    n, c = k // 2, k % 2
                    if n == 0:
                        if c == 0:
                            act.wait_ge(dve_pre, dve_at(b, "soft", 0, 3))
                        else:
                            act.wait_ge(soft, SOFT * b + 2)
                    if k >= AS:
                        act.wait_ge(scan_done, S0 + k - AS + 1)
                    act.activation(a[:, k % AS, :], dt[:, c, :], ACT.Exp, scale=av[:, c * NS + n:c * NS + n + 1]).then_inc(a_done, 1)
                    if c == 0:
                        act.wait_ge(cc_done, NS * b + n + 1)
                        if n >= 2:
                            act.wait_ge(hc_done, POOLED * b + 2 * n - 2)
                        act.activation(cs[:, n % 2, :], pc, ACT.Copy).then_inc(c_copied, 1)

            act.wait_ge(set_ok, 3)
            sequences(act, body, lambda b: None)

        @block.tensor
        def _(pe):
            def project(base, banks, c, half):
                cols = slice(base + c * P, base + (c + 1) * P)
                at = slice(half * BANK, (half + 1) * BANK)
                dst = bank(banks[c, half])
                pe.matmul(dst, wph[:, cols], xh[:, at], start=True, stop=False)
                pe.matmul(dst, wph[:, cols], xl[:, at], start=False, stop=False)
                pe.matmul(dst, wpl[:, cols], xh[:, at], start=False, stop=True).then_inc(pe_pre, 1)

            def finish(b):
                pe.wait_ge(gate_ok, NB * (b + 1))
                for t in range(NT):
                    cols = slice(t * P, (t + 1) * P)
                    for c in range(NB):
                        m = pe.matmul(pb[:, cols], yz[:, c, cols], wo_s[:, c, :], start=(c == 0), stop=(c == NB - 1))
                m.then_inc(o_done, 1)

            def add_up(b, k):
                n, c = k // 2, k % 2
                if k < POOLED:
                    pe.wait_ge(hc_done, POOLED * b + k + 1)
                else:
                    pe.wait_ge(hc_last, NB * b + k - POOLED + 1)
                for half in range(HALVES):
                    cols = slice(half * BANK, (half + 1) * BANK)
                    m = pe.matmul(py[c][:, cols], idf[:, :], hc[:, k % HC, cols], start=(n == 0), stop=(n == NS - 1))
                m.then_inc(y_acc, 1)

            def prepare(b, first):
                pe.wait_ge(xt_in, 16 * HALVES * (b + 1))
                if first:
                    pe.wait_ge(id_in, 16)
                else:
                    pe.wait_ge(c_copied, NS * b)
                for t in range(NT):
                    m = pe.transpose(pc[:, t * P:(t + 1) * P], xt[:, t, :], idf[:, :])
                    if t % TILES == TILES - 1:
                        m.then_inc(pe_pre, 1)
                if first:
                    pe.wait_ge(raw_lo, WEIGHTS)
                else:
                    for k in range(ADDED, STEPS):
                        add_up(b - 1, k)
                for half in range(HALVES):
                    pe.wait_ge(dve_pre, dve_at(b, f"xl{half}"))
                    if not first:
                        pe.wait_ge(chain, LINKS * (b - 1) + half + 1)
                    for c in range(NB):
                        project(0, X_BANK, c, half)
                if not first:
                    finish(b - 1)

                def project_z(half):
                    for c in range(NB):
                        if half == 0:
                            pe.wait_ge(dve_pre, dve_at(b, "xl1"))
                        else:
                            pe.wait_ge(act_pre, act_at(b, "xin", c, 0))
                        project(2 * P, Z_BANK, c, half)

                def double(half):
                    cols = slice(half * BANK, (half + 1) * BANK)
                    pe.wait_ge(act_pre, act_at(b, "xc", 1, half))
                    for c in range(NB):
                        m = pe.matmul(bank(DBL_BANK[half])[0:DK, :], wx[:, c, :], xc[:, c, cols], start=(c == 0), stop=(c == NB - 1))
                    m.then_inc(pe_pre, 1)

                def widen(half):
                    cols = slice(half * BANK, (half + 1) * BANK)
                    pe.wait_ge(dve_pre, dve_at(b, "xs", half))
                    for c in range(NB):
                        dst = bank(DT_BANK[c, half])
                        pe.wait_ge(act_pre, act_at(b, "z", c, half))
                        pe.matmul(dst, wdh[:, c * P:(c + 1) * P], xs[:, cols], start=True, stop=False)
                        pe.matmul(dst, wdl[:, c * P:(c + 1) * P], xs[:, cols], start=False, stop=True).then_inc(pe_pre, 1)

                project_z(0)
                if first:
                    pe.wait_ge(c_in, 64)
                double(0)
                project_z(1)
                widen(0)
                double(1)
                widen(1)

            def body(b, first):
                prepare(b, first)
                S0 = STEPS * b

                def broadcast_b(n):
                    if n:
                        pe.wait_ge(bx_done, S0 + 2 * n)
                    elif not first:
                        pe.wait_ge(chain, LINKS * (b - 1) + 3)
                    for half in range(HALVES):
                        cols = slice(half * BANK, (half + 1) * BANK)
                        m = pe.matmul(pb[:, cols], sl[:, n * P:(n + 1) * P], xs[:, cols], start=True, stop=True)
                    m.then_inc(bb_done, 1)

                def broadcast_c(n):
                    if n:
                        pe.wait_ge(c_copied, NS * b + n)
                    else:
                        pe.wait_ge(act_pre, act_at(b, "abs", 1, 1))
                        pe.wait_ge(dve_pre, dve_at(b, "relu", 1, 1))
                    for half in range(HALVES):
                        cols = slice(half * BANK, (half + 1) * BANK)
                        m = pe.matmul(pc[:, cols], sl[:, (NS + n) * P:(NS + n + 1) * P], xs[:, cols], start=True, stop=True)
                    m.then_inc(cc_done, 1)

                if first:
                    pe.wait_ge(sel_ok, len(STAGED) - WEIGHTS)
                broadcast_b(0)
                broadcast_c(0)
                broadcast_b(1)
                broadcast_c(1)
                broadcast_b(2)
                for k in range(STEPS):
                    n = k // 2
                    if k % 2 == 0 and n + 2 < NS:
                        broadcast_c(n + 2)
                    if k % 2 == 1 and n + 3 < NS:
                        broadcast_b(n + 3)
                    if k < ADDED:
                        add_up(b, k)

            def end(b):
                for k in range(ADDED, STEPS):
                    add_up(b, k)
                finish(b)

            sequences(pe, body, end)

        @block.vector
        def _(dve):
            for k, (lo, hi) in enumerate(((wpl[:, :], wph[:, :]), (wdl[:, :], wdh[:, :]))):
                dve.wait_ge(raw_hi, k + 1)
                dve.tensor_tensor(lo, raw[:, k, 0:lo.shape[1]], hi.bitcast(F32), ALU.subtract).then_inc(raw_lo, 1)
            dve.memset(xin[:, 0, 0:KW - 1], 0.0).then_inc(set_ok, 1)
            dve.memset(xin[:, 1, 0:KW - 1], 0.0).then_inc(set_ok, 1)
            dve.wait_ge(a_exp, 1)
            dve.tensor_scalar(av[:, :], av[:, :], -1.0, None, ALU.mult).then_inc(set_ok, 1)
            dve.wait_ge(set_ok, 2)

            def gated(b, c):
                dve.wait_ge(y_acc, STEPS * b + STEPS - NB + c + 1)
                dve.scalar_tensor_tensor(yz[:, c, :], xc[:, c, :], cv[:, c, CD:CD + 1], py[c], ALU.mult,
                                         ALU.add).then_inc(chain, 1)

            def residual(b):
                dve.wait_ge(o_done, b + 1)
                dve.wait_ge(res_ok, b + 1)
                dve.tensor_tensor(r[:, :, :], pb.rearrange("p (t d) -> p t d", t=NT), xres[:, :, :], ALU.add).then_inc(chain, 1)

            def moments(b):
                dve.wait_ge(chain, LINKS * b + 3)
                for t in range(NT):
                    m = dve.bn_stats(st[:, t, :], r[:, t, :])
                m.then_inc(chain, 1)
                dve.wait_ge(chain, LINKS * b + 4)
                dve.sem_inc(held, 1)
                for t in range(NT):
                    m = dve.bn_aggr(mv[:, t, :], st[:, t, :])
                m.then_inc(chain, 1)
                dve.wait_ge(chain, LINKS * b + 5)
                dve.tensor_scalar(ve[:, :], mv[:, :, 1], EPS, None, ALU.add).then_inc(chain, 1)

            def normed(b):
                dve.wait_ge(pow_done, b + 1)
                dve.wait_ge(z_out, 16 * HALVES * (b + 1))
                for t in range(NT):
                    m = dve.tensor_scalar(y3[:, t, :], r[:, t, :], mv[:, t, 0:1], rstd[:, t:t + 1], ALU.subtract, ALU.mult)
                m.then_inc(y_ok, 1)

            def prepare(b, first):
                def convolve(c, half):
                    at = half * BANK
                    acc = dtx[:, c, at:at + BANK]
                    dve.wait_ge(act_pre, act_at(b, "tap", c, half))
                    for k in range(1, KW):
                        if k > 1:
                            dve.wait_ge(dve_pre, dve_at(b, "conv", c, half, k - 1))
                        dve.scalar_tensor_tensor(acc, xin[:, c, at + k:at + k + BANK], cv[:, c, k:k + 1], acc,
                                                 ALU.mult, ALU.add).then_inc(dve_pre, 1)

                def xs_part(half):
                    cols = slice(half * BANK, (half + 1) * BANK)
                    dve.wait_ge(act_pre, act_at(b, "xs", half))
                    dve.tensor_tensor(xs[DK:P, cols], bank(DBL_BANK[half])[0:DK, :], xs[0:DK, cols].bitcast(F32),
                                      ALU.subtract).then_inc(dve_pre, 1)

                for half in range(HALVES):
                    cols = slice(half * BANK, (half + 1) * BANK)
                    dve.wait_ge(act_pre, act_at(b, f"xh{half}"))
                    dve.tensor_tensor(xl[:, cols], bank(TR_BANK[half]), xh[:, cols].bitcast(F32), ALU.subtract).then_inc(dve_pre, 1)
                if not first:
                    for c in range(NB):
                        gated(b - 1, c)
                for c, half in BOTH:
                    convolve(c, half)
                xs_part(0)
                if not first:
                    residual(b - 1)
                    moments(b - 1)
                xs_part(1)
                for c, half in BOTH:
                    cols = slice(half * BANK, (half + 1) * BANK)
                    dve.wait_ge(pe_pre, pe_at(b, "dt", c, half))
                    dve.wait_ge(act_pre, act_at(b, "abs", c, half))
                    dve.tensor_scalar(rl[:, c, cols], bank(DT_BANK[c, half]), cv[:, c, CT:CT + 1], 0.0, ALU.add,
                                      ALU.max).then_inc(dve_pre, 1)
                for c in range(NB):
                    dve.wait_ge(act_pre, act_at(b, "exp", c))
                    dve.tensor_scalar(dtx[:, c, :], ex[:, c, :], 1.0, None, ALU.add).then_inc(dve_pre, 1)
                for c in range(NB):
                    dve.wait_ge(dve_pre, dve_at(b, "soft", c, 0))
                    dve.scalar_tensor_tensor(dtx[:, c, :], dtx[:, c, :], -1.0, ex[:, c, :], ALU.add,
                                             ALU.subtract).then_inc(dve_pre, 1)
                dve.wait_ge(dve_pre, dve_at(b, "soft", 0, 1))
                dve.tensor_tensor(rl[:, 0, :], rl[:, 0, :], dtx[:, 0, :], ALU.subtract).then_inc(dve_pre, 1)
                dve.wait_ge(act_pre, act_at(b, "ln", 0))
                dve.wait_ge(dve_pre, dve_at(b, "soft", 0, 2))
                dve.tensor_tensor(dt[:, 0, :], dt[:, 0, :], rl[:, 0, :], ALU.add).then_inc(dve_pre, 1)
                dve.wait_ge(dve_pre, dve_at(b, "soft", 0, 3))
                dve.tensor_tensor(dtx[:, 0, :], dt[:, 0, :], xc[:, 0, :], ALU.mult).then_inc(dve_pre, 1)

            def body(b, first):
                prepare(b, first)
                S0 = STEPS * b

                def inputs(n):
                    dve.wait_ge(bb_done, NS * b + n + 1)
                    for c in range(NB):
                        k = 2 * n + c
                        if n == 0:
                            if c == 0:
                                dve.wait_ge(dve_pre, dve_at(b, "soft", 0, 4))
                            else:
                                dve.wait_ge(soft, SOFT * b + 3)
                        if k >= BX:
                            dve.wait_ge(scan_done, S0 + k - BX + 1)
                        dve.tensor_tensor(px[:, k % BX, :], pb, dtx[:, c, :], ALU.mult).then_inc(bx_done, 1)
                        if k == 0 and not first:
                            normed(b - 1)

                def scan(k):
                    dve.wait_ge(bx_done, S0 + k + 1)
                    dve.wait_ge(a_done, S0 + k + 1)
                    if k >= HS:
                        dve.wait_ge(hc_done, POOLED * b + k - HS + 1)
                    dve.tensor_tensor_scan(hs[:, k % HS, :], a[:, k % AS, :], px[:, k % BX, :], 0.0, ALU.mult,
                                           ALU.add).then_inc(scan_done, 1)

                inputs(0)
                scan(0)
                inputs(1)
                scan(1)
                for n in range(1, NS):
                    if n + 1 < NS:
                        inputs(n + 1)
                    scan(2 * n)
                    scan(2 * n + 1)
                dve.wait_ge(c_copied, NS * (b + 1))
                for k in range(POOLED, STEPS):
                    dve.wait_ge(scan_done, S0 + k + 1)
                    dve.wait_ge(y_acc, S0 + k - HC + 1)
                    dve.tensor_tensor(hc[:, k % HC, :], hs[:, k % HS, :], cs[:, (NS - 1) % 2, :], ALU.mult).then_inc(hc_last, 1)

            def end(b):
                for c in range(NB):
                    gated(b, c)
                dve.wait_ge(chain, LINKS * b + NB)
                dve.tensor_tensor(yz[:, NB - 1, :], yz[:, NB - 1, :], sz[:, NB - 1, :], ALU.mult).then_inc(gate_ok, 1)
                residual(b)
                moments(b)
                normed(b)

            sequences(dve, body, end)


def ternary_ffn(nc, given, z_d, out):
    KC = HID // P
    ROUNDS = CHUNKS // 2
    LINKS = 7

    with ExitStack() as ctx:
        def sb(name, shape, dt):
            return ctx.enter_context(nc.sbuf_tensor(name, shape, dt))

        def sem(name):
            return ctx.enter_context(nc.semaphore(name))

        wr, idf, bv1, bv2 = given.wr, given.idf, given.b1, given.b2
        c_in = given.c_in
        below = sb("t_below", [P, 2, HID], F32)
        wq = sb("t_wq", [P, 2, HID], F32R)
        asum = sb("t_asum", [P, 2], F32)
        th = sb("t_th", [P, 2, 2], F32)
        ones = sb("t_ones", [P, P], F32)
        mhalf = sb("t_mhalf", [P, 2 * TILES], F32)
        warm = sb("t_warm", [P, 2 * TILES], F32)
        xt = sb("t_xt", [P, 2, 2, TILES, P], F32)
        xb = sb("t_xb", [P, 2, 2, TILES, P], F32)
        xh = sb("t_xh", [P, 2, BANK], F32R)
        xl = sb("t_xl", [P, 2, BANK], F32R)
        hf = sb("t_hf", [P, 2, 2, KC, BANK], F32)
        hh = sb("t_hh", [P, 2, 2, KC, BANK], F32R)
        hl = sb("t_hl", [P, 2, 2, KC, BANK], F32R)
        r = sb("t_r", [P, 2, TILES, P], F32)
        y = sb("t_y", [P, 2, TILES, P], F32)
        st = sb("t_st", [P, 2 * TILES, 6], F32)
        mv = sb("t_mv", [P, 2 * TILES, 2], F32)
        ve = sb("t_ve", [P, 2 * TILES], F32)
        rstd = sb("t_rstd", [P, 2 * TILES], F32)
        pu = ctx.enter_context(nc.psum_tensor("t_pu", [P, KC, BANK], F32))
        pt = ctx.enter_context(nc.psum_tensor("t_pt", [P, 2, TILES, P], F32))
        pz = ctx.enter_context(nc.psum_tensor("t_pz", [P, 2, TILES, P], F32))

        held = sem("t_held")
        set_ok = sem("t_set_ok")
        q_sum = sem("t_q_sum")
        q_dve = sem("t_q_dve")
        xt_in = [[sem(f"t_xt_in{i}{s}") for s in range(2)] for i in range(2)]
        tr_done = sem("t_tr_done")
        tr_hi = sem("t_tr_hi")
        tr_lo = sem("t_tr_lo")
        xb_ok = sem("t_xb_ok")
        u_done = sem("t_u_done")
        relu_ok = sem("t_relu_ok")
        hi_ok = sem("t_hi_ok")
        lo_ok = sem("t_lo_ok")
        z_done = sem("t_z_done")
        chain = sem("t_chain")
        pow_done = sem("t_pow_done")
        y_out = [sem(f"t_y_out{i}") for i in range(2)]

        block = ctx.enter_context(nc.Block())

        def rounds(engine, body):
            with engine.Fori(0, ROUNDS // 2 - 1) as i:
                for k in range(2):
                    body(2 * i + k, k, 2)
            body(ROUNDS - 2, 0, 1)
            body(ROUNDS - 1, 1, 0)

        def loads(g, k):
            return 8 * (g - k) + 16

        @block.sync
        def _(sp):
            for k in range(2):
                for s in range(2):
                    sp.dma_start(xt[:, k, s], z_d[2 * k + s]).then_inc(xt_in[k][s], 16)
            for s in range(2):
                sp.sem_inc(y_out[s], 16)

            def body(g, turn, left):
                for s in range(2):
                    if left > 1:
                        sp.wait_ge(xb_ok, 2 * g + s + 1)
                        sp.dma_start(xt[:, turn, s], z_d[2 * g + 4 + s]).then_inc(xt_in[turn][s], 16)
                for s in range(2):
                    sp.wait_ge(chain, LINKS * (g + 1) + 6 + s)
                    sp.dma_start(out[2 * g + s], y[:, s]).then_inc(y_out[s], 16)

            rounds(sp, body)
            for s in range(2):
                sp.wait_ge(y_out[s], 16 * (ROUNDS + 1))

        @block.gpsimd
        def _(pool):
            def residual(g, k, s, first):
                pool.wait_ge(xt_in[k][s], loads(g, k))
                pool.wait_ge(tr_done, 2 * g + s + 1)
                if not first:
                    pool.wait_ge(chain, LINKS * (g - 1) + s + 1)
                pool.tensor_tensor(xb[:, k, s], xt[:, k, s], bv2[:, :].unsqueeze(1).to_broadcast([P, TILES, P]),
                                   ALU.add).then_inc(xb_ok, 1)

            def hidden_hi(g, slot):
                for s in range(2):
                    for k in range(KC):
                        pool.wait_ge(relu_ok, KC * (2 * g + s) + k + 1 + KC)
                        pool.sem_inc(held, 1)
                        pool.tensor_scalar(hh[:, slot, s, k, :], hf[:, slot, s, k, :], 1.0, 1.0, ALU.mult,
                                           ALU.mult).then_inc(hi_ok, 1)

            def body(g, turn, left):
                if left:
                    hidden_hi(g + 1, 1 - turn)
                if left > 1:
                    for s in range(2):
                        residual(g + 2, turn, s, False)
                pool.wait_ge(chain, LINKS * (g + 1) + 5)
                pool.tensor_tensor(rstd[:, :], ve[:, :], mhalf[:, :], ALU.pow).then_inc(pow_done, 1)

            pool.memset(ones[:, :], 1.0).then_inc(set_ok, 1)
            pool.memset(mhalf[:, :], -0.5).then_inc(set_ok, 1)
            pool.wait_ge(set_ok, 2)
            pool.wait_ge(c_in, 80)
            for s in range(2):
                residual(0, 0, s, True)
            hidden_hi(0, 0)
            for s in range(2):
                residual(1, 1, s, True)
            rounds(pool, body)

        @block.scalar
        def _(act):
            def tokens_hi(i, s):
                act.wait_ge(tr_done, i + 1)
                act.activation(xh[:, s, :], pt[:, s].rearrange("p t d -> p (t d)"), ACT.Copy).then_inc(tr_hi, 1)

            def hidden(g, slot):
                for s in range(2):
                    for k in range(KC):
                        act.wait_ge(u_done, KC * (2 * g + s) + k + 1)
                        act.activation(hf[:, slot, s, k, :], pu[:, k, :], ACT.Relu, bias=bv1[:, k:k + 1]).then_inc(relu_ok, 1)

            def body(g, turn, left):
                if left:
                    hidden(g + 1, 1 - turn)
                if left > 1:
                    for s in range(2):
                        tokens_hi(2 * g + 4 + s, s)

            act.sem_inc(relu_ok, KC)
            act.wait_ge(set_ok, 2)
            act.activation(warm[:, :], mhalf[:, :], ACT.Relu)
            act.wait_ge(c_in, 80)
            for s in range(2):
                tokens_hi(s, s)
            hidden(0, 0)
            for s in range(2):
                tokens_hi(2 + s, s)
            rounds(act, body)

        @block.tensor
        def _(pe):
            def transposes(g, k, s):
                pe.wait_ge(xt_in[k][s], loads(g, k))
                for t in range(TILES):
                    m = pe.transpose(pt[:, s, t, :], xt[:, k, s, t, :], idf[:, :])
                m.then_inc(tr_done, 1)

            def up(g):
                for s in range(2):
                    i = 2 * g + s
                    pe.wait_ge(tr_lo, i + 1)
                    for k in range(KC):
                        pe.wait_ge(relu_ok, KC * i + k + 1)
                        cols = slice(k * P, (k + 1) * P)
                        pe.matmul(pu[:, k, :], wq[:, 0, cols], xh[:, s, :], start=True, stop=False)
                        pe.matmul(pu[:, k, :], wq[:, 0, cols], xl[:, s, :], start=False, stop=True).then_inc(u_done, 1)

            def down(g, slot):
                for s in range(2):
                    pe.wait_ge(lo_ok, KC * (2 * g + s + 1))
                    pe.wait_ge(chain, LINKS * g + s + 1)
                    for t in range(TILES):
                        cols = slice(t * P, (t + 1) * P)
                        for k in range(KC):
                            pe.matmul(pz[:, s, t, :], hh[:, slot, s, k, cols], wq[:, 1, k * P:(k + 1) * P], start=(k == 0), stop=False)
                            m = pe.matmul(pz[:, s, t, :], hl[:, slot, s, k, cols], wq[:, 1, k * P:(k + 1) * P], start=False, stop=(k == KC - 1))
                    m.then_inc(z_done, 1)

            def body(g, turn, left):
                if left:
                    up(g + 1)
                if left > 1:
                    for s in range(2):
                        transposes(g + 2, turn, s)
                down(g, turn)

            pe.wait_ge(c_in, 80)
            pe.wait_ge(set_ok, 2)
            pe.wait_ge(q_dve, 2)
            pe.matmul(pz[:, 0, 0, 0:2], ones[:, :], asum[:, :], start=True, stop=True).then_inc(q_sum, 1)
            for s in range(2):
                transposes(0, 0, s)
            pe.wait_ge(q_dve, 7)
            up(0)
            for s in range(2):
                transposes(1, 1, s)
            pe.wait_ge(q_dve, 9)
            rounds(pe, body)

        @block.vector
        def _(dve):
            def tokens_lo(i, s):
                dve.wait_ge(tr_hi, i + 1)
                dve.tensor_tensor(xl[:, s, :], pt[:, s].rearrange("p t d -> p (t d)"), xh[:, s, :].bitcast(F32),
                                  ALU.subtract).then_inc(tr_lo, 1)

            def hidden_lo(g, slot):
                for s in range(2):
                    for k in range(KC):
                        dve.wait_ge(hi_ok, KC * (2 * g + s) + k + 1)
                        dve.tensor_tensor(hl[:, slot, s, k, :], hf[:, slot, s, k, :], hh[:, slot, s, k, :].bitcast(F32),
                                          ALU.subtract).then_inc(lo_ok, 1)

            def body(g, turn, left):
                if left:
                    hidden_lo(g + 1, 1 - turn)
                if left > 1:
                    for s in range(2):
                        tokens_lo(2 * g + 4 + s, s)
                at = LINKS * (g + 1)
                dve.wait_ge(chain, at)
                for s in range(2):
                    dve.wait_ge(z_done, 2 * g + s + 1)
                    dve.wait_ge(xb_ok, 2 * g + s + 1)
                    dve.tensor_tensor(r[:, s], pz[:, s], xb[:, turn, s], ALU.add).then_inc(chain, 1)
                for s in range(2):
                    dve.wait_ge(chain, at + 1 + s)
                    for t in range(TILES):
                        m = dve.bn_stats(st[:, TILES * s + t, :], r[:, s, t, :])
                m.then_inc(chain, 1)
                dve.wait_ge(chain, at + 3)
                dve.sem_inc(held, 1)
                for t in range(2 * TILES):
                    m = dve.bn_aggr(mv[:, t, :], st[:, t, :])
                m.then_inc(chain, 1)
                dve.wait_ge(chain, at + 4)
                dve.tensor_scalar(ve[:, :], mv[:, :, 1], EPS, None, ALU.add).then_inc(chain, 1)
                dve.wait_ge(pow_done, g + 1)
                for s in range(2):
                    dve.wait_ge(y_out[s], 16 * (g + 1))
                    for t in range(TILES):
                        at_t = TILES * s + t
                        m = dve.tensor_scalar(y[:, s, t, :], r[:, s, t, :], mv[:, at_t, 0:1],
                                              rstd[:, at_t:at_t + 1], ALU.subtract, ALU.mult)
                    m.then_inc(chain, 1)

            dve.sem_inc(chain, LINKS)
            dve.wait_ge(c_in, 80)
            for j in range(2):
                dve.tensor_reduce(asum[:, j:j + 1], wr[:, j, :], AX.X, ALU.add, apply_absolute_value=True).then_inc(q_dve, 1)
            dve.wait_ge(q_sum, 1)
            dve.tensor_scalar(th[:, 0, :], pz[:, 0, 0, 0:2], 1.0 / (D * HID), EPS, ALU.mult, ALU.add).then_inc(q_dve, 1)
            dve.wait_ge(q_dve, 3)
            dve.tensor_scalar(th[:, 1, :], th[:, 0, :], -0.5, None, ALU.mult).then_inc(q_dve, 1)
            dve.wait_ge(q_dve, 4)
            dve.tensor_scalar(th[:, 0, :], th[:, 1, :], -1.0, None, ALU.mult).then_inc(q_dve, 1)
            dve.wait_ge(q_dve, 5)

            def quantise(j):
                dve.tensor_scalar(below[:, j, :], wr[:, j, :], th[:, 1, j:j + 1], None, ALU.is_lt).then_inc(q_dve, 1)
                dve.wait_ge(q_dve, 6 + 2 * j)
                dve.scalar_tensor_tensor(wq[:, j, :], wr[:, j, :], th[:, 0, j:j + 1], below[:, j, :], ALU.is_gt,
                                         ALU.subtract).then_inc(q_dve, 1)

            quantise(0)
            for s in range(2):
                tokens_lo(s, s)
            quantise(1)
            hidden_lo(0, 0)
            for s in range(2):
                tokens_lo(2 + s, s)
            rounds(dve, body)


def program(nc, x_tok, xT, wpk, masks, pick, wo, w_in, w_hid, w_out, scales, s3, w_proj, conv, w_x, w_dt, a_log,
            w_mix, sel, w1, w2, b1, b2, ident, out):
    ot_d = nc.dram_tensor("attended", [CHUNKS, P, PAIRS, BANK], F32, kind="Internal").ap()
    y_d = nc.dram_tensor("after_gated", [CHUNKS, P, TILES, P], F32, kind="Internal").ap()
    z_d = nc.dram_tensor("after_mixer", [CHUNKS, P, TILES, P], F32, kind="Internal").ap()
    with ExitStack() as ctx:
        given = GatedInputs(nc, ctx, ot_d, x_tok, wo, w_in, w_hid, w_out)
        attention(nc, xT, wpk, ident, masks, pick, ot_d, given)
        gated_ffn(nc, given, ot_d, x_tok, scales, s3, ident, y_d)
    with ExitStack() as ctx:
        given = TernaryInputs(nc, ctx, w1, w2, b1, b2, ident)
        state_space(nc, y_d, w_proj, conv, w_x, w_dt, a_log, w_mix, sel, ident, z_d, given)
        ternary_ffn(nc, given, z_d, out)


def kernel(**inputs):
    import numpy as np
    import concourse.bacc as bacc
    from concourse.bass_utils import run_bass_kernel_spmd

    t = {k: np.asarray(v) for k, v in inputs.items()}

    def tiled(m):
        return np.ascontiguousarray(m.reshape(-1, P, m.shape[1]).transpose(1, 0, 2))

    def spread(vec):
        return np.ascontiguousarray(np.broadcast_to(vec, (P, vec.shape[0])))

    x = t["L0_attn_x"].reshape(TOK, D)
    wpk = np.empty((PAIRS, P, WCOLS), np.float32)
    for pair in range(PAIRS):
        both = slice(2 * DK * pair, 2 * DK * (pair + 1))
        for at, bias_at, n in ((WQ, WBQ, "q"), (WK, WBK, "k")):
            wpk[pair, :, at:at + P] = t[f"L0_attn_W{n}"][:, both]
            wpk[pair, :, bias_at] = t[f"L0_attn_b{n}"][both]
        wpk[pair, :, WV:WV + P] = t["L0_attn_Wv"][:, both]
        wpk[pair, :, WBV:WBV + P] = t["L0_attn_bv"][both]

    key = np.arange(P)
    mask = np.where(key[None, :] <= key[:, None], 0.0, -1e30).astype(np.float32)
    pick = np.zeros((P, 8), np.float32)
    pick[DK + np.arange(8), np.arange(8)] = 1.0
    per_block = lambda vec: vec.reshape(-1, P).T
    conv = np.concatenate([t["L1_attn_conv_w"].reshape(2, P, 4).transpose(1, 0, 2)] +
                          [per_block(t[n])[:, :, None] for n in ("L1_attn_conv_b", "L1_attn_D_param", "L1_attn_dt_proj_b")], 2)
    w_x = np.zeros((P, 2, DK), np.float32)
    w_x[:, :, 0:40] = tiled(t["L1_attn_x_proj_w"].T)
    w_dt = np.zeros((P, 256), np.float32)
    sel = np.zeros((P, 32, P), np.float32)
    for lo in (0, DK):
        w_dt[lo:lo + 8] = t["L1_attn_dt_proj_w"].T
        for n in range(32):
            sel[lo + 8 + n, n] = 1.0

    arrays = {
        "x_tok": x.reshape(CHUNKS, TILES, P, D).transpose(0, 2, 1, 3),
        "xT": x.T,
        "wpk": wpk,
        "masks": np.stack([mask, mask.T], 1),
        "pick": pick,
        "wo": tiled(t["L0_attn_Wo"]),
        "w_in": np.stack([t["L0_ffn_w1_w"].T, t["L0_ffn_w2_w"].T]),
        "w_hid": np.stack([tiled(t[n].T).reshape(P, -1) for n in ("L0_ffn_h1_w", "L0_ffn_h2_w")]),
        "w_out": tiled(t["L0_ffn_w3_w"].T).reshape(P, -1),
        "scales": np.stack([per_block(t[f"L0_ffn_{n}_s"]) for n in ("w1", "w2", "h1", "h2")], 1),
        "s3": spread(t["L0_ffn_w3_s"]),
        "w_proj": t["L1_attn_in_proj_w"].T,
        "conv": conv,
        "w_x": w_x,
        "w_dt": w_dt,
        "a_log": tiled(t["L1_attn_A_log"]).reshape(P, -1),
        "w_mix": tiled(t["L1_attn_out_proj_w"].T),
        "sel": sel.reshape(P, -1),
        "w1": t["L1_ffn_W1"].T,
        "w2": tiled(t["L1_ffn_W2"].T).reshape(P, -1),
        "b1": per_block(t["L1_ffn_b1"]),
        "b2": spread(t["L1_ffn_b2"]),
        "ident": np.eye(P, dtype=np.float32),
    }
    arrays = {f"in_{k}": np.ascontiguousarray(v) for k, v in arrays.items()}
    nc = bacc.Bacc("TRN2", target_bir_lowering=False, num_devices=1)
    args = [nc.dram_tensor(k, v.shape, mybir.dt.from_np(v.dtype), kind="ExternalInput").ap() for k, v in arrays.items()]
    out = nc.dram_tensor("tokens_out", [CHUNKS, P, TILES, P], F32, kind="ExternalOutput").ap()
    program(nc, *args, out)
    got = run_bass_kernel_spmd(nc, [arrays], core_ids=[0]).results[0]["tokens_out"]
    return got.reshape(CHUNKS, P, TILES, D).transpose(0, 2, 1, 3).reshape(BATCH, CTX, D)
```
